# Optimizing a Trainium2 kernel written in Bass

```python
import numpy as np
import jax
import jax.numpy as jnp

def _softmax(x, axis=-1):
    return jax.nn.softmax(x, axis=axis)

def _gelu(x):
    return jax.nn.gelu(x, approximate=True)

def _silu(x):
    return jax.nn.silu(x)

def _sigmoid(x):
    return jax.nn.sigmoid(x)

def _layernorm(x, axis=-1, eps=1e-05):
    m = jnp.mean(x, axis=axis, keepdims=True)
    v = jnp.var(x, axis=axis, keepdims=True)
    return (x - m) / jnp.sqrt(v + eps)

def _scatter_add(tgt, idx, src, axis=0):
    return tgt.at[idx].add(src)

def _segment_sum(src, seg, n):
    return jax.ops.segment_sum(src, seg, n)
kernel_name = 'mk_decoder_postln_d1_seqx_r8_54f13d'

def setup_inputs(seed: int=0):
    np.random.seed(seed)
    _w = jnp.asarray

    def _rec_inputs():
        import jax
        import jax.numpy as jnp
        _rk = jax.random.key(seed)
        x = -0.0002928 + 1 * jax.random.normal(jax.random.fold_in(_rk, 1), (32, 56, 128), jnp.float32)
        _lenS = 56 - jax.random.randint(jax.random.fold_in(_rk, 7), (32,), 0, max(1, 56 // 4) + 1, jnp.int32)
        _lenS2 = 1500 - jax.random.randint(jax.random.fold_in(_rk, 8), (32,), 0, max(1, 1500 // 4) + 1, jnp.int32)
        _ctx_1024P = jax.random.normal(jax.random.fold_in(_rk, 11), (32, 16, 128), jnp.float32)
        _ctx_1024c = jax.random.dirichlet(jax.random.fold_in(_rk, 511), 0.3 * jnp.ones((16,), jnp.float32), (32, 1500))
        _ctx_1024t = jnp.einsum('bsk,bkd->bsd', _ctx_1024c, _ctx_1024P)
        _ctx_1024t = _ctx_1024t * jax.lax.rsqrt(jnp.mean(jnp.square(_ctx_1024t)) + 1e-12) * 0.953939
        ctx_1024 = -1.39393e-06 + 0.999914 * (_ctx_1024t + 0.3 * jax.random.normal(jax.random.fold_in(_rk, 611), (32, 1500, 128), jnp.float32))
        return (x, ctx_1024)
    x, ctx_1024 = _rec_inputs()

    def _L0_attn_setup():
        import jax, jax.numpy as jnp
        import numpy as np
        B, L, DIM, H, D = (4, 128, 128, 8, 32)
        key = jax.random.key(seed)
        ks = jax.random.split(key, 8)
        s = 0.02
        return dict(x=jax.random.normal(ks[0], (B, L, DIM), jnp.float32), W_in=jax.random.normal(ks[1], (DIM, DIM), jnp.float32) * s, b_in=jnp.zeros((DIM,), jnp.float32), W_qkva=jax.random.normal(ks[2], (H * D * 8, DIM), jnp.float32) * s, b_qkva=jnp.zeros((H * D * 8,), jnp.float32), W_y=jax.random.normal(ks[3], (DIM, H * D * 2), jnp.float32) * s, b_y=jnp.zeros((DIM,), jnp.float32), W_out=jax.random.normal(ks[4], (DIM, DIM), jnp.float32) * s, b_out=jnp.zeros((DIM,), jnp.float32), h0_re=jax.random.normal(ks[5], (H, D, D), jnp.float32), h0_im=jax.random.normal(ks[6], (H, D, D), jnp.float32))
    _L0_attn_all = _L0_attn_setup()
    _L0_attn_in = {k: v for k, v in _L0_attn_all.items() if k in ('W_in', 'b_in', 'W_qkva', 'b_qkva', 'W_y', 'b_y', 'W_out', 'b_out', 'h0_re', 'h0_im')}
    del _L0_attn_all

    def _L0_xattn_setup():
        import jax, jax.numpy as jnp
        import numpy as np
        EMBED_DIM = 128
        NUM_HEADS = 16
        HEAD_DIM = EMBED_DIM // NUM_HEADS
        key = jax.random.key(seed)
        ks = jax.random.split(key, 7)
        B, S, E = (2, 256, EMBED_DIM)
        bound = float(np.sqrt(6.0 / (E + E)))
        mkw = lambda k: jax.random.uniform(k, (E, E), jnp.float32, -bound, bound)
        return {'query': jax.random.normal(ks[0], (B, S, E), jnp.float32), 'key': jax.random.normal(ks[1], (B, S, E), jnp.float32), 'value': jax.random.normal(ks[2], (B, S, E), jnp.float32), 'Wq': mkw(ks[3]), 'Wk': mkw(ks[4]), 'Wv': mkw(ks[5]), 'Wo': mkw(ks[6])}
    _L0_xattn_all = _L0_xattn_setup()
    _L0_xattn_in = {k: v for k, v in _L0_xattn_all.items() if k in ('Wq', 'Wk', 'Wv', 'Wo')}
    del _L0_xattn_all

    def _L0_ffn_setup():
        import jax, jax.numpy as jnp
        import numpy as np
        S, B, D, H, DH = (512, 8, 128, 16, 64)

        def _forward(x, Wg, Wq, bq, Wkv, bkv, Wo, bo, ln_g, ln_b):
            s_len, bsz, d_model = x.shape
            n_head, _, d_head = Wq.shape
            cap = s_len // n_head
            scale = 1.0 / d_head ** 0.5
            h = jnp.transpose(x, (1, 0, 2))
            t = h
            probs = jax.nn.softmax(h @ Wg, axis=-1)
            scores = jnp.transpose(probs, (0, 2, 1))
            _, idx = jax.lax.top_k(scores, cap)
            idx = jnp.sort(idx, axis=-1)
            hg = jnp.take_along_axis(h[:, None, :, :], idx[..., None], axis=2)
            hg = jnp.transpose(hg, (1, 0, 2, 3))
            q = jnp.einsum('hbcd,hde->hbce', hg, Wq) + bq[:, None, None, :]
            kv = jnp.einsum('hbcd,hde->hbce', hg, Wkv) + bkv[:, None, None, :]
            k, v = jnp.split(kv, 2, axis=-1)
            att = jnp.einsum('hbid,hbjd->hbij', q, k) * scale
            p = jax.nn.softmax(att, axis=1)
            av = jnp.einsum('hbij,hbjd->hbid', p, v)
            ao = jnp.einsum('hbid,hde->hbie', av, Wo) + bo
            tok = jnp.transpose(idx, (1, 0, 2))
            b_ids = jnp.arange(bsz)[None, :, None]
            outs = jnp.zeros_like(t).at[b_ids, tok].add(ao)
            y = t + outs
            mu = jnp.mean(y, axis=-1, keepdims=True)
            var = jnp.var(y, axis=-1, keepdims=True)
            yn = (y - mu) * jax.lax.rsqrt(var + 1e-05) * ln_g + ln_b
            return jnp.transpose(yn, (1, 0, 2))
        key = jax.random.key(seed)
        ks = jax.random.split(key, 6)
        s = 0.02
        return {'x': jax.random.normal(ks[0], (S, B, D), jnp.float32), 'attn_mask': jnp.zeros((S, S), jnp.bool_), 'Wg': jax.random.normal(ks[1], (D, H), jnp.float32) * s, 'Wq': jax.random.normal(ks[2], (H, D, DH), jnp.float32) * s, 'bq': jnp.zeros((H, DH), jnp.float32), 'Wkv': jax.random.normal(ks[3], (H, D, 2 * DH), jnp.float32) * s, 'bkv': jnp.zeros((H, 2 * DH), jnp.float32), 'Wo': jax.random.normal(ks[4], (H, DH, D), jnp.float32) * s, 'bo': jnp.zeros((D,), jnp.float32), 'ln_g': jnp.ones((D,), jnp.float32), 'ln_b': jnp.zeros((D,), jnp.float32)}
    _L0_ffn_all = _L0_ffn_setup()
    _L0_ffn_in = {k: v for k, v in _L0_ffn_all.items() if k in ('attn_mask', 'Wg', 'Wq', 'bq', 'Wkv', 'bkv', 'Wo', 'bo', 'ln_g', 'ln_b')}
    del _L0_ffn_all
    return {'x': x, 'ctx_1024': ctx_1024, 'L0_attn_W_in': _L0_attn_in['W_in'], 'L0_attn_b_in': _L0_attn_in['b_in'], 'L0_attn_W_qkva': _L0_attn_in['W_qkva'], 'L0_attn_b_qkva': _L0_attn_in['b_qkva'], 'L0_attn_W_y': _L0_attn_in['W_y'], 'L0_attn_b_y': _L0_attn_in['b_y'], 'L0_attn_W_out': _L0_attn_in['W_out'], 'L0_attn_b_out': _L0_attn_in['b_out'], 'L0_attn_h0_re': _L0_attn_in['h0_re'], 'L0_attn_h0_im': _L0_attn_in['h0_im'], 'L0_xattn_Wq': _L0_xattn_in['Wq'], 'L0_xattn_Wk': _L0_xattn_in['Wk'], 'L0_xattn_Wv': _L0_xattn_in['Wv'], 'L0_xattn_Wo': _L0_xattn_in['Wo'], 'L0_ffn_attn_mask': _L0_ffn_in['attn_mask'], 'L0_ffn_Wg': _L0_ffn_in['Wg'], 'L0_ffn_Wq': _L0_ffn_in['Wq'], 'L0_ffn_bq': _L0_ffn_in['bq'], 'L0_ffn_Wkv': _L0_ffn_in['Wkv'], 'L0_ffn_bkv': _L0_ffn_in['bkv'], 'L0_ffn_Wo': _L0_ffn_in['Wo'], 'L0_ffn_bo': _L0_ffn_in['bo'], 'L0_ffn_ln_g': _L0_ffn_in['ln_g'], 'L0_ffn_ln_b': _L0_ffn_in['ln_b']}

def reference(x, ctx_1024, L0_attn_W_in, L0_attn_b_in, L0_attn_W_qkva, L0_attn_b_qkva, L0_attn_W_y, L0_attn_b_y, L0_attn_W_out, L0_attn_b_out, L0_attn_h0_re, L0_attn_h0_im, L0_xattn_Wq, L0_xattn_Wk, L0_xattn_Wv, L0_xattn_Wo, L0_ffn_attn_mask, L0_ffn_Wg, L0_ffn_Wq, L0_ffn_bq, L0_ffn_Wkv, L0_ffn_bkv, L0_ffn_Wo, L0_ffn_bo, L0_ffn_ln_g, L0_ffn_ln_b):
    import jax
    import jax.numpy as jnp

    def _L0_attn_ref(x, W_in, b_in, W_qkva, b_qkva, W_y, b_y, W_out, b_out, h0_re, h0_im):
        import jax, jax.numpy as jnp
        import numpy as np
        B, L, DIM, H, D = (4, 128, 128, 8, 32)
        b, Ls, dim = x.shape
        Hh, Dd = (h0_re.shape[0], h0_re.shape[1])
        u = jax.nn.silu(x @ W_in.T + b_in)
        qkva = (u @ W_qkva.T + b_qkva).reshape(b, Ls, Hh, Dd, 4, 2)
        c = jax.lax.complex(qkva[..., 0], qkva[..., 1])
        q, k, v, a = (c[..., 0], c[..., 1], c[..., 2], c[..., 3])
        mag2 = a.real * a.real + a.imag * a.imag
        a = a * (jax.lax.rsqrt(mag2) * jax.nn.sigmoid(jnp.log(mag2)))
        kv = jnp.einsum('blhd,blhe->blhde', k, v)
        h0 = jax.lax.complex(h0_re, h0_im)[None]
        kv = kv.at[:, 0].add(a[:, 0, ..., None] * h0)
        a_e = a[..., None]

        def comb(c1, c2):
            a1, x1 = c1
            a2, x2 = c2
            return (a1 * a2, a2 * x1 + x2)
        _, h = jax.lax.associative_scan(comb, (a_e, kv), axis=1)
        y = jnp.einsum('blhd,blhde->blhe', q, h)
        y2 = jnp.stack([y.real, y.imag], axis=-1).reshape(b, Ls, Hh * Dd * 2)
        y2 = jax.nn.silu(y2 @ W_y.T + b_y)
        return y2 @ W_out.T + b_out

    def _L0_xattn_ref(query, key, value, Wq, Wk, Wv, Wo):
        import jax, jax.numpy as jnp
        import numpy as np
        EMBED_DIM = 128
        NUM_HEADS = 16
        HEAD_DIM = EMBED_DIM // NUM_HEADS
        B, L, E = query.shape
        H, D = (NUM_HEADS, HEAD_DIM)
        scale = D ** (-0.5)
        q = (query @ Wq.T).reshape(B, L, H, D) * scale
        k = (key @ Wk.T).reshape(B, -1, H, D)
        v = (value @ Wv.T).reshape(B, -1, H, D)
        scores = jax.nn.sigmoid(jnp.einsum('blhd,bshd->bhls', q, k))
        o = jnp.einsum('bhls,bshd->blhd', scores, v).reshape(B, L, E)
        return o @ Wo.T

    def _L0_ffn_ref(x, attn_mask, Wg, Wq, bq, Wkv, bkv, Wo, bo, ln_g, ln_b):
        import jax, jax.numpy as jnp
        import numpy as np
        S, B, D, H, DH = (512, 8, 128, 16, 64)

        def _forward(x, Wg, Wq, bq, Wkv, bkv, Wo, bo, ln_g, ln_b):
            s_len, bsz, d_model = x.shape
            n_head, _, d_head = Wq.shape
            cap = s_len // n_head
            scale = 1.0 / d_head ** 0.5
            h = jnp.transpose(x, (1, 0, 2))
            t = h
            probs = jax.nn.softmax(h @ Wg, axis=-1)
            scores = jnp.transpose(probs, (0, 2, 1))
            _, idx = jax.lax.top_k(scores, cap)
            idx = jnp.sort(idx, axis=-1)
            hg = jnp.take_along_axis(h[:, None, :, :], idx[..., None], axis=2)
            hg = jnp.transpose(hg, (1, 0, 2, 3))
            q = jnp.einsum('hbcd,hde->hbce', hg, Wq) + bq[:, None, None, :]
            kv = jnp.einsum('hbcd,hde->hbce', hg, Wkv) + bkv[:, None, None, :]
            k, v = jnp.split(kv, 2, axis=-1)
            att = jnp.einsum('hbid,hbjd->hbij', q, k) * scale
            p = jax.nn.softmax(att, axis=1)
            av = jnp.einsum('hbij,hbjd->hbid', p, v)
            ao = jnp.einsum('hbid,hde->hbie', av, Wo) + bo
            tok = jnp.transpose(idx, (1, 0, 2))
            b_ids = jnp.arange(bsz)[None, :, None]
            outs = jnp.zeros_like(t).at[b_ids, tok].add(ao)
            y = t + outs
            mu = jnp.mean(y, axis=-1, keepdims=True)
            var = jnp.var(y, axis=-1, keepdims=True)
            yn = (y - mu) * jax.lax.rsqrt(var + 1e-05) * ln_g + ln_b
            return jnp.transpose(yn, (1, 0, 2))
        return _forward(x, Wg, Wq, bq, Wkv, bkv, Wo, bo, ln_g, ln_b)
    x = _layernorm(x + _L0_attn_ref(x, L0_attn_W_in, L0_attn_b_in, L0_attn_W_qkva, L0_attn_b_qkva, L0_attn_W_y, L0_attn_b_y, L0_attn_W_out, L0_attn_b_out, L0_attn_h0_re, L0_attn_h0_im), axis=-1)
    x = _layernorm(x + _L0_xattn_ref(x, ctx_1024, ctx_1024, L0_xattn_Wq, L0_xattn_Wk, L0_xattn_Wv, L0_xattn_Wo), axis=-1)
    x = _layernorm(x + _L0_ffn_ref(x, L0_ffn_attn_mask, L0_ffn_Wg, L0_ffn_Wq, L0_ffn_bq, L0_ffn_Wkv, L0_ffn_bkv, L0_ffn_Wo, L0_ffn_bo, L0_ffn_ln_g, L0_ffn_ln_b), axis=-1)
    return x

_drawn_inputs = setup_inputs


def setup_inputs(seed=0):
    import zlib

    import numpy as np

    out = dict(_drawn_inputs(seed))
    spreads = {'L0_attn_b_in': (0.0, 0.8),
     'L0_attn_b_qkva': (0.0, 0.8),
     'L0_attn_b_y': (0.0, 0.8),
     'L0_attn_b_out': (0.0, 0.318),
     'L0_ffn_bq': (0.0, 0.8),
     'L0_ffn_bkv': (0.0, 0.8),
     'L0_ffn_bo': (0.0, 0.1),
     'L0_ffn_ln_g': (1.0, 0.2),
     'L0_ffn_ln_b': (0.0, 0.1)}
    factors = {'L0_attn_W_in': 8.0,
     'L0_attn_W_qkva': 8.0,
     'L0_attn_W_y': 8.0,
     'L0_attn_W_out': 8.0,
     'L0_attn_h0_re': 8.0,
     'L0_attn_h0_im': 8.0,
     'L0_ffn_Wq': 8.0,
     'L0_ffn_Wkv': 8.0,
     'L0_ffn_Wo': 8.0}
    for name, (base, spread) in spreads.items():
        noise = np.random.default_rng([zlib.crc32(name.encode()), seed]).standard_normal(out[name].shape)
        drawn = base * np.exp(spread * noise) if base else spread * noise
        out[name] = jnp.asarray(drawn.astype(out[name].dtype))
    for name, factor in factors.items():
        out[name] = (out[name] * factor).astype(out[name].dtype)
    return out
```

```python
from contextlib import ExitStack

import numpy as np

import concourse.bass as bass
from concourse import mybir

F32 = mybir.dt.float32
F32R = mybir.dt.float32r
ACT = mybir.ActivationFunctionType
ALU = mybir.AluOpType
AX = mybir.AxisListType

BATCH, TIME, DM = 32, 56, 128
HEADS, DH = 8, 32
PAIRS = HEADS // 2
TP = 64
GB = 4
GROUPS = BATCH // GB
PB = PAIRS * GB
GT = GB * TIME
TOKENS = BATCH * TIME
ROWS = 2 * TIME
TILES = BATCH // 2
HALVES = [32, 16, 8, 4, 2, 1]
SLOTS = len(HALVES) + 2
CTX = 1500
KT_N = 12
KP = CTX // KT_N
XH, XD = 16, 8
XSCALE = float(XD) ** -0.5
CH = 500
QC = XH // 4 * TIME
EX, EDH = 16, 64
CAP = BATCH // EX
KL = TIME // 4
EPS = 1e-5


def spread(ap, axis, count):
    ap = ap.unsqueeze(axis)
    shape = list(ap.shape)
    shape[axis] = count
    return ap.broadcast_to(shape)


class Chain:

    def __init__(self, eng, sem, base):
        self.eng, self.sem, self.base, self.n = eng, sem, base, 0

    def step(self, ins):
        ins.then_inc(self.sem, 1)
        self.n += 1

    def wait(self):
        self.eng.wait_ge(self.sem, self.base + self.n)



FRONT = 11


def mixer(nc, io, keep, pb):
    x1, xT = keep["x1"], keep["xT"]
    ident = keep["ident"]
    with ExitStack() as ctx:
        def sb(name, shape):
            return ctx.enter_context(nc.sbuf_tensor("m_" + name, shape, F32))

        def sem(name):
            return ctx.enter_context(nc.semaphore("m_" + name))

        win, wout = sb("win", [128, 128]), sb("wout", [128, 128])
        wy = sb("wy", [128, PAIRS, 128])
        wgate = sb("wgate", [128, 2, 2, 128])
        wqk = sb("wqk", [128, 4, PAIRS, 128])
        bgate, bqk = sb("bgate", [128, 4]), sb("bqk", [128, 16])
        bcol = sb("bcol", [128, 2])
        wv, bv = sb("wv", [128, 512]), sb("bv", [128, 512])
        bout = sb("bout", [128, 128])
        h0 = sb("h0", [128, PAIRS, 128])
        mask = sb("mask", [128, 2, TP])
        silu_a, silu_b = sb("silu_a", [128, GT]), sb("silu_b", [128, GT])
        uT = sb("uT", [128, GB, TP])
        uS = sb("uS", [128, GB, SLOTS, 32])
        ag = sb("ag", [128, 2, 8, TP])
        mag, root = sb("mag", [128, 8 * TP]), sb("root", [128, 8 * TP])
        qk = sb("qk", [128, 4, PAIRS, GB, TP])
        tmp = sb("tmp", [128, 2, PB * TP])
        inv, den = tmp[:, 0, 8 * TP:], tmp[:, 1, 8 * TP:]
        pp = sb("pp", [128, 2, 8, TP])
        sq = pp[:].rearrange("p r c t -> p r (c t)")
        gx = sb("gx", [128, 3, 8, TP])
        bp = sb("bp", [128, 2, 8, 8])
        gd = sb("gd", [128, 3, PAIRS, GB, TP])
        suf = sb("suf", [128, PB * TP])
        qv = sb("qv", [128, 2, PB, TP])
        kv = sb("kv", [128, PB, TP])
        qd = sb("qd", [128, 2, PB, TP])
        kd = sb("kd", [128, PB, TP])
        ql = sb("ql", [128, 6, 2, PB, 32])
        kl = sb("kl", [128, 6, PB, 32])
        qf = gd[:, 0]
        v1 = sb("v1", [128, GB * 2, 512])
        v2 = sb("v2", [128, GB * 2, 512])
        sm = sb("sm", [128, 4, GB, 2, TP])
        ysb = sb("ysb", [128, PAIRS, GT])
        z2 = sb("z2", [128, GT])
        stats, mv = sb("stats", [ROWS, TILES, 6]), sb("mv", [ROWS, TILES, 2])
        rstd = sb("rstd", [ROWS, TILES])
        x1T = xT

        s_load = sem("consts_loaded")
        s_xt_ps, s_xt = sem("xT_in_psum"), sem("xT_ready")
        s_pfill, s_pevac = sem("proj_filled"), sem("proj_read")
        s_silu = sem("silu_ready")
        s_us = sem("slot_u_ready")
        s_sq, s_mag, s_root = sem("squares"), sem("mag2_ready"), sem("root_ready")
        s_pp, s_gates, s_exp = sem("phases_ready"), sem("gates_ready"), sem("gates_spread")
        s_qv, s_kv, s_diag, s_lev = sem("q_turned"), sem("k_turned"), sem("diag_copied"), sem("levels_ready")
        s_S, s_mask, s_Y, s_yev = sem("scores_filled"), sem("scores_masked"), sem("y_unit_done"), sem("y_read")
        s_h0 = sem("h0_added")
        s_vfill, s_vevac, s_v2 = sem("v_filled"), sem("v_read"), sem("v_turned")
        s_dve, s_pool = sem("dve_chain"), sem("pool_chain")
        s_pads, s_signs = sem("pads_set"), sem("signs_set")
        s_stats = sem("stats_ready")
        s_ln, s_root1, s_x1 = sem("ln_chain"), sem("rstd_root"), sem("x1_ready")
        s_x1T_ps, s_x1T = sem("x1T_in_psum"), sem("x1T_ready")

        n_load = [0]

        def load(eng, dst, src):
            eng.dma_start(dst, src).then_inc(s_load, 16)
            n_load[0] += 16

        LOADS = 16 * (18 + 2 * 4)

        def pbase(g):
            return 22 + 12 * g if not (isinstance(g, int) and g == GROUPS - 1) else 22 + 12 * (g - 1) + 1

        def silu_base(g):
            return 2 + 2 * g if not (isinstance(g, int) and g == GROUPS - 1) else 2 + 2 * (g - 1) + 1

        def front_end(g):
            return 12 * g + 10 if not (isinstance(g, int) and g == 0) else FRONT

        def vbase(g):
            return 8 + 10 * g

        block = ctx.enter_context(nc.Block())

        @block.sync
        def _(sp):
            x_v = io["x"].rearrange("(j two) t d -> (two t) j d", two=2)
            for c in range(4):
                load(sp, x1[:, 4 * c:4 * c + 4, :], x_v[:, 4 * c:4 * c + 4, :])
            load(sp, ident[:], io["ident"])
            load(sp, win[:], io["w_inT"])
            load(sp, wgate[:], io["w_gate"])
            load(sp, wqk[:], io["w_qk"])
            load(sp, bgate[:], io["b_gate"])
            load(sp, bqk[:], io["b_qk"])
            load(sp, bcol[:], io["b_col"])
            load(sp, wv[:], io["w_v"])
            load(sp, bv[:], io["b_v"].partition_broadcast(128))
            load(sp, bout[:], io["b_out"].partition_broadcast(128))
            load(sp, wout[:], io["w_outT"])
            load(sp, wy[:], io["w_yT"])
            load(sp, mask[:], io["mask"])
            load(sp, keep["hmask"][:], io["hmask"])
            sp.wait_ge(s_pads, 1)
            for hh in range(2):
                for r, (left, right) in enumerate((("h0_re", "h0_im"), ("h0_im", "h0_re"))):
                    rows = slice(64 * hh + 32 * r, 64 * hh + 32 * r + 32)
                    for c, name in enumerate((left, right)):
                        load(sp, h0[rows, :, 64 * hh + 32 * c:64 * hh + 32 * c + 32],
                             io[name].rearrange("(p hh) d e -> hh d p e", hh=2)[hh])
            assert n_load[0] == LOADS, n_load
            def spread_gates(j):
                sp.wait_ge(s_gates, j + 1)
                sp.wait_ge(s_kv, j)
                sp.wait_ge(s_h0, j)
                for hh in range(2):
                    for odd in range(2):
                        src = gx[64 * hh + 32 * odd:64 * hh + 32 * odd + 32, :, :, :].rearrange(
                            "p g (c b) t -> p g c (b t)", c=2)
                        for r in range(2):
                            rows = slice(64 * hh + 32 * r, 64 * hh + 32 * r + 32)
                            dst = gd[rows, :, odd::2, :, :].rearrange("p g c b t -> p g c (b t)")
                            sp.dma_start(dst, src).then_inc(s_exp, 16)

            spread_gates(0)
            with sp.Fori(1, GROUPS) as j:
                spread_gates(j)

        @block.tensor
        def _(pe):
            pe.wait_ge(s_load, LOADS)
            for j in range(TILES):
                t = pe.transpose(pb[j // 4][:, (j % 4) * ROWS:(j % 4 + 1) * ROWS], x1[:, j, :], ident[0:ROWS, 0:ROWS])
                if j % 4 == 3:
                    t.then_inc(s_xt_ps, 1)
            pe.sem_inc(s_Y, 2)
            pe.wait_ge(s_xt, 4)
            pe.wait_ge(s_pads, 4)
            pe.wait_ge(s_signs, 8)

            def front(g, f0, silu_idx, known):
                par = f0 % 2 if isinstance(f0, int) else 1
                if known:
                    pe.wait_ge(s_pevac, 2 * (f0 - 1))
                pe.matmul(pb[par][:, 0:GT], win[:], xT[:, bass.ds(g * GT, GT)], start=True, stop=True).then_inc(s_pfill, 1)
                pe.wait_ge(s_silu, silu_idx + 1)
                for k in range(10):
                    f, bank = f0 + 1 + k, pb[(par + 1 + k) % 2]
                    if known or k >= 1:
                        pe.wait_ge(s_pevac, 2 * (f - 1))
                    for c in range(2):
                        w = wgate[:, k, c, :] if k < 2 else wqk[:, (k - 2) // 2, 2 * (k % 2) + c, :]
                        m = pe.matmul(bank[:, c * GT:(c + 1) * GT], w, uT[:, :, 0:TIME], start=(c == 0), stop=(c == 1),
                                      skip_group_check=True)
                    m.then_inc(s_pfill, 1)

            def values(g, f0):
                pe.wait_ge(s_us, 8 * g + 8)
                for k in range(2 * GB):
                    b, tile = k // 2, k % 2
                    pe.wait_ge(s_vevac, f0 + k - 1) if not isinstance(f0, int) or f0 + k >= 2 else None
                    pe.matmul(pb[2 + k % 2][:, 0:512], uS[:, b, 4 * tile:4 * tile + 4, :], wv[:],
                              start=True, stop=True).then_inc(s_vfill, 1)

            def scores(u, tile):
                pair, hh = u // 2, u % 2
                rows = slice(64 * hh, 64 * hh + 64)
                bank = pb[4 + tile][:, :].rearrange("p (b v t) -> p b v t", b=GB, v=2)
                for b in range(GB):
                    pbi = pair * GB + b
                    for q in range(4):
                        slot, prt = 4 * tile + q, slice(32 * q, 32 * q + 32)
                        if slot < 6:
                            h = HALVES[slot]
                            out = bank[prt, b, :, :].rearrange("p v (n two h) -> p v n two h", two=2, h=h)[:, :, :, 1, :]
                            lhs = kl[rows, slot, pbi, :]
                            rhs = ql[rows, slot, :, pbi, :].rearrange("p v (n h) -> p v n h", h=h)
                        else:
                            d = slice(32 * (slot - 6), 32 * (slot - 6) + 32)
                            out, lhs, rhs = bank[prt, b, :, d], kd[rows, pbi, d], qd[rows, :, pbi, d]
                        m = pe.matmul(out, lhs, rhs, start=True, stop=True, skip_group_check=True)
                m.then_inc(s_S, 1)

            def mix(g, u, tile):
                pair, hh = u // 2, u % 2
                pe.wait_ge(s_mask, 16 * g + 2 * u + tile + 3)
                for b in range(GB):
                    c0 = (pair % 2) * GT + b * TIME
                    for v, vt in enumerate((v1, v2)):
                        m = pe.matmul(pb[6 + pair // 2][64 * hh:64 * hh + 64, c0:c0 + TIME],
                                      vt[:, 2 * b + tile, 64 * u:64 * u + 64],
                                      sm[:, (2 * u + tile) % 4, b, v, 0:TIME],
                                      start=False, stop=True, skip_group_check=True)
                if tile == 1:
                    m.then_inc(s_Y, 1)

            def body(g):
                last, before = isinstance(g, int) and g == GROUPS - 1, isinstance(g, int) and g >= GROUPS - 2
                pe.wait_ge(s_lev, g + 1)
                pe.wait_ge(s_diag, 2 * g + 2)
                pe.wait_ge(s_mask, 16 * g + 2)
                pe.wait_ge(s_yev, 2 * g)
                for pair in range(PAIRS):
                    m = pe.matmul(pb[6 + pair // 2][:, (pair % 2) * GT:(pair % 2 + 1) * GT], h0[:, pair, :],
                                  qf[:, pair, :, 0:TIME], start=(pair % 2 == 0), stop=True, skip_group_check=True)
                m.then_inc(s_h0, 1)
                for tile in range(2):
                    scores(0, tile)
                pe.wait_ge(s_vevac, vbase(g))
                pe.wait_ge(s_v2, 8 * g + 8)
                for u in range(8):
                    for tile in range(2):
                        mix(g, u, tile)
                        if u + 1 < 8:
                            scores(u + 1, tile)
                f = pbase(g)
                zb = pb[1] if last else pb[0]
                pe.wait_ge(s_yev, 2 * g + 2)
                pe.wait_ge(s_pevac, 2 * (f - 1))
                for pair in range(PAIRS):
                    m = pe.matmul(zb[:, 0:GT], wy[:, pair, :], ysb[:, pair, :], start=(pair == 0), stop=(pair == PAIRS - 1))
                m.then_inc(s_pfill, 1)
                if not before:
                    front(g + 2, f + 1, silu_base(g) + 1, True)
                if not last:
                    values(g + 1, vbase(g))
                pe.wait_ge(s_silu, silu_base(g) + 1)
                for tl in range(2):
                    fv = vbase(g) + (0 if last else 8) + tl
                    pe.wait_ge(s_vevac, fv - 1)
                    pe.matmul(pb[2 + tl][0:ROWS, 0:DM], z2[:, tl * ROWS:(tl + 1) * ROWS], wout[:],
                              start=True, stop=True).then_inc(s_vfill, 1)

            front(0, 0, 0, False)
            values(0, 0)
            front(1, FRONT, 1, True)
            body(0)
            with pe.Fori(1, GROUPS - 2) as g:
                body(g)
            body(GROUPS - 2)
            body(GROUPS - 1)

            for j in range(TILES):
                if j % 4 == 0:
                    pe.wait_ge(s_x1, j + 4)
                t = pe.transpose(pb[j // 4][:, (j % 4) * ROWS:(j % 4 + 1) * ROWS], x1[:, j, :], ident[0:ROWS, 0:ROWS])
                if j % 4 == 3:
                    t.then_inc(s_x1T_ps, 1)

        @block.scalar
        def _(act):
            act.wait_ge(s_load, LOADS)
            act.wait_ge(s_pads, 4)
            act.wait_ge(s_signs, 8)

            def silu(idx, count, bank, bias):
                act.wait_ge(s_pfill, count)
                if not (isinstance(idx, int) and idx == 0):
                    act.wait_ge(s_silu, idx)
                act.activation(silu_a[:], bank[:, 0:GT], ACT.Sigmoid, bias=bias).then_inc(s_pevac, 1)
                act.activation(silu_b[:], bank[:, 0:GT], ACT.Identity, bias=bias).then_inc(s_pevac, 1)

            def front(g, f0, idx):
                par = f0 % 2 if isinstance(f0, int) else 1
                silu(idx, f0 + 1, pb[par], bcol[:, 0:1])
                for k in range(10):
                    act.wait_ge(s_pfill, f0 + 2 + k)
                    bank = pb[(par + 1 + k) % 2]
                    if k == 0:
                        act.wait_ge(s_pp, g)
                    if k == 2:
                        act.wait_ge(s_qv, g)
                        act.wait_ge(s_kv, g)
                    for c in range(2):
                        src = bank[:, c * GT:(c + 1) * GT].rearrange("p (b t) -> p b t", b=GB)
                        if k < 2:
                            i = act.activation(ag[:, k, c * GB:(c + 1) * GB, 0:TIME], src, ACT.Identity,
                                               bias=bgate[:, 2 * k + c:2 * k + c + 1])
                        else:
                            kind, pair = (k - 2) // 2, 2 * (k % 2) + c
                            i = act.activation(qk[:, kind, pair, :, 0:TIME], src, ACT.Identity,
                                               bias=bqk[:, 4 * kind + pair:4 * kind + pair + 1])
                        i.then_inc(s_pevac, 1)
                act.wait_ge(s_mag, g)
                act.wait_ge(s_gates, g)
                act.wait_ge(s_pevac, 2 * (f0 + 3))
                for r in range(2):
                    act.activation(sq[:, r, :], ag[:, r, :, :].rearrange("p c t -> p (c t)"), ACT.Square).then_inc(s_sq, 1)
                act.wait_ge(s_mag, g + 1)
                act.activation(root[:], mag[:], ACT.Sqrt).then_inc(s_root, 1)

            def slot_tokens(g, idx):
                act.wait_ge(s_silu, idx + 1)
                for slot in range(SLOTS):
                    if slot < 6:
                        h = HALVES[slot]
                        src = uT[:].rearrange("p b (n two h) -> p b n two h", two=2, h=h)[:, :, :, 0, :]
                        dst = uS[:, :, slot, :].rearrange("p b (n h) -> p b n h", h=h)
                    else:
                        src, dst = uT[:, :, 32 * (slot - 6):32 * (slot - 6) + 32], uS[:, :, slot, :]
                    act.activation(dst, src, ACT.Copy).then_inc(s_us, 1)

            def diagonal(g):
                act.wait_ge(s_qv, g + 1)
                act.wait_ge(s_kv, g + 1)
                act.activation(qd[:].rearrange("p v c t -> p (v c t)"), qv[:].rearrange("p v c t -> p (v c t)"), ACT.Copy).then_inc(s_diag, 1)
                act.activation(kd[:].rearrange("p c t -> p (c t)"), kv[:].rearrange("p c t -> p (c t)"), ACT.Copy).then_inc(s_diag, 1)

            def turn_v(g, f0):
                for b in range(GB):
                    act.wait_ge(s_vevac, f0 + 2 * b + 2)
                    a = v1[:, 2 * b:2 * b + 2, :].rearrange("p k (h r e) -> p (k h) r e", r=2, e=DH)
                    o = v2[:, 2 * b:2 * b + 2, :].rearrange("p k (h r e) -> p (k h) r e", r=2, e=DH)
                    act.activation(o[:, :, 0, :], a[:, :, 1, :], ACT.Copy, scale=-1.0).then_inc(s_v2, 1)
                    act.activation(o[:, :, 1, :], a[:, :, 0, :], ACT.Copy).then_inc(s_v2, 1)

            def body(g):
                last, before = isinstance(g, int) and g == GROUPS - 1, isinstance(g, int) and g >= GROUPS - 2
                if not last:
                    act.wait_ge(s_vfill, vbase(g))
                    slot_tokens(g + 1, 2 * g)
                    act.wait_ge(s_S, 16 * g + 16)
                    diagonal(g + 1)
                act.wait_ge(s_Y, 2 + 8 * g + 8)
                for c in range(2):
                    act.activation(ysb[:, 2 * c:2 * c + 2, :], pb[6 + c][:, 0:2 * GT].rearrange("p (c t) -> p c t", c=2),
                                   ACT.Copy).then_inc(s_yev, 1)
                f = pbase(g)
                silu(silu_base(g), f + 1, pb[1] if last else pb[0], bcol[:, 1:2])
                if not before:
                    front(g + 2, f + 1, silu_base(g) + 1)
                if not last:
                    turn_v(g + 1, vbase(g))

            front(0, 0, 0)
            slot_tokens(0, 0)
            diagonal(0)
            turn_v(0, 0)
            front(1, FRONT, 1)
            body(0)
            with act.Fori(1, GROUPS - 2) as g:
                body(g)
            body(GROUPS - 2)
            body(GROUPS - 1)
            act.wait_ge(s_ln, TILES + 1)
            act.activation(rstd[:], rstd[:], ACT.Sqrt).then_inc(s_root1, 1)

        @block.gpsimd
        def _(pool):
            pool.memset(h0[:], 0.0).then_inc(s_pads, 1)
            pool.wait_ge(s_pads, 1)
            pool.memset(uT[:], 0.0).then_inc(s_pads, 1)
            pool.memset(qk[:], 0.0).then_inc(s_pads, 1)
            pool.memset(ag[:], 1.0).then_inc(s_pads, 1)
            pool.wait_ge(s_load, LOADS)
            pool.wait_ge(s_xt_ps, 4)
            ch = Chain(pool, s_pool, 0)
            ch.step(pool.tensor_tensor(x1[:], x1[:], spread(bout[0:ROWS, :], 1, TILES), ALU.add))

            def silu(fill, out):
                pool.wait_ge(s_pevac, 2 * fill + 2)
                pool.tensor_tensor(out, silu_a[:].rearrange("p (b t) -> p b t", b=GB),
                                   silu_b[:].rearrange("p (b t) -> p b t", b=GB), ALU.mult).then_inc(s_silu, 1)

            def squares(g):
                pool.wait_ge(s_sq, 2 * g + 2)
                pool.wait_ge(s_pp, g)
                pool.tensor_tensor(mag[:], sq[:, 0, :], sq[:, 1, :], ALU.add).then_inc(s_mag, 1)

            def turn_k(g, base):
                c = Chain(pool, s_pool, base)
                pool.wait_ge(s_exp, 128 * g + 128)
                pool.wait_ge(s_pevac, 2 * front_end(g))
                ka, kb = (qk[:, i].rearrange("p a b t -> p (a b t)") for i in (2, 3))
                c.step(pool.tensor_tensor(ka, ka, gd[:, 1].rearrange("p a b t -> p (a b t)"), ALU.mult))
                c.step(pool.tensor_tensor(kb, kb, gd[:, 2].rearrange("p a b t -> p (a b t)"), ALU.mult))
                c.wait()
                if not (isinstance(g, int) and g == 0):
                    pool.wait_ge(s_diag, 2 * g)
                    pool.wait_ge(s_lev, g)
                pool.tensor_tensor(kv[:].rearrange("p c t -> p (c t)"), ka, kb, ALU.add).then_inc(s_kv, 1)

            def u_of(g, fill, pfills):
                if pfills is not None:
                    pool.wait_ge(s_pfill, pfills)
                pool.wait_ge(s_us, 8 * g)
                silu(fill, uT[:, :, 0:TIME])

            u_of(0, 0, None)
            squares(0)
            turn_k(0, 1)
            u_of(1, FRONT, FRONT)
            squares(1)

            def body(g):
                last, before = isinstance(g, int) and g == GROUPS - 1, isinstance(g, int) and g >= GROUPS - 2
                if not last:
                    turn_k(g + 1, 3 + 2 * g)
                silu(pbase(g), z2[:].rearrange("p (b t) -> p b t", b=GB))
                if not before:
                    u_of(g + 2, pbase(g) + 1, 22 + 12 * g)
                    squares(g + 2)

            body(0)
            with pool.Fori(1, GROUPS - 2) as g:
                body(g)
            body(GROUPS - 2)
            body(GROUPS - 1)

        @block.vector
        def _(dve):
            dve.memset(pb[4][:, :], 0.0).then_inc(s_mask, 1)
            dve.memset(pb[5][:, :], 0.0).then_inc(s_mask, 1)
            dve.wait_ge(s_load, LOADS)
            for hh in range(2):
                im = slice(64 * hh + 32, 64 * hh + 64)
                dve.tensor_scalar(h0[im, :, 64 * hh + 32:64 * hh + 64], h0[im, :, 64 * hh + 32:64 * hh + 64], -1.0, None,
                                  ALU.mult).then_inc(s_signs, 1)
            for c in range(4):
                dve.wait_ge(s_xt_ps, c + 1)
                dve.tensor_copy(xT[:, c * 4 * ROWS:(c + 1) * 4 * ROWS], pb[c][:, 0:4 * ROWS]).then_inc(s_xt, 1)
            for kind in (0, 3):
                w = wqk[:, kind].rearrange("p a (hh r d) -> p a hh r d", hh=2, r=2)[:, :, :, 1, :]
                dve.tensor_scalar(w, w, -1.0, None, ALU.mult).then_inc(s_signs, 1)
                for hh in range(2):
                    b = bqk[64 * hh + 32:64 * hh + 64, 4 * kind:4 * kind + 4]
                    dve.tensor_scalar(b, b, -1.0, None, ALU.mult).then_inc(s_signs, 1)

            def cmul_split(c, t, out0, out1):
                c.step(dve.tensor_tensor(out0, t[0][0], t[1][1], ALU.subtract))
                c.step(dve.tensor_tensor(out1, t[0][1], t[1][0], ALU.add))

            def gates_1(c, g):
                dve.wait_ge(s_root, g + 1)
                c.step(dve.tensor_scalar(den, mag[:], 1.0, None, ALU.add))
                c.wait()
                c.step(dve.tensor_tensor(inv, root[:], den, ALU.mult))
                c.wait()
                c.step(dve.reciprocal(inv, inv))
                c.wait()
                t = tmp[:, 0, 0:8 * TP]
                c.step(dve.tensor_tensor(t, inv, root[:], ALU.mult))
                c.step(dve.tensor_tensor(inv, inv, den, ALU.mult))
                c.wait()
                dve.wait_ge(s_exp, 128 * g)
                c.step(dve.tensor_tensor(gx[:, 0].rearrange("p c t -> p (c t)"), mag[:], t, ALU.mult))
                t = tmp[:, 1, 0:8 * TP]
                c.step(dve.tensor_tensor(t, inv, inv, ALU.mult))
                c.wait()
                c.step(dve.tensor_tensor(t, t, mag[:], ALU.mult))
                c.wait()
                c.step(dve.tensor_scalar(t, t, -0.5, 1.5, ALU.mult, ALU.add))
                c.wait()
                c.step(dve.tensor_tensor(inv, inv, t, ALU.mult))
                c.wait()
                dve.tensor_tensor(pp[:].rearrange("p r c t -> p r (c t)"), ag[:].rearrange("p r c t -> p r (c t)"),
                                  spread(inv, 1, 2), ALU.mult).then_inc(s_pp, 1)

            def eighths(t):
                return t.rearrange("p r c (n j) -> p r (c n) j", j=8)

            def gates_2(c, g):
                run, one = eighths(gx[:, 1:3]), eighths(pp[:])
                dve.wait_ge(s_pp, g + 1)
                c.step(dve.tensor_copy(run[:, :, :, 0], one[:, :, :, 0]))
                c.wait()
                ta, tb = tmp[:, :, 0:64], tmp[:, :, 64:128]
                for j in range(1, 8):
                    c.step(dve.tensor_tensor(ta, run[:, :, :, j - 1], spread(one[:, 0, :, j], 1, 2), ALU.mult))
                    c.step(dve.tensor_tensor(tb, run[:, :, :, j - 1], spread(one[:, 1, :, j], 1, 2), ALU.mult))
                    c.wait()
                    cmul_split(c, ((ta[:, 0], ta[:, 1]), (tb[:, 0], tb[:, 1])), run[:, 0, :, j], run[:, 1, :, j])
                    c.wait()

            def gates_3(c, g):
                run = gx[:, 1:3].rearrange("p r c (n j) -> p r c n j", j=8)
                c.step(dve.memset(bp[:, 0, :, 0], 1.0))
                c.step(dve.memset(bp[:, 1, :, 0], 0.0))
                c.wait()
                ta, tb = tmp[:, :, 0:8], tmp[:, :, 64:72]
                for n in range(1, 8):
                    c.step(dve.tensor_tensor(ta, bp[:, :, :, n - 1], spread(run[:, 0, :, n - 1, 7], 1, 2), ALU.mult))
                    c.step(dve.tensor_tensor(tb, bp[:, :, :, n - 1], spread(run[:, 1, :, n - 1, 7], 1, 2), ALU.mult))
                    c.wait()
                    cmul_split(c, ((ta[:, 0], ta[:, 1]), (tb[:, 0], tb[:, 1])), bp[:, 0, :, n], bp[:, 1, :, n])
                    c.wait()
                run, b = eighths(gx[:, 1:3]), bp[:].rearrange("p r c n -> p r (c n)")
                ta = tmp[:, :, 0:512].rearrange("p r (m j) -> p r m j", j=8)
                tb = tmp[:, :, 512:1024].rearrange("p r (m j) -> p r m j", j=8)
                for r in range(2):
                    c.step(dve.tensor_tensor(ta[:, r], run[:, r], spread(b[:, 0], 2, 8), ALU.mult))
                    c.step(dve.tensor_tensor(tb[:, r], run[:, r], spread(b[:, 1], 2, 8), ALU.mult))
                c.wait()
                c.step(dve.tensor_tensor(run[:, 0], ta[:, 0], tb[:, 1], ALU.subtract))
                c.wait()
                dve.tensor_tensor(run[:, 1], ta[:, 1], tb[:, 0], ALU.add).then_inc(s_gates, 1)

            def turn_q(c, g, half):
                def flat(a):
                    return a.rearrange("p a b t -> p (a b t)")
                dve.wait_ge(s_exp, 128 * g + 128)
                dve.wait_ge(s_pevac, 2 * front_end(g))
                qa, qc, cr, ci = flat(qk[:, 0]), flat(qk[:, 1]), flat(gd[:, 1]), flat(gd[:, 2])
                out = qv[:].rearrange("p v c t -> p v (c t)")
                if not (isinstance(g, int) and g == 0):
                    dve.wait_ge(s_diag, 2 * g)
                if half == 0:
                    c.step(dve.tensor_tensor(tmp[:, 0], qa, cr, ALU.mult))
                    c.step(dve.tensor_tensor(tmp[:, 1], qc, ci, ALU.mult))
                    c.wait()
                    c.step(dve.tensor_tensor(out[:, 0], tmp[:, 0], tmp[:, 1], ALU.subtract))
                else:
                    c.wait()
                    c.step(dve.tensor_tensor(tmp[:, 0], qc, cr, ALU.mult))
                    c.step(dve.tensor_tensor(tmp[:, 1], qa, ci, ALU.mult))
                    c.wait()
                    dve.tensor_tensor(out[:, 1], tmp[:, 0], tmp[:, 1], ALU.add).then_inc(s_qv, 1)

            def levels(c, g, sizes):
                pre = gd[:, 0].rearrange("p a b t -> p (a b t)")
                for h in sizes:
                    slot, n = HALVES.index(h), PB * TP // (2 * h)
                    pv = pre.rearrange("p (n two h) -> p n two h", two=2, h=h)
                    sv = suf[:].rearrange("p (n two h) -> p n two h", two=2, h=h)
                    qs = qv[:].rearrange("p v c (n two h) -> p v (c n) two h", two=2, h=h)[:, :, :, 1, :]
                    ks = kv[:].rearrange("p c (n two h) -> p (c n) two h", two=2, h=h)[:, :, 0, :]
                    qo = ql[:, slot].rearrange("p v c (n h) -> p v (c n) h", h=h)
                    ko = kl[:, slot].rearrange("p c (n h) -> p (c n) h", h=h)
                    for v in range(2):
                        c.step(dve.tensor_tensor(qo[:, v], qs[:, v], pv[:, :, 1, :], ALU.mult))
                    total = spread(pv[:, :, 1, h - 1], 2, h)
                    if h == 1:
                        c.step(dve.tensor_copy(ko, ks))
                        c.step(dve.memset(sv[:, :, 1, :], 1.0))
                        c.step(dve.tensor_copy(sv[:, :, 0, :], total))
                    else:
                        c.step(dve.tensor_tensor(ko, ks, sv[:, :, 0, :], ALU.mult))
                        c.wait()
                        c.step(dve.tensor_tensor(sv[:, :, 0, :], sv[:, :, 0, :], total, ALU.mult))
                    c.wait()
                    c.step(dve.tensor_tensor(pv[:, :, 1, :], pv[:, :, 1, :], spread(pv[:, :, 0, h - 1], 2, h), ALU.mult))
                    c.wait()

            def levels_last(c, g):
                dve.tensor_tensor(qf.rearrange("p a b t -> p (a b t)"), qv[:, 0].rearrange("p c t -> p (c t)"),
                                  gd[:, 0].rearrange("p a b t -> p (a b t)"), ALU.mult).then_inc(s_lev, 1)

            def values(g, f0):
                for k in range(2 * GB):
                    dve.wait_ge(s_vfill, f0 + k + 1)
                    dve.tensor_tensor(v1[:, k, :], pb[2 + k % 2][:, 0:512], bv[:], ALU.add).then_inc(s_vevac, 1)

            def masked(g, u):
                for tile in range(2):
                    dve.wait_ge(s_S, 16 * g + 2 * u + tile + 1)
                    dve.wait_ge(s_Y, 8 * g + u + 1)
                    dve.tensor_tensor(sm[:, (2 * u + tile) % 4].rearrange("p b v t -> p (b v) t"),
                                      pb[4 + tile][:, :].rearrange("p (b t) -> p b t", t=TP),
                                      spread(mask[:, tile, :], 1, 2 * GB), ALU.mult).then_inc(s_mask, 1)

            def residual(g, last):
                dve.wait_ge(s_pool, 1)
                for tl in range(2):
                    fv = vbase(g) + (0 if last else 8) + tl
                    dve.wait_ge(s_vfill, fv + 1)
                    j = 2 * g + tl
                    dve.tensor_tensor(x1[:, bass.ds(j, 1), :].rearrange("p a d -> p (a d)"), pb[2 + tl][0:ROWS, 0:DM],
                                      x1[:, bass.ds(j, 1), :].rearrange("p a d -> p (a d)"), ALU.add).then_inc(s_vevac, 1)
                    dve.wait_ge(s_vevac, fv + 1)
                    dve.bn_stats(stats[:, bass.ds(j, 1), :].rearrange("p a d -> p (a d)"),
                                 x1[:, bass.ds(j, 1), :].rearrange("p a d -> p (a d)")).then_inc(s_stats, 1)

            c = Chain(dve, s_dve, 0)
            dve.wait_ge(s_pads, 4)
            gates_1(c, 0)
            gates_2(c, 0)
            gates_3(c, 0)
            turn_q(c, 0, 0)
            turn_q(c, 0, 1)
            dve.wait_ge(s_qv, 1)
            dve.wait_ge(s_kv, 1)
            levels(c, 0, [1, 2, 4])
            values(0, 0)
            levels(c, 0, [8, 16, 32])
            levels_last(c, 0)
            STEPS = c.n

            def body(g):
                last = isinstance(g, int) and g == GROUPS - 1
                c = Chain(dve, s_dve, STEPS + g * STEPS)
                for u in range(8):
                    if not last:
                        if u == 0:
                            dve.wait_ge(s_lev, g + 1)
                            gates_1(c, g + 1)
                        if u == 1:
                            gates_2(c, g + 1)
                        if u == 3:
                            gates_3(c, g + 1)
                        if u == 6:
                            turn_q(c, g + 1, 0)
                        if u == 7:
                            turn_q(c, g + 1, 1)
                    masked(g, u)
                if not last:
                    dve.wait_ge(s_qv, g + 2)
                    dve.wait_ge(s_kv, g + 2)
                    dve.wait_ge(s_S, 16 * g + 16)
                    levels(c, g + 1, [1, 2, 4])
                    values(g + 1, vbase(g))
                    levels(c, g + 1, [8, 16, 32])
                    levels_last(c, g + 1)
                residual(g, last)
                assert last or c.n == STEPS

            body(0)
            with dve.Fori(1, GROUPS - 2) as g:
                body(g)
            body(GROUPS - 2)
            body(GROUPS - 1)
            dve.wait_ge(s_stats, TILES)
            for j in range(TILES):
                dve.bn_aggr(mv[:, j, :], stats[:, j, :]).then_inc(s_ln, 1)
            dve.wait_ge(s_ln, TILES)
            dve.tensor_scalar(rstd[:], mv[:, :, 1], EPS, None, ALU.add).then_inc(s_ln, 1)
            dve.wait_ge(s_root1, 1)
            dve.reciprocal(rstd[:], rstd[:]).then_inc(s_ln, 1)
            dve.wait_ge(s_ln, TILES + 2)
            for j in range(TILES):
                dve.tensor_scalar(x1[:, j, :], x1[:, j, :], mv[:, j, 0:1], rstd[:, j:j + 1], ALU.subtract, ALU.mult).then_inc(s_x1, 1)
            for c in range(4):
                dve.wait_ge(s_x1T_ps, c + 1)
                dve.tensor_copy(x1T[:, c * 4 * ROWS:(c + 1) * 4 * ROWS], pb[c][:, 0:4 * ROWS]).then_inc(s_x1T, 1)



def cross(nc, io, keep, late, psum, pb):
    x1, x1T = keep["x1"], keep["xT"]
    QN = 4
    HQ = XH // QN
    S_FILLS = 9
    with ExitStack() as ctx:
        def sb(name, shape, dt=F32):
            return ctx.enter_context(nc.sbuf_tensor("x_" + name, shape, dt))

        def sem(name):
            return ctx.enter_context(nc.semaphore("x_" + name))

        wq = sb("wq", [128, QN, 96])
        wk, wvx, wo = sb("wk", [128, 128]), sb("wv", [128, 128]), sb("wo", [128, 128])
        wom = sb("wom", [128, HQ, 128])
        qr = sb("qr", [96, QN, TOKENS], F32R)
        qbd = [sb(f"qbd{i}", [96, QN, HQ, TIME], F32R) for i in range(2)]
        raw = [sb(f"ctx{i}", [KP, KT_N, DM]) for i in range(2)]
        ctxT = [sb(f"ctxT{i}", [128, CTX]) for i in range(2)]
        khi = [sb(f"khi{i}", [128, CTX], F32R) for i in range(2)]
        klo = [sb(f"klo{i}", [128, CTX], F32R) for i in range(2)]
        k3 = [sb(f"k3_{i}", [96, QN, CTX], F32R) for i in range(2)]
        vx = [sb(f"v{i}", [KP, KT_N, 128]) for i in range(2)]
        probs = [sb(f"probs{i}", [KP, QN * QC]) for i in range(3)]
        o_sb = sb("o", [128, HQ, 2, TIME])
        stats, mv, rstd = sb("stats", [ROWS, TILES, 6]), sb("mv", [ROWS, TILES, 2]), sb("rstd", [ROWS, TILES])

        s_w, s_wom = sem("weights_loaded"), sem("wo_masked")
        s_ctx = [sem("ctx_loaded0"), sem("ctx_loaded1")]
        s_qf, s_qhi, s_qlo, s_qbd = sem("q_filled"), sem("q_hi"), sem("q_split"), sem("q_blocks")
        s_stage, s_read, s_khi = sem("staged"), sem("stage_read"), sem("k_hi")
        s_k3 = [sem("k_stacked0"), sem("k_stacked1")]
        s_qk, s_act, s_pv = sem("scores_made"), sem("probs_made"), sem("pv_done")
        s_oev, s_out, s_res, s_stats = sem("o_read"), sem("out_made"), sem("residual_added"), sem("stats_ready")
        s_ln, s_root, s_norm, s_x2 = sem("ln_chain"), sem("rstd_root"), sem("normed"), sem("x2_stored")

        bank_stage = [pb[5], pb[6]]

        def sfill(n):
            return 15 + S_FILLS * n

        def stacked(n, par):
            return 96 * (n - par) + 192

        block = ctx.enter_context(nc.Block())

        @block.sync
        def _(sp):
            for dst, src in ((wq, "xq3"), (wk, "xk"), (wvx, "xv"), (wo, "xo")):
                sp.dma_start(dst[:], io[src]).then_inc(s_w, 16)

            def context(m, par):
                sp.dma_start(raw[par][:], io["ctx"][m].rearrange("(p k) d -> p k d", k=KT_N) if isinstance(m, int) else
                             io["ctx"][bass.ds(m, 1)].rearrange("a (p k) d -> p (a k) d", k=KT_N)).then_inc(s_ctx[par], 16)

            def stack(par):
                for part, half in enumerate((khi, khi, klo)):
                    for q in range(QN):
                        sp.dma_start(k3[par][32 * part:32 * part + 32, q, :].bitcast(F32), half[par][32 * q:32 * q + 32, :].bitcast(F32)).then_inc(s_k3[par], 16)

            context(0, 0)
            context(1, 1)
            for m in range(2):
                sp.wait_ge(s_read, 2 + 9 * m + 6)
                stack(m)
                context_wait = 9 * m + 4
                sp.wait_ge(s_stage, context_wait)
                context(m + 2, m)
            for (dst, src) in late["loads"]:
                sp.dma_start(dst, src).then_inc(late["sem"], 16)

            def pair(i, last):
                for par in range(2):
                    m = 2 * i + par
                    sp.wait_ge(s_read, 2 + 9 * m + 6)
                    sp.wait_ge(s_qk, 12 * m - 12)
                    stack(par)
                    if not last:
                        sp.wait_ge(s_stage, 9 * m + 4)
                        context(m + 2, par)

            with sp.Fori(1, TILES - 1) as i:
                pair(i, False)
            pair(TILES - 1, True)
            sp.wait_ge(s_norm, TILES)
            sp.dma_start(late["x2d"].rearrange("(j r) d -> r j d", r=ROWS), x1[:]).then_inc(s_x2, 16)
            sp.wait_ge(s_x2, 16)
            sp.wait_ge(late["sem"], 16 * len(late["loads"]))

        @block.tensor
        def _(pe):
            pe.wait_ge(s_w, 64)
            for f in range(16):
                q, c = f // 4, f % 4
                if f >= 4:
                    pe.wait_ge(s_qlo, f - 3)
                pe.matmul(pb[f % 4][0:96, 0:4 * ROWS], wq[:, q, :], x1T[:, c * 4 * ROWS:(c + 1) * 4 * ROWS],
                          start=True, stop=True).then_inc(s_qf, 1)
            pe.sem_inc(s_pv, 3)
            pe.wait_ge(s_qlo, 16)

            def transposes(m, par, c, f):
                if c == 0:
                    pe.wait_ge(s_ctx[par], 16 * (m // 2 + 1) if isinstance(m, int) else 8 * (m - par) + 16)
                pe.wait_ge(s_read, f + 1)
                for t in range(4):
                    i = pe.transpose(bank_stage[fpar(f)][:, t * KP:(t + 1) * KP], raw[par][:, 4 * c + t, :], keep["ident"][0:KP, 0:KP])
                i.then_inc(s_stage, 1)

            parity = [0]

            def fpar(f):
                return parity[0] % 2

            def keys(par, c, f, after):
                pe.wait_ge(s_read, after + 3)
                pe.wait_ge(s_read, f + 1)
                pe.matmul(bank_stage[fpar(f)][:, 0:CH], wk[:], ctxT[par][:, c * CH:(c + 1) * CH], start=True, stop=True).then_inc(s_stage, 1)

            def vals(par, c, f):
                pe.wait_ge(s_read, f + 1)
                for t in range(4):
                    col = (4 * c + t) * KP
                    i = pe.matmul(bank_stage[fpar(f)][0:KP, t * 128:(t + 1) * 128], ctxT[par][:, col:col + KP], wvx[:],
                                  start=True, stop=True, skip_group_check=True)
                i.then_inc(s_stage, 1)

            def piece(n, par, k, f, has_v, has_tk):
                if k < 3 and has_v:
                    vals(1 - par, k, f)
                elif k >= 3 and has_tk:
                    what = ("T0", "T1", "K0", "T2", "K1", "K2")[k - 3]
                    c = int(what[1])
                    if what[0] == "T":
                        transposes(n + 2, par, c, f)
                    else:
                        keys(par, c, f, f - {0: 2, 1: 3, 2: 2}[c])
                parity[0] += 1

            f = 0
            for m in range(2):
                for k in range(3, 9):
                    piece(m - 2, m, k, f, True, True)
                    f += 1
                if m == 0:
                    for k in range(3):
                        piece(-1, 1, k, f, True, True)
                        f += 1

            def out_proj(i):
                pe.wait_ge(s_oev, 2 * i + 2)
                pe.wait_ge(s_res, i)
                for h in range(HQ):
                    m = pe.matmul(pb[7][0:ROWS, 0:DM], o_sb[:, h, :, :].rearrange("p b t -> p (b t)"), wom[:, h, :],
                                  start=(h == 0), stop=(h == HQ - 1))
                m.then_inc(s_out, 1)

            def pv(n, par, k):
                T = 12 * n + k
                pe.wait_ge(s_act, T + 3)
                if k == 0:
                    pe.wait_ge(s_oev, n)
                for q in range(QN):
                    m = pe.matmul(pb[4][32 * q:32 * q + 32, 0:QC], vx[par][:, k, 32 * q:32 * q + 32],
                                  probs[k % 3][:, q * QC:(q + 1) * QC], start=(k == 0), stop=(k == KT_N - 1))
                m.then_inc(s_pv, 1)

            def batch(n, par, first, has_v, has_tk):
                parity[0] = 1 + par
                pe.wait_ge(s_qbd, n + 1)
                pe.wait_ge(s_k3[par], stacked(n, par))
                for k in range(KT_N):
                    T = 12 * n + k
                    pe.wait_ge(s_act, T + 1)
                    for q in range(QN):
                        m = pe.matmul(pb[2 * (k % 2) + q // 2][0:KP, (q % 2) * QC:(q % 2 + 1) * QC],
                                      k3[par][:, q, k * KP:(k + 1) * KP], qbd[par][:, q, :, :].rearrange("p h t -> p (h t)"),
                                      start=(q % 2 == 0), stop=True, skip_group_check=True)
                    m.then_inc(s_qk, 1)
                    if k < 9:
                        piece(n, par, k, sfill(n) + k, has_v, has_tk)
                    if k == 2 and par == 0 and not first:
                        out_proj((n - 1) // 2 if isinstance(n, int) else pair_of[0] - 1)
                    if k >= 1:
                        if k == 1:
                            pe.wait_ge(s_read, 2 + (sfill(n) - 6 if not (isinstance(n, int) and n == 0) else 9))
                        pv(n, par, k - 1)
                pv(n, par, KT_N - 1)

            pair_of = [0]

            def pair(i, first, last):
                pair_of[0] = i
                batch(2 * i, 0, first, True, not last)
                batch(2 * i + 1, 1, first, not last, not last)

            pair(0, True, False)
            with pe.Fori(1, TILES - 1) as i:
                pair(i, False, False)
            pair(TILES - 1, False, True)
            out_proj(TILES - 1)

        @block.scalar
        def _(act):
            act.sem_inc(s_act, 2)
            for f in range(16):
                q, c = f // 4, f % 4
                act.wait_ge(s_qf, f + 1)
                act.activation(qr[:, q, c * 4 * ROWS:(c + 1) * 4 * ROWS], pb[f % 4][0:96, 0:4 * ROWS], ACT.Copy).then_inc(s_qhi, 1)

            def k_hi(par, c, f, bank):
                act.wait_ge(s_stage, f + 1)
                act.activation(khi[par][:, c * CH:(c + 1) * CH], bank[:, 0:CH], ACT.Copy).then_inc(s_khi, 1)

            for m in range(2):
                for c, k in ((0, 2), (1, 4), (2, 5)):
                    f = 9 * m + k
                    k_hi(m, c, f, bank_stage[f % 2])

            def batch(n, par, has_tk):
                for k in range(KT_N):
                    T = 12 * n + k
                    act.wait_ge(s_qk, T + 1)
                    act.wait_ge(s_pv, T + 1)
                    src = psum[0:KP, 1024 * (k % 2):1024 * (k % 2) + 1024].rearrange("p (a c) -> p a c", a=2)[:, :, 0:2 * QC]
                    act.activation(probs[k % 3][:].rearrange("p (a c) -> p a c", a=2), src, ACT.Sigmoid, scale=XSCALE).then_inc(s_act, 1)
                    if has_tk and k in (5, 7, 8):
                        if k == 5:
                            act.wait_ge(s_k3[par], stacked(n, par))
                        k_hi(par, {5: 0, 7: 1, 8: 2}[k], sfill(n) + k, bank_stage[(1 + par + k) % 2])

            with act.Fori(0, TILES - 1) as i:
                batch(2 * i, 0, True)
                batch(2 * i + 1, 1, True)
            batch(2 * TILES - 2, 0, False)
            batch(2 * TILES - 1, 1, False)
            act.wait_ge(s_ln, TILES + 1)
            act.activation(rstd[:], rstd[:], ACT.Sqrt).then_inc(s_root, 1)

        @block.vector
        def _(dve):
            dve.sem_inc(s_read, 2)
            for f in range(16):
                q, c = f // 4, f % 4
                cols = slice(c * 4 * ROWS, (c + 1) * 4 * ROWS)
                dve.wait_ge(s_qhi, f + 1)
                dve.tensor_tensor(qr[32:64, q, cols], pb[f % 4][32:64, 0:4 * ROWS], qr[32:64, q, cols].bitcast(F32),
                                  ALU.subtract).then_inc(s_qlo, 1)
            dve.wait_ge(s_w, 64)
            for h in range(HQ):
                dve.tensor_scalar(wom[:, h, :], wo[:], keep["hmask"][:, h:h + 1], None, ALU.mult).then_inc(s_wom, 1)

            def blocks(n, par):
                src = qr[:, :, bass.ds(n * TIME, TIME)].bitcast(F32)
                dve.tensor_tensor(qbd[par][:], spread(src, 2, HQ),
                                  keep["hmask"][0:96, 0:HQ].unsqueeze(1).unsqueeze(3).broadcast_to([96, QN, HQ, TIME]), ALU.mult).then_inc(s_qbd, 1)

            def t_read(par, c, f, bank):
                dve.wait_ge(s_stage, f + 1)
                dve.tensor_copy(ctxT[par][:, c * CH:(c + 1) * CH], bank[:, 0:CH]).then_inc(s_read, 1)

            def k_lo(par, c, f, bank, khis):
                dve.wait_ge(s_khi, khis)
                dve.tensor_tensor(klo[par][:, c * CH:(c + 1) * CH], bank[:, 0:CH],
                                  khi[par][:, c * CH:(c + 1) * CH].bitcast(F32), ALU.subtract).then_inc(s_read, 1)

            def v_read(par, c, f, bank):
                dve.wait_ge(s_stage, f + 1)
                dve.tensor_copy(vx[par][:, 4 * c:4 * c + 4, :], bank[0:KP, :].rearrange("p (t d) -> p t d", t=4)).then_inc(s_read, 1)

            def tk(m, par, f, p):
                for k, what in enumerate(("T0", "T1", "K0", "T2", "K1", "K2")):
                    c, bank = int(what[1]), bank_stage[(p + k) % 2]
                    if what[0] == "T":
                        t_read(par, c, f + k, bank)
                    else:
                        k_lo(par, c, f + k, bank, 3 * m + c + 1)

            tk(0, 0, 0, 0)
            for c in range(3):
                v_read(0, c, 6 + c, bank_stage[(6 + c) % 2])
            tk(1, 1, 9, 1)
            dve.wait_ge(s_qlo, 16)
            blocks(0, 0)

            def batch(n, par, has_next, has_tk, i):
                if has_next:
                    dve.wait_ge(s_qk, 12 * n)
                    blocks(n + 1, 1 - par)
                    for c in range(3):
                        v_read(1 - par, c, sfill(n) + c, bank_stage[(1 + par + c) % 2])
                if has_tk:
                    dve.wait_ge(s_k3[par], stacked(n, par))
                    tk(n + 2, par, sfill(n) + 3, 1 + par + 3)
                if par == 0:
                    dve.wait_ge(s_out, i)
                dve.wait_ge(s_pv, 3 + 12 * n + 12)
                dve.tensor_copy(o_sb[:, :, par, :], pb[4][:, 0:QC].rearrange("p (h t) -> p h t", h=HQ)).then_inc(s_oev, 1)

            def residual(i):
                row = bass.ds(i, 1)
                dve.wait_ge(s_out, i + 1)
                dve.tensor_tensor(x1[:, row, :].rearrange("p a d -> p (a d)"), pb[7][0:ROWS, 0:DM],
                                  x1[:, row, :].rearrange("p a d -> p (a d)"), ALU.add).then_inc(s_res, 1)
                dve.wait_ge(s_res, i + 1)
                dve.bn_stats(stats[:, row, :].rearrange("p a d -> p (a d)"), x1[:, row, :].rearrange("p a d -> p (a d)")).then_inc(s_stats, 1)

            def pair(i, last):
                batch(2 * i, 0, True, not last, i)
                if not (isinstance(i, int) and i == 0):
                    residual(i - 1)
                batch(2 * i + 1, 1, not last, not last, i)

            pair(0, False)
            with dve.Fori(1, TILES - 1) as i:
                pair(i, False)
            pair(TILES - 1, True)
            residual(TILES - 1)
            dve.wait_ge(s_stats, TILES)
            for j in range(TILES):
                dve.bn_aggr(mv[:, j, :], stats[:, j, :]).then_inc(s_ln, 1)
            dve.wait_ge(s_ln, TILES)
            dve.tensor_scalar(rstd[:], mv[:, :, 1], EPS, None, ALU.add).then_inc(s_ln, 1)
            dve.wait_ge(s_root, 1)
            dve.reciprocal(rstd[:], rstd[:]).then_inc(s_ln, 1)
            dve.wait_ge(s_ln, TILES + 2)
            for j in range(TILES):
                dve.tensor_scalar(x1[:, j, :], x1[:, j, :], mv[:, j, 0:1], rstd[:, j:j + 1], ALU.subtract, ALU.mult).then_inc(s_norm, 1)



def experts(nc, io, keep, late, psum, pb):
    CE = CAP * EX
    KK = 4
    w = late["t"]
    with ExitStack() as ctx:
        def sb(name, shape, dt=F32):
            return ctx.enter_context(nc.sbuf_tensor("e_" + name, shape, dt))

        def sem(name):
            return ctx.enter_context(nc.semaphore("e_" + name))

        ident = keep["ident"]
        X2 = sb("x2", [128, KL, DM])
        X2T = sb("x2T", [128, KL, 128])
        lg = sb("lg", [128, KL, EX])
        red = sb("red", [128, KL])
        pr = sb("pr", [128, 16, CAP, EX])
        sc = sb("sc", [128, 16, BATCH])
        oh = sb("oh", [128, 16, BATCH])
        t1 = sb("t1", [128, 16, BATCH])
        i1, i2, m1 = sb("i1", [128, 16]), sb("i2", [128, 16]), sb("m1", [128, 16])
        ohn = sb("ohn", [128, 16, CE])
        hg = sb("hg", [128, CE, TIME])
        qkv = sb("qkv", [TIME, EX, CAP, 3 * EDH])
        ta, tb = sb("ta", [TIME, EX, EDH]), sb("tb", [TIME, EX, EDH])
        att = sb("att", [TIME, EX, CAP, CAP])
        attT = sb("attT", [64, TIME])
        am, asum = sb("am", [64, 1]), sb("asum", [64, 1])
        pT = sb("pT", [TIME, EX, CAP, CAP])
        av = sb("av", [TIME, CAP, EX, EDH])
        avT = sb("avT", [128, CAP, EX // 2, TIME])
        ao = sb("ao", [TIME, CE, DM])
        aoT = sb("aoT", [128, KK, 4, DM])
        y = sb("y", [128, KL, DM])
        stats, mv, rstd = sb("stats", [128, KL, 6]), sb("mv", [128, KL, 2]), sb("rstd", [128, KL])

        s_x2, s_x2T_ps, s_x2T = sem("x2_loaded"), sem("x2T_in_psum"), sem("x2T_ready")
        s_lg, s_sub, s_exp, s_pr, s_sc_ps, s_oh, s_ohn_ps, s_ohn = (sem(n) for n in (
            "logits", "logits_less_max", "exps", "probs", "probs_turned", "one_hot", "one_hot_turned", "one_hot_read"))
        s_hg_ps, s_hg, s_qkv_ps, s_qkv, s_att = (sem(n) for n in ("gathered", "gathered_read", "qkv_filled", "qkv_read", "att_ready"))
        s_attT, s_amax, s_aexp, s_asum, s_pn, s_pT_ps, s_pT = (sem(n) for n in (
            "att_turned", "att_max", "att_exp", "att_sum", "att_normed", "p_turned", "p_ready"))
        s_av, s_avT_ps, s_avT, s_ao_ps, s_ao, s_aod, s_aoT = (sem(n) for n in (
            "av_ready", "av_turned", "avT_ready", "ao_filled", "ao_read", "ao_stored", "ao_loaded"))
        s_y_ps, s_var, s_root, s_res, s_outn, s_fin = (sem(n) for n in ("scattered", "variance", "root", "residual", "out_normed", "out_stored"))
        s_dve = sem("dve_chain")
        s_pad = sem("pad_set")

        block = ctx.enter_context(nc.Block())

        @block.sync
        def _(sp):
            src = late["x2d"].rearrange("(n k q) d -> q n k d", k=KL, q=4)
            for q in range(4):
                sp.dma_start(X2[32 * q:32 * q + 32, :, :], src[q]).then_inc(s_x2, 16)
            sp.wait_ge(s_ao, 8)
            sp.dma_start(late["aod"][0:TIME].rearrange("l c d -> l (c d)"), ao[:].rearrange("l c d -> l (c d)")).then_inc(s_aod, 16)
            sp.wait_ge(s_aod, 16)
            src = late["aod"].rearrange("(kk k4 q) c d -> k4 c kk q d", kk=KK, k4=4)
            for k4 in range(4):
                n = KK if k4 < 2 else KK - 1
                for kk in range(n):
                    sp.dma_start(aoT[32 * k4:32 * k4 + 32, kk, :, :], src[k4][:, kk, :, :]).then_inc(s_aoT, 16)
            dst = io["out"].rearrange("n (k q) d -> q n k d", q=4)
            sp.wait_ge(s_outn, KL)
            for q in range(4):
                sp.dma_start(dst[q], y[32 * q:32 * q + 32, :, :]).then_inc(s_fin, 16)
            sp.wait_ge(s_fin, 64)

        @block.tensor
        def _(pe):
            pe.wait_ge(s_x2, 64)
            for k in range(KL):
                t = pe.transpose(pb[k // 4][:, (k % 4) * 128:(k % 4 + 1) * 128], X2[:, k, :], ident[:])
                if k % 4 == 3 or k == KL - 1:
                    t.then_inc(s_x2T_ps, 1)
            for k in range(KL):
                if k % 4 == 0:
                    pe.wait_ge(s_x2T, k // 4 + 1)
                m = pe.matmul(pb[4][:, k * EX:(k + 1) * EX], X2T[:, k, :], w["wg"][:], start=True, stop=True, skip_group_check=True)
            m.then_inc(s_lg, 1)
            pe.wait_ge(s_pr, 2)
            for kk in range(KK):
                t = pe.transpose(pb[5][:, kk * 128:(kk + 1) * 128], pr[:, 4 * kk:4 * kk + 4, :, :].rearrange("p k c e -> p (k c e)"), ident[:])
            t.then_inc(s_sc_ps, 1)
            pe.wait_ge(s_oh, 1)
            for kk in range(KK):
                t = pe.transpose(pb[6][:, kk * 128:(kk + 1) * 128], oh[:, 4 * kk:4 * kk + 4, :].rearrange("p q n -> p (q n)"), ident[:])
            t.then_inc(s_ohn_ps, 1)
            pe.wait_ge(s_ohn, 1)
            for k in range(KL):
                for q in range(4):
                    rows = slice(32 * q, 32 * q + 32)
                    m = pe.matmul(pb[q][:, k * CE:(k + 1) * CE], X2[rows, k, :], ohn[rows, k, :], start=True, stop=True, skip_group_check=True)
                    if k == KL - 1:
                        m.then_inc(s_hg_ps, 1)
            pe.wait_ge(s_hg, 4)
            for e in range(EX):
                if e >= 4:
                    pe.wait_ge(s_qkv, e - 3)
                for c in range(CAP):
                    m = pe.matmul(pb[4 + e % 4][0:TIME, c * 192:(c + 1) * 192], hg[:, c * EX + e, :], w["wqkv"][:, e, :],
                                  start=(c == 0), stop=True, skip_group_check=True)
                m.then_inc(s_qkv_ps, 1)
            pe.wait_ge(s_att, 4)
            pe.transpose(pb[0][0:64, 0:TIME], att[:].rearrange("l e i j -> l (e i j)"), ident[0:TIME, 0:TIME]).then_inc(s_attT, 1)
            pe.wait_ge(s_pn, 1)
            pe.transpose(pb[1][0:TIME, 0:64], attT[:], ident[0:64, 0:64]).then_inc(s_pT_ps, 1)
            for i in range(CAP):
                pe.wait_ge(s_av, i + 1)
                for hp in range(EX // 2):
                    t = pe.transpose(pb[2 + i][:, hp * TIME:(hp + 1) * TIME], av[:, i, 2 * hp:2 * hp + 2, :].rearrange("l e d -> l (e d)"), ident[0:TIME, 0:TIME])
                t.then_inc(s_avT_ps, 1)
            for f in range(8):
                i, half, odd = f // 4, f // 2 % 2, f % 2
                if f % 4 == 0:
                    pe.wait_ge(s_avT, i + 1)
                if f >= 4:
                    pe.wait_ge(s_ao, f - 3)
                rows = slice(64 * odd, 64 * odd + 64)
                for s in range(4):
                    hp = 4 * half + s
                    m = pe.matmul(pb[4 + f % 4][0:TIME, s * DM:(s + 1) * DM], avT[rows, i, hp, :], w["woP"][rows, hp, :],
                                  start=True, stop=True, skip_group_check=True)
                m.then_inc(s_ao_ps, 1)
            pe.wait_ge(s_aoT, 16 * KL)
            for k4 in range(4):
                for kk in range(KK if k4 < 2 else KK - 1):
                    for q in range(4):
                        rows = slice(32 * k4, 32 * k4 + 32)
                        m = pe.matmul(pb[k4][32 * q:32 * q + 32, kk * DM:(kk + 1) * DM], oh[rows, 4 * kk + q, :], aoT[rows, kk, q, :],
                                      start=True, stop=True, skip_group_check=True)
                m.then_inc(s_y_ps, 1)

        @block.scalar
        def _(act):
            act.wait_ge(s_sub, 1)
            act.activation(lg[:], lg[:], ACT.Exp).then_inc(s_exp, 1)
            act.wait_ge(s_amax, 1)
            act.activation(attT[:], pb[0][0:64, 0:TIME], ACT.Exp, bias=am[:, 0:1], scale=float(EDH) ** -0.5, accum_out=asum[:, 0:1]).then_inc(s_aexp, 1)
            for r in range(2):
                act.wait_ge(s_var, r + 1)
                act.activation(rstd[:], rstd[:], ACT.Sqrt).then_inc(s_root, 1)

        @block.gpsimd
        def _(pool):
            pool.memset(pr[:, KL:16, :, :], 0.0).then_inc(s_pad, 1)

        @block.vector
        def _(dve):
            c = Chain(dve, s_dve, 0)
            for b in range(4):
                n = 4 if b < 3 else KL - 12
                dve.wait_ge(s_x2T_ps, b + 1)
                dve.tensor_copy(X2T[:, 4 * b:4 * b + n, :], pb[b][:, 0:n * 128].rearrange("p (k t) -> p k t", t=128)).then_inc(s_x2T, 1)
            dve.wait_ge(s_lg, 1)
            L = pb[4][:, 0:KL * EX].rearrange("p (k e) -> p k e", e=EX)
            c.step(dve.tensor_reduce(red[:], L, AX.X, ALU.max))
            c.wait()
            dve.tensor_tensor(lg[:], L, spread(red[:], 2, EX), ALU.subtract).then_inc(s_sub, 1)
            dve.wait_ge(s_exp, 1)
            c.step(dve.tensor_reduce(red[:], lg[:], AX.X, ALU.add))
            c.wait()
            c.step(dve.reciprocal(red[:], red[:]))
            c.wait()
            dve.wait_ge(s_pad, 1)
            for h in range(CAP):
                dve.tensor_tensor(pr[:, 0:KL, h, :], lg[:], spread(red[:], 2, EX), ALU.mult).then_inc(s_pr, 1)
            iota = spread(w["iota"][:], 1, 16)
            dve.wait_ge(s_sc_ps, 1)
            c.step(dve.tensor_copy(sc[:], pb[5][:, :].rearrange("p (l n) -> p l n", n=BATCH)))
            c.wait()
            for rnd, idx in enumerate((i1, i2)):
                c.step(dve.tensor_reduce(m1[:], sc[:], AX.X, ALU.max))
                c.wait()
                c.step(dve.tensor_tensor(t1[:], sc[:], spread(m1[:], 2, BATCH), ALU.is_equal))
                c.wait()
                c.step(dve.tensor_tensor(t1[:], t1[:], iota, ALU.mult))
                c.wait()
                c.step(dve.tensor_reduce(idx[:], t1[:], AX.X, ALU.max))
                c.wait()
                if rnd == 0:
                    c.step(dve.tensor_tensor(t1[:], iota, spread(idx[:], 2, BATCH), ALU.is_equal))
                    c.wait()
                    c.step(dve.scalar_tensor_tensor(sc[:], t1[:], -4.0, sc[:], ALU.mult, ALU.add))
                    c.wait()
            c.step(dve.tensor_tensor(m1[:], i1[:], i2[:], ALU.max))
            c.step(dve.tensor_tensor(i1[:], i1[:], i2[:], ALU.min))
            c.wait()
            c.step(dve.tensor_tensor(m1[:], m1[:], i1[:], ALU.subtract))
            c.wait()
            c.step(dve.tensor_scalar(m1[:], m1[:], w["first"][:, 0:1], None, ALU.mult))
            c.wait()
            c.step(dve.tensor_tensor(i1[:], i1[:], m1[:], ALU.add))
            c.wait()
            dve.tensor_tensor(oh[:], iota, spread(i1[:], 2, BATCH), ALU.is_equal).then_inc(s_oh, 1)
            dve.wait_ge(s_ohn_ps, 1)
            dve.tensor_copy(ohn[:], pb[6][:, :].rearrange("p (k c) -> p k c", c=CE)).then_inc(s_ohn, 1)
            hgv = hg[:].rearrange("p c (k q) -> p q k c", q=4)
            for q in range(4):
                dve.wait_ge(s_hg_ps, q + 1)
                dve.tensor_copy(hgv[:, q], pb[q][:, 0:KL * CE].rearrange("p (k c) -> p k c", c=CE)).then_inc(s_hg, 1)
            for e in range(EX):
                dve.wait_ge(s_qkv_ps, e + 1)
                dve.tensor_tensor(qkv[:, e, :, :], pb[4 + e % 4][0:TIME, 0:CAP * 192].rearrange("l (c x) -> l c x", c=CAP),
                                  spread(w["bqkv"][:, e, :], 1, CAP), ALU.add).then_inc(s_qkv, 1)
            dve.wait_ge(s_qkv, EX)
            for i in range(CAP):
                for j in range(CAP):
                    c.step(dve.tensor_tensor(ta[:], qkv[:, :, i, 0:EDH], qkv[:, :, j, EDH:2 * EDH], ALU.mult))
                    c.wait()
                    dve.tensor_reduce(att[:, :, i, j], ta[:], AX.X, ALU.add).then_inc(s_att, 1)
                    dve.wait_ge(s_att, 2 * i + j + 1)
            dve.wait_ge(s_attT, 1)
            c.step(dve.tensor_reduce(am[:], pb[0][0:64, 0:TIME], AX.X, ALU.max))
            c.wait()
            dve.tensor_scalar(am[:], am[:], -float(EDH) ** -0.5, None, ALU.mult).then_inc(s_amax, 1)
            dve.wait_ge(s_aexp, 1)
            c.step(dve.reciprocal(asum[:], asum[:]))
            c.wait()
            dve.tensor_scalar(attT[:], attT[:], asum[:, 0:1], None, ALU.mult).then_inc(s_pn, 1)
            dve.wait_ge(s_pT_ps, 1)
            dve.tensor_copy(pT[:].rearrange("l e i j -> l (e i j)"), pb[1][0:TIME, 0:64]).then_inc(s_pT, 1)
            dve.wait_ge(s_pT, 1)
            for i in range(CAP):
                c.step(dve.tensor_tensor(ta[:], qkv[:, :, 0, 2 * EDH:], spread(pT[:, :, i, 0], 2, EDH), ALU.mult))
                c.step(dve.tensor_tensor(tb[:], qkv[:, :, 1, 2 * EDH:], spread(pT[:, :, i, 1], 2, EDH), ALU.mult))
                c.wait()
                dve.tensor_tensor(av[:, i, :, :], ta[:], tb[:], ALU.add).then_inc(s_av, 1)
                dve.wait_ge(s_av, i + 1)
            for i in range(CAP):
                dve.wait_ge(s_avT_ps, i + 1)
                dve.tensor_copy(avT[:, i, :, :].rearrange("p a t -> p (a t)"), pb[2 + i][:, 0:EX // 2 * TIME]).then_inc(s_avT, 1)
            for f in range(8):
                i, half, odd = f // 4, f // 2 % 2, f % 2
                c0 = i * EX + 8 * half + odd
                dve.wait_ge(s_ao_ps, f + 1)
                dve.tensor_tensor(ao[:, c0:c0 + 7:2, :], pb[4 + f % 4][0:TIME, :].rearrange("l (s d) -> l s d", s=4),
                                  spread(w["bo"][0:TIME, :], 1, 4), ALU.add).then_inc(s_ao, 1)
            for k4 in range(4):
                n = KK if k4 < 2 else KK - 1
                dve.wait_ge(s_y_ps, k4 + 1)
                c.step(dve.tensor_tensor(y[:, k4::4, :], pb[k4][:, 0:n * DM].rearrange("p (k d) -> p k d", d=DM), X2[:, k4::4, :], ALU.add))
            for r in range(2):
                c.wait()
                for k in range(KL):
                    c.step(dve.bn_stats(stats[:, k, :], y[:, k, :]))
                c.wait()
                for k in range(KL):
                    c.step(dve.bn_aggr(mv[:, k, :], stats[:, k, :]))
                c.wait()
                dve.tensor_scalar(rstd[:], mv[:, :, 1], EPS, None, ALU.add).then_inc(s_var, 1)
                dve.wait_ge(s_root, r + 1)
                c.step(dve.reciprocal(rstd[:], rstd[:]))
                c.wait()
                for k in range(KL):
                    i = dve.tensor_scalar(y[:, k, :], y[:, k, :], mv[:, k, 0:1], rstd[:, k:k + 1], ALU.subtract, ALU.mult)
                    if r == 0:
                        c.step(i)
                    else:
                        i.then_inc(s_outn, 1)
                if r == 0:
                    c.wait()
                    c.step(dve.tensor_tensor(y[:], y[:], spread(w["lng"][:], 1, KL), ALU.mult))
                    c.wait()
                    c.step(dve.tensor_tensor(y[:], y[:], spread(w["lnb"][:], 1, KL), ALU.add))
                    c.wait()
                    c.step(dve.tensor_tensor(y[:], y[:], X2[:], ALU.add))



def program(nc, io):
    with ExitStack() as ctx:
        def sb(name, shape):
            return ctx.enter_context(nc.sbuf_tensor(name, shape, F32))

        psum = ctx.enter_context(nc.psum_tensor("psum", [128, 8 * 512], F32))
        pb = [psum[:, 512 * i:512 * i + 512] for i in range(8)]
        keep = {"ident": sb("ident", [128, 128]), "hmask": sb("hmask", [128, 4]),
                "x1": sb("x1", [ROWS, TILES, DM]), "xT": sb("xT", [128, TOKENS])}
        mixer(nc, io, keep, pb)
        t = {"wg": sb("wg", [128, EX]), "wqkv": sb("wqkv", [128, EX, 3 * EDH]), "bqkv": sb("bqkv", [TIME, EX, 3 * EDH]),
             "woP": sb("woP", [128, EX // 2, DM]), "bo": sb("bo", [128, DM]), "lng": sb("lng", [128, DM]),
             "lnb": sb("lnb", [128, DM]), "iota": sb("iota", [128, BATCH]), "first": sb("first", [128, 1])}
        late = {"t": t, "sem": ctx.enter_context(nc.semaphore("late_loads")),
                "loads": [(t[n][:], io["e_" + n].partition_broadcast(t[n].shape[0]) if n in ("bqkv", "bo", "lng", "lnb", "iota")
                           else io["e_" + n]) for n in t],
                "x2d": nc.dram_tensor("x2_scratch", (TOKENS, DM), F32, kind="Internal").ap(),
                "aod": nc.dram_tensor("ao_scratch", (64, CAP * EX, DM), F32, kind="Internal").ap()}
        cross(nc, io, keep, late, psum, pb)
        experts(nc, io, keep, late, psum, pb)


def layouts(inputs):
    a = {k: np.ascontiguousarray(v) for k, v in inputs.items()}
    out = {"x": a["x"], "ctx": a["ctx_1024"]}
    out["w_inT"] = a["L0_attn_W_in"].T
    out["w_outT"] = a["L0_attn_W_out"].T
    w = a["L0_attn_W_qkva"].reshape(PAIRS, 2, DH, 4, 2, DM)
    b = a["L0_attn_b_qkva"].reshape(PAIRS, 2, DH, 4, 2)
    kinds = [(0, (0, 1)), (0, (1, 0)), (1, (0, 1)), (1, (1, 0))]
    out["w_qk"] = np.stack([w[:, :, :, c][:, :, :, list(r)].transpose(4, 0, 1, 3, 2).reshape(DM, PAIRS, 128) for c, r in kinds], 1)
    out["b_qk"] = np.stack([b[:, :, :, c][:, :, :, list(r)].transpose(1, 3, 2, 0).reshape(128, PAIRS) for c, r in kinds], 1).reshape(128, 16)
    wa = w[:, :, :, 3].reshape(2, 2, 2, DH, 2, DM)
    out["w_gate"] = wa.transpose(5, 4, 0, 2, 1, 3).reshape(DM, 2, 2, 128)
    out["b_gate"] = b[:, :, :, 3].reshape(2, 2, 2, DH, 2).transpose(2, 1, 3, 4, 0).reshape(128, 4)
    out["w_v"] = w[:, :, :, 2].transpose(4, 0, 1, 3, 2).reshape(DM, 512)
    out["b_v"] = b[:, :, :, 2].transpose(0, 1, 3, 2).reshape(512)
    out["b_col"] = np.stack([a["L0_attn_b_in"], a["L0_attn_b_y"]], 1)
    out["b_out"] = a["L0_attn_b_out"]
    wy = a["L0_attn_W_y"].reshape(DM, PAIRS, 2, DH, 2)
    out["w_yT"] = wy.transpose(2, 4, 3, 1, 0).reshape(128, PAIRS, DM)
    out["h0_re"], out["h0_im"] = a["L0_attn_h0_re"], a["L0_attn_h0_im"]
    wq = a["L0_xattn_Wq"].T.reshape(DM, 4, 1, 32)
    out["xq3"] = np.broadcast_to(wq, (DM, 4, 3, 32)).reshape(DM, 4, 96)
    out["xk"], out["xv"], out["xo"] = (a["L0_xattn_" + n].T for n in ("Wk", "Wv", "Wo"))
    out["e_wg"] = a["L0_ffn_Wg"]
    out["e_wqkv"] = np.concatenate([a["L0_ffn_Wq"], a["L0_ffn_Wkv"]], 2).transpose(1, 0, 2)
    out["e_bqkv"] = np.concatenate([a["L0_ffn_bq"], a["L0_ffn_bkv"]], 1)
    out["e_woP"] = a["L0_ffn_Wo"].reshape(EX // 2, 2 * EDH, DM).transpose(1, 0, 2)
    out["e_bo"], out["e_lng"], out["e_lnb"] = a["L0_ffn_bo"], a["L0_ffn_ln_g"], a["L0_ffn_ln_b"]
    out["e_iota"] = np.arange(BATCH, 0, -1).astype(np.float32)
    out["e_first"] = (np.arange(128) // EX % CAP == 0).astype(np.float32)[:, None]
    out["ident"] = np.eye(128, dtype=np.float32)
    mask = np.zeros((2, 4, 32, TP), np.float32)
    for slot in range(SLOTS):
        for i in range(32):
            if slot < 6:
                h = HALVES[slot]
                s = i // h * 2 * h + i % h
                t = [t for t in range(TP) if t // (2 * h) == s // (2 * h) and t // h % 2]
            else:
                s = 32 * (slot - 6) + i
                t = [s]
            if s < TIME:
                mask[slot // 4, slot % 4, i, t] = 1
    out["mask"] = mask.transpose(1, 2, 0, 3).reshape(128, 2, TP)
    head = np.arange(128) // XD
    out["hmask"] = (head[:, None] % 4 == np.arange(4)).astype(np.float32)
    return {k: np.ascontiguousarray(v) for k, v in out.items()}


def kernel(**inputs):
    import concourse.bacc as bacc
    from concourse.bass_utils import run_bass_kernel_spmd

    arrays = layouts(inputs)
    nc = bacc.Bacc("TRN2", target_bir_lowering=False, num_devices=1)
    io = {n: nc.dram_tensor(f"in_{n}", a.shape, mybir.dt.from_np(a.dtype), kind="ExternalInput").ap() for n, a in arrays.items()}
    io["out"] = nc.dram_tensor("out", (BATCH, TIME, DM), F32, kind="ExternalOutput").ap()
    program(nc, io)
    r = run_bass_kernel_spmd(nc, [{f"in_{n}": a for n, a in arrays.items()}], core_ids=[0])
    return r.results[0]["out"]
```

```python
from contextlib import ExitStack

import numpy as np

import concourse.bass as bass
from concourse import mybir

F32 = mybir.dt.float32
F32R = mybir.dt.float32r
ACT = mybir.ActivationFunctionType
ALU = mybir.AluOpType
AX = mybir.AxisListType

BATCH, TIME, DM = 32, 56, 128
HEADS, DH = 8, 32
PAIRS = HEADS // 2
TP = 64
GB = 4
GROUPS = BATCH // GB
PB = PAIRS * GB
GT = GB * TIME
TOKENS = BATCH * TIME
ROWS = 2 * TIME
TILES = BATCH // 2
HALVES = [32, 16, 8, 4, 2, 1]
SLOTS = len(HALVES) + 2
CTX = 1500
KT_N = 12
KP = CTX // KT_N
XH, XD = 16, 8
XSCALE = float(XD) ** -0.5
CH = 500
QC = XH // 4 * TIME
EX, EDH = 16, 64
CAP = BATCH // EX
KL = TIME // 4
EPS = 1e-5


def spread(ap, axis, count):
    ap = ap.unsqueeze(axis)
    shape = list(ap.shape)
    shape[axis] = count
    return ap.broadcast_to(shape)


class Chain:

    def __init__(self, eng, sem, base):
        self.eng, self.sem, self.base, self.n = eng, sem, base, 0

    def step(self, ins):
        ins.then_inc(self.sem, 1)
        self.n += 1

    def wait(self):
        self.eng.wait_ge(self.sem, self.base + self.n)



FILLS = [(0, "VB", 0), (0, "VB", 1), (1, "VB", 2), (1, "VB", 3), (1, "Z", 0), (2, "QB", 0), (2, "QB", 1),
         (3, "QB", 2), (3, "QB", 3), (3, "U", 0), (4, "VA", 0), (4, "VA", 1), (5, "VA", 2), (5, "VA", 3),
         (5, "A", 0), (5, "A", 1), (6, "QA", 0), (6, "QA", 1), (6, "O", 0), (6, "O", 1), (7, "QA", 2), (7, "QA", 3)]
RING = {(kind, k): i % 2 for i, (_, kind, k) in enumerate(FILLS)}
AHEAD = [("U", 0, 0), ("A", 0, 0), ("A", 0, 1), ("QA", 0, 0), ("QA", 0, 1), ("QA", 0, 2), ("QA", 0, 3),
         ("QB", 0, 0), ("QB", 0, 1), ("QB", 0, 2), ("QB", 0, 3), ("VA", 0, 0), ("VA", 0, 1), ("VA", 0, 2), ("VA", 0, 3),
         ("U", 1, 0), ("A", 1, 0), ("A", 1, 1), ("QA", 1, 0), ("QA", 1, 1), ("QA", 1, 2), ("QA", 1, 3)]
TO_DVE = ("O",)


def mixer(nc, io, keep, early, psum, pb):
    x1, xT = keep["x1"], keep["xT"]
    ident = keep["ident"]
    HALF = PAIRS // 2
    HB = HALF * GB
    LAST = GROUPS - 1
    with ExitStack() as ctx:
        def sb(name, shape):
            return ctx.enter_context(nc.sbuf_tensor("m_" + name, shape, F32))

        def sem(name):
            return ctx.enter_context(nc.semaphore("m_" + name))

        win, wout = sb("win", [128, 128]), sb("wout", [128, 128])
        wy = sb("wy", [128, 2, PAIRS, 128])
        wgate = sb("wgate", [128, 2, 2, 128])
        wqk = sb("wqk", [128, 4, PAIRS, 128])
        bgate, bqk = sb("bgate", [128, 4]), sb("bqk", [128, 16])
        bcol = sb("bcol", [128, 2])
        wv, bv = sb("wv", [128, 512]), sb("bv", [128, 512])
        bout = sb("bout", [128, 128])
        h0 = sb("h0", [128, PAIRS, 128])
        mask = sb("mask", [128, 2, TP])
        silu_a, silu_b = sb("silu_a", [128, GT]), sb("silu_b", [128, GT])
        uT = sb("uT", [128, GB, TP])
        uS = sb("uS", [128, GB, SLOTS, 32])
        ag = sb("ag", [128, 2, 8, TP])
        mag, root = sb("mag", [128, 8 * TP]), sb("root", [128, 8 * TP])
        qk = sb("qk", [128, 4, PAIRS, GB, TP])
        tmp = sb("tmp", [128, 2, PB * TP])
        den, inv, third = sb("den", [128, 8 * TP]), sb("inv", [128, 8 * TP]), sb("third", [128, 8 * TP])
        pp = sb("pp", [128, 2, 8, TP])
        sq = pp[:].rearrange("p r c t -> p r (c t)")
        gx = sb("gx", [128, 3, 8, TP])
        bp = sb("bp", [128, 2, 8, 8])
        gd = sb("gd", [128, 3, PAIRS, GB, TP])
        rk = sb("rk", [128, HB * TP])
        suf = sb("suf", [128, HB * TP])
        qv = sb("qv", [128, 2, PB, TP])
        kv = sb("kv", [128, PB, TP])
        ql = sb("ql", [128, 6, 2, PB, 32])
        kl = sb("kl", [128, 6, PB, 32])
        qf = gd[:, 0]
        v1 = sb("v1", [128, GB * 2, 512])
        sm = sb("sm", [128, 2, 2, GB, 2, TP])
        ysb = sb("ysb", [128, PAIRS, GB, 2, TIME])
        z2 = sb("z2", [128, GT])
        stats, mv = sb("stats", [ROWS, TILES, 6]), sb("mv", [ROWS, TILES, 2])
        rstd = sb("rstd", [ROWS, TILES])
        x1T = xT
        sign = keep["hmask"][:, 4:5]

        s_x, s_ident, s_front, s_load = sem("x_loaded"), sem("ident_loaded"), sem("front_loaded"), sem("rest_loaded")
        s_x0 = sem("first_x_loaded")
        s_h0in = sem("h0_loaded")
        s_xt_ps, s_xt = sem("xT_in_psum"), sem("xT_ready")
        s_pfill, s_pevac = sem("fills_for_act"), sem("fills_read_by_act")
        s_vfill, s_vevac = sem("fills_for_dve"), sem("fills_read_by_dve")
        s_silu, s_us = sem("silu_ready"), sem("slot_u_ready")
        s_sq, s_mag, s_root, s_inv, s_rho = sem("squares"), sem("mag2_ready"), sem("root_ready"), sem("inv_ready"), sem("rho_ready")
        s_pp, s_gates = sem("phases_ready"), sem("gates_ready")
        s_exp = [sem("gates_spread0"), sem("gates_spread1")]
        s_rk = sem("rho_for_pool")
        s_turn = sem("q_turned_first")
        s_v = sem("v_ready")
        s_qv, s_kv, s_lev, s_klev = sem("q_turned"), sem("k_turned"), sem("q_levels"), sem("k_levels")
        s_S, s_mask, s_Y, s_yev = sem("scores_filled"), sem("scores_masked"), sem("y_step_done"), sem("y_read")
        s_h0 = sem("h0_added")
        s_dve, s_pool = sem("dve_chain"), sem("pool_chain")
        s_bout = sem("bout_added")
        s_pads, s_h0pad, s_signs, s_h0sign = sem("pads_set"), sem("h0_zeroed"), sem("signs_set"), sem("h0_signed")
        s_stats = sem("stats_ready")
        s_ln, s_root1, s_x1 = sem("ln_chain"), sem("rstd_root"), sem("x1_ready")
        s_x1T_ps, s_x1T = sem("x1T_in_psum"), sem("x1T_ready")

        def isfirst(g):
            return isinstance(g, int) and g == 0

        def isfinal(g):
            return isinstance(g, int) and g == LAST

        def has(kind, g):
            if kind in ("Z", "O"):
                return not isfirst(g)
            ahead = {"VB": 0, "QB": 1, "VA": 1, "U": 2, "A": 2, "QA": 2}[kind]
            return not (isinstance(g, int) and g + ahead > LAST)

        def fills_before(g, dve):
            if dve:
                return 0 if isfirst(g) else 2 * g - 2
            return len(AHEAD) if isfirst(g) else 21 + 20 * g if not isfinal(g) else 21 + 20 * (g - 1) + 13

        def fill_index(g, kind, k):
            dve = kind in TO_DVE
            n = 0
            for _, other, j in FILLS:
                if (other, j) == (kind, k):
                    return fills_before(g, dve) + n
                n += (other in TO_DVE) == dve and has(other, g)

        def ahead_index(kind, g, k):
            dve = kind in TO_DVE
            return sum((other in TO_DVE) == dve for other, _, _ in AHEAD[:AHEAD.index((kind, g, k))])

        def silu_index(g, kind):
            if isinstance(g, int) and g == LAST:
                return 14
            return 1 + 2 * g if kind == "Z" else 2 + 2 * g

        def qk_read(g, half):
            if isinstance(g, int) and (g == 0 or (g == 1 and half == 0)):
                return 2 * ahead_index("QB" if half else "QA", g, 3) + 2
            if half == 0:
                return 2 * (fills_before(g - 1, False) if not isinstance(g, int) else fill_index(g - 2, "QA", 3) + 1)
            return 2 * (fill_index(g - 1, "QB", 3) + 1 if isinstance(g, int) else fills_before(g, False) - 11)


        block = ctx.enter_context(nc.Block())

        @block.sync
        def _(sp):
            x_v = io["x"].rearrange("(j two) t d -> (two t) j d", two=2)
            sp.dma_start(x1[:, 0:4, :], x_v[:, 0:4, :]).then_inc(s_x0, 16)
            sp.dma_start(win[:], io["w_inT"]).then_inc(s_front, 16)
            sp.dma_start(bcol[:], io["b_col"]).then_inc(s_front, 16)
            sp.dma_start(wgate[:], io["w_gate"]).then_inc(s_front, 16)
            sp.dma_start(bgate[:], io["b_gate"]).then_inc(s_front, 16)
            sp.dma_start(wqk[:], io["w_qk"]).then_inc(s_load, 16)
            sp.dma_start(bqk[:], io["b_qk"]).then_inc(s_load, 16)
            sp.dma_start(wv[:], io["w_v"]).then_inc(s_load, 16)
            sp.dma_start(bv[:], io["b_v"].partition_broadcast(128)).then_inc(s_load, 16)
            sp.dma_start(mask[:], io["mask"]).then_inc(s_load, 16)
            sp.wait_ge(s_h0pad, 1)
            for hh in range(2):
                for r, (left, right) in enumerate((("h0_re", "h0_im"), ("h0_im", "h0_re"))):
                    rows = slice(64 * hh + 32 * r, 64 * hh + 32 * r + 32)
                    for c, name in enumerate((left, right)):
                        sp.dma_start(h0[rows, :, 64 * hh + 32 * c:64 * hh + 32 * c + 32],
                                     io[name].rearrange("(p hh) d e -> hh d p e", hh=2)[hh]).then_inc(s_h0in, 16)

            for n in early["w"]:
                sp.dma_start(early["w"][n][:], io["x_w" + n]).then_inc(early["sem"], 16)
            for i in range(2):
                sp.dma_start(early["raw"][i][:], io["ctx"][i].rearrange("(p k) d -> p k d", k=KT_N)).then_inc(early["ctx"][i], 16)

            def spread_gates(j, half):
                for hh in range(2):
                    for odd in range(2):
                        for r in range(2):
                            rows = slice(64 * hh + 32 * r, 64 * hh + 32 * r + 32)
                            sp.dma_start(gd[rows, :, 2 * half + odd, :, :].rearrange("p g b t -> p g (b t)"),
                                         gx[64 * hh + 32 * odd:64 * hh + 32 * odd + 32, :, GB * half:GB * half + GB, :].rearrange(
                                             "p g b t -> p g (b t)")).then_inc(s_exp[half], 16)

            def spread_group(j):
                sp.wait_ge(s_gates, j + 1)
                sp.wait_ge(s_rho, j + 1)
                for half in range(2):
                    sp.wait_ge(s_h0, 2 * j + half - 1) if not (isinstance(j, int) and j == 0) else None
                    spread_gates(j, half)

            spread_group(0)
            with sp.Fori(1, GROUPS) as j:
                spread_group(j)

        @block.tensor
        def _(pe):
            held = {0: None, 1: None}

            def fill(kind, g, k, index, bank):
                if held[bank] is not None:
                    pe.wait_ge(*held[bank])
                out = pb[bank]
                if kind == "U":
                    pe.matmul(out[:, 0:GT], win[:], xT[:, bass.ds(g * GT, GT)], start=True, stop=True).then_inc(s_pfill, 1)
                if kind == "A":
                    for c in range(2):
                        m = pe.matmul(out[:, c * GT:(c + 1) * GT], wgate[:, k, c, :], uT[:, :, 0:TIME], start=(c == 0), stop=(c == 1),
                                      skip_group_check=True)
                    m.then_inc(s_pfill, 1)
                if kind in ("QA", "QB"):
                    for c in range(2):
                        m = pe.matmul(out[:, c * GT:(c + 1) * GT], wqk[:, k, 2 * (kind == "QB") + c, :], uT[:, :, 0:TIME],
                                      start=(c == 0), stop=(c == 1), skip_group_check=True)
                    m.then_inc(s_pfill, 1)
                if kind in ("VA", "VB"):
                    cols = slice(256 * (kind == "VB"), 256 * (kind == "VB") + 256)
                    for tile in range(2):
                        m = pe.matmul(out[:, 256 * tile:256 * tile + 256], uS[:, k, 4 * tile:4 * tile + 4, :], wv[:, cols],
                                      start=(tile == 0), stop=(tile == 1), skip_group_check=True)
                    m.then_inc(s_pfill, 1)
                if kind == "Z":
                    for i in range(2 * PAIRS):
                        m = pe.matmul(out[:, 0:GT], wy[:, i % 2, i // 2, :], ysb[:, i // 2, :, i % 2, :],
                                      start=(i == 0), stop=(i == 2 * PAIRS - 1))
                    m.then_inc(s_pfill, 1)
                if kind == "O":
                    pe.matmul(out[0:ROWS, 0:DM], z2[:, k * ROWS:(k + 1) * ROWS], wout[:], start=True, stop=True).then_inc(s_vfill, 1)
                held[bank] = (s_vevac, index + 1) if kind in TO_DVE else (s_pevac, 2 * index + 2)

            def scores(step):
                pair, tile = step // 2, step % 2
                for b in range(GB):
                    pbi = pair * GB + b
                    for hh in range(2):
                        rows = slice(64 * hh, 64 * hh + 64)
                        bank = pb[2 + hh][:, :].rearrange("p (b v t) -> p b v t", b=GB, v=2)
                        for q in range(4):
                            slot, prt = 4 * tile + q, slice(32 * q, 32 * q + 32)
                            if slot < 6:
                                h = HALVES[slot]
                                out = bank[prt, b, :, :].rearrange("p v (n two h) -> p v n two h", two=2, h=h)[:, :, :, 1, :]
                                lhs = kl[rows, slot, pbi, :] if h > 1 else kv[rows, pbi, 0:TP:2]
                                rhs = ql[rows, slot, :, pbi, :].rearrange("p v (n h) -> p v n h", h=h)
                            else:
                                d = slice(32 * (slot - 6), 32 * (slot - 6) + 32)
                                out, lhs, rhs = bank[prt, b, :, d], kv[rows, pbi, d], qv[rows, :, pbi, d]
                            m = pe.matmul(out, lhs, rhs, start=True, stop=True, skip_group_check=True)
                m.then_inc(s_S, 1)

            def mix(g, step):
                pair, tile = step // 2, step % 2
                pe.wait_ge(s_mask, 8 * g + step + 2)
                for b in range(GB):
                    for hh in range(2):
                        u = 2 * pair + hh
                        m = pe.matmul(pb[4 + pair][64 * hh:64 * hh + 64, b * 2 * TIME:(b + 1) * 2 * TIME].rearrange("p (v t) -> p v t", v=2),
                                      v1[:, 2 * b + tile, 64 * u:64 * u + 64], sm[:, step % 2, hh, b, :, 0:TIME],
                                      start=False, stop=True, skip_group_check=True)
                m.then_inc(s_Y, 1)

            def initial(g, half):
                pe.wait_ge(s_lev, 2 * g + half + 1)
                pe.wait_ge(s_klev, 2 * g + half + 1)
                if not isfirst(g):
                    pe.wait_ge(s_yev, 4 * g - 2 + 2 * half)
                for pair in range(HALF * half, HALF * half + HALF):
                    m = pe.matmul(pb[4 + pair][:, 0:2 * GT].rearrange("p (b v t) -> p b v t", b=GB, v=2)[:, :, 0, :], h0[:, pair, :],
                                  qf[:, pair, :, 0:TIME], start=True, stop=True, skip_group_check=True)
                m.then_inc(s_h0, 1)

            def body(g):
                initial(g, 0)
                scores(0)
                for step in range(8):
                    if step == 0:
                        pe.wait_ge(s_v, 8 * g + 4)
                    if step == 4:
                        pe.wait_ge(s_v, 8 * g + 8)
                    mix(g, step)
                    if step == 3:
                        initial(g, 1)
                    if step + 1 < 8:
                        scores(step + 1)
                    for at, kind, k in FILLS:
                        if at != step or not has(kind, g):
                            continue
                        if kind == "Z":
                            pe.wait_ge(s_yev, 4 * g)
                        if (kind, k) == ("VA", 0):
                            pe.wait_ge(s_us, 8 * g + 16)
                        if (kind, k) == ("A", 0):
                            pe.wait_ge(s_silu, silu_index(g, "U") + 1)
                        if (kind, k) == ("O", 0):
                            pe.wait_ge(s_silu, silu_index(g, "Z") + 1)
                        fill(kind, g + 2 if kind == "U" else g, k, fill_index(g, kind, k), RING[kind, k])

            pe.wait_ge(s_ident, 16)
            pe.wait_ge(s_x0, 16)
            for j in range(TILES):
                if j == 4:
                    pe.wait_ge(s_x, 16)
                t = pe.transpose(pb[4 + j // 4][:, (j % 4) * ROWS:(j % 4 + 1) * ROWS], x1[:, j, :], ident[0:ROWS, 0:ROWS])
                if j % 4 == 3:
                    t.then_inc(s_xt_ps, 1)
                if j == 3:
                    pe.wait_ge(s_front, 64)
                    pe.wait_ge(s_xt, 1)
                    fill("U", 0, 0, 0, 0)
            pe.wait_ge(s_silu, 1)
            pe.wait_ge(s_xt, 4)
            for i, (kind, g, k) in enumerate(AHEAD):
                if i == 0:
                    continue
                if (kind, g, k) == ("QA", 0, 0):
                    pe.wait_ge(s_signs, 4)
                if (kind, k) == ("VA", 0):
                    pe.wait_ge(s_load, 144)
                    pe.wait_ge(s_us, 8)
                if (kind, g, k) == ("A", 1, 0):
                    pe.wait_ge(s_silu, 2)
                fill(kind, g, k, ahead_index(kind, g, k), i % 2)
            pe.wait_ge(s_h0sign, 2)
            body(0)
            with pe.Fori(1, GROUPS - 2) as g:
                for i, k in ((0, 2), (1, 3)):
                    held[i] = (s_pevac, 2 * fills_before(g, False) - 2 + 2 * i)
                body(g)
            for i in range(2):
                held[i] = (s_pevac, 2 * fills_before(GROUPS - 2, False) - 2 + 2 * i)
            body(GROUPS - 2)
            body(LAST)
            pe.wait_ge(s_yev, 4 * GROUPS)
            fill("Z", LAST, 0, fills_before(LAST, False) + 5, 0)
            pe.wait_ge(s_silu, 16)
            for k in range(2):
                fill("O", LAST, k, fills_before(LAST, True) + 2 + k, k)

            for j in range(TILES):
                if j % 4 == 0:
                    pe.wait_ge(s_x1, j + 4)
                t = pe.transpose(pb[4 + j // 4][:, (j % 4) * ROWS:(j % 4 + 1) * ROWS], x1[:, j, :], ident[0:ROWS, 0:ROWS])
                if j % 4 == 3:
                    t.then_inc(s_x1T_ps, 1)

        @block.scalar
        def _(act):
            x_v = io["x"].rearrange("(j two) t d -> (two t) j d", two=2)
            act.dma_start(ident[:], io["ident"]).then_inc(s_ident, 16)
            act.dma_start(x1[:, 4:16, :], x_v[:, 4:16, :]).then_inc(s_x, 16)
            act.dma_start(bout[:], io["b_out"].partition_broadcast(128)).then_inc(s_load, 16)
            act.dma_start(wout[:], io["w_outT"]).then_inc(s_load, 16)
            act.dma_start(wy[:], io["w_yT"]).then_inc(s_load, 16)
            act.dma_start(keep["hmask"][:], io["hmask"]).then_inc(s_load, 16)

            def silu(idx, count, bank, bias):
                act.wait_ge(s_pfill, count + 1)
                if not (isinstance(idx, int) and idx == 0):
                    act.wait_ge(s_silu, idx)
                act.activation(silu_a[:], bank[:, 0:GT], ACT.Sigmoid, bias=bias).then_inc(s_pevac, 1)
                act.activation(silu_b[:], bank[:, 0:GT], ACT.Identity, bias=bias).then_inc(s_pevac, 1)

            def read(kind, g, k, index, bank):
                act.wait_ge(s_pfill, index + 1)
                for c in range(2):
                    src = pb[bank][:, c * GT:(c + 1) * GT].rearrange("p (b t) -> p b t", b=GB)
                    if kind in ("VA", "VB"):
                        half = kind == "VB"
                        i = act.activation(v1[:, 2 * k + c, 256 * half:256 * half + 256], pb[bank][:, 256 * c:256 * c + 256], ACT.Copy)
                    elif kind == "A":
                        i = act.activation(ag[:, k, c * GB:(c + 1) * GB, 0:TIME], src, ACT.Identity,
                                           bias=bgate[:, 2 * k + c:2 * k + c + 1])
                    else:
                        pair = HALF * (kind == "QB") + c
                        i = act.activation(qk[:, k, pair, :, 0:TIME], src, ACT.Identity,
                                           bias=bqk[:, 4 * k + pair:4 * k + pair + 1])
                    i.then_inc(s_pevac, 1)

            def slot_tokens(g, idx):
                act.wait_ge(s_silu, idx + 1)
                for slot in range(SLOTS):
                    if slot < 6:
                        h = HALVES[slot]
                        src = uT[:].rearrange("p b (n two h) -> p b n two h", two=2, h=h)[:, :, :, 0, :]
                        dst = uS[:, :, slot, :].rearrange("p b (n h) -> p b n h", h=h)
                    else:
                        src, dst = uT[:, :, 32 * (slot - 6):32 * (slot - 6) + 32], uS[:, :, slot, :]
                    act.activation(dst, src, ACT.Copy).then_inc(s_us, 1)

            def squares(g, gates_read):
                act.wait_ge(s_pevac, gates_read)
                for r in range(2):
                    act.activation(sq[:, r, :], ag[:, r, :, :].rearrange("p c t -> p (c t)"), ACT.Square).then_inc(s_sq, 1)

            def roots(g):
                act.wait_ge(s_mag, g + 1)
                act.activation(root[:], mag[:], ACT.Sqrt).then_inc(s_root, 1)

            def y_out(g, pair):
                act.wait_ge(s_Y, 8 * g + 2 * pair + 2)
                act.activation(ysb[:, pair, :, :, :].rearrange("p b v t -> p (b v t)"), pb[4 + pair][:, 0:2 * GT], ACT.Copy).then_inc(s_yev, 1)

            def body(g):
                if not isfirst(g):
                    act.wait_ge(s_Y, 8 * g)
                for k in range(4):
                    read("VB", g, k, fill_index(g, "VB", k), RING["VB", k])
                if has("Z", g):
                    silu(silu_index(g, "Z"), fill_index(g, "Z", 0), pb[RING["Z", 0]], bcol[:, 1:2])
                y_out(g, 0)
                if has("QB", g):
                    act.wait_ge(s_pfill, fill_index(g, "VB", 3) + 1)
                    slot_tokens(g + 1, 1 if isfirst(g) else silu_index(g - 1, "U") if isinstance(g, int) else 2 * g)
                    act.wait_ge(s_qv, 2 * g + 2)
                    act.wait_ge(s_kv, 2 * g + 2)
                    for k in range(4):
                        read("QB", g + 1, k, fill_index(g, "QB", k), RING["QB", k])
                if has("U", g):
                    silu(silu_index(g, "U"), fill_index(g, "U", 0), pb[RING["U", 0]], bcol[:, 0:1])
                y_out(g, 1)
                if has("VA", g):
                    for k in range(4):
                        read("VA", g + 1, k, fill_index(g, "VA", k), RING["VA", k])
                y_out(g, 2)
                if has("A", g):
                    act.wait_ge(s_pp, g + 2)
                    for k in range(2):
                        read("A", g + 2, k, fill_index(g, "A", k), RING["A", k])
                    act.wait_ge(s_gates, g + 2)
                    act.wait_ge(s_rho, g + 2)
                    squares(g + 2, 2 * fill_index(g, "A", 1) + 2)
                    roots(g + 2)
                    act.wait_ge(s_qv, 2 * g + 3)
                    act.wait_ge(s_kv, 2 * g + 3)
                    for k in range(4):
                        read("QA", g + 2, k, fill_index(g, "QA", k), RING["QA", k])
                y_out(g, 3)

            for i, (kind, g, k) in enumerate(AHEAD):
                index = ahead_index(kind, g, k)
                if kind == "U":
                    act.wait_ge(s_front, 64)
                    silu(g, index, pb[i % 2], bcol[:, 0:1])
                    if g == 0:
                        act.wait_ge(s_pads, 3)
                        slot_tokens(0, 0)
                else:
                    if (kind, g, k) == ("QA", 0, 0):
                        act.wait_ge(s_signs, 4)
                    if (kind, g, k) == ("A", 1, 0):
                        act.wait_ge(s_pp, 1)
                    if (kind, g, k) == ("QA", 1, 0):
                        act.wait_ge(s_qv, 1)
                        act.wait_ge(s_kv, 1)
                    read(kind, g, k, index, i % 2)
                if (kind, k) == ("A", 1):
                    act.wait_ge(s_gates, g) if g else None
                    act.wait_ge(s_rho, g) if g else None
                    squares(g, 2 * index + 2)
                    roots(g)
            body(0)
            with act.Fori(1, GROUPS - 2) as g:
                body(g)
            body(GROUPS - 2)
            body(LAST)
            silu(15, fills_before(LAST, False) + 5, pb[0], bcol[:, 1:2])
            act.wait_ge(s_ln, TILES + 1)
            act.activation(rstd[:], rstd[:], ACT.Sqrt).then_inc(s_root1, 1)

        @block.gpsimd
        def _(pool):
            pool.memset(uT[:], 0.0).then_inc(s_pads, 1)
            pool.memset(ag[:], 1.0).then_inc(s_pads, 1)
            pool.memset(h0[:], 0.0).then_inc(s_h0pad, 1)
            pool.memset(qk[:], 0.0).then_inc(s_pads, 1)

            def silu(count, out):
                pool.wait_ge(s_pevac, 2 * count + 2)
                pool.tensor_tensor(out, silu_a[:].rearrange("p (b t) -> p b t", b=GB),
                                   silu_b[:].rearrange("p (b t) -> p b t", b=GB), ALU.mult).then_inc(s_silu, 1)

            def half_of(a, half):
                return a[:, HALF * half:HALF * half + HALF].rearrange("p a b t -> p (a b t)")

            def rho(g, base):
                c = Chain(pool, s_pool, base)
                pool.wait_ge(s_inv, g + 1)
                if not isfirst(g):
                    for half in range(2):
                        pool.wait_ge(s_exp[half], 128 * g)
                c.step(pool.tensor_tensor(third[:], third[:], root[:], ALU.mult))
                c.wait()
                pool.tensor_tensor(gx[:, 0].rearrange("p c t -> p (c t)"), mag[:], third[:], ALU.mult).then_inc(s_rho, 1)
                return c.n

            def turn_k(g, half, base):
                c = Chain(pool, s_pool, base)
                n = 128 * g + 128
                pool.wait_ge(s_exp[half], n)
                pool.wait_ge(s_pevac, qk_read(g, half))
                ka, kb = half_of(qk[:, 2], half), half_of(qk[:, 3], half)
                c.step(pool.tensor_tensor(ka, ka, half_of(gd[:, 1], half), ALU.mult))
                c.step(pool.tensor_tensor(kb, kb, half_of(gd[:, 2], half), ALU.mult))
                c.wait()
                if not isfirst(g):
                    pool.wait_ge(s_S, 8 * g - 4 + 4 * half)
                pool.tensor_tensor(kv[:, HB * half:HB * half + HB].rearrange("p c t -> p (c t)"), ka, kb, ALU.add).then_inc(s_kv, 1)
                return c.n

            def levels_k(g, half, base):
                c = Chain(pool, s_pool, base)
                pool.wait_ge(s_rk, 3 * (2 * g + half) + 3)
                pool.wait_ge(s_kv, 2 * g + half + 1)
                kvh = kv[:, HB * half:HB * half + HB]
                for h in HALVES[::-1][1:]:
                    slot = HALVES.index(h)
                    sv = suf[:].rearrange("p (n two h) -> p n two h", two=2, h=h)
                    ks = kvh.rearrange("p c (n two h) -> p (c n) two h", two=2, h=h)[:, :, 0, :]
                    ko = kl[:, slot, HB * half:HB * half + HB].rearrange("p c (n h) -> p (c n) h", h=h)
                    whole = rk[:].rearrange("p (n two j) -> p n two j", two=2, j=h // 2)[:, :, :, h // 2 - 1]
                    if h < 32:
                        c.step(pool.tensor_tensor(whole[:, :, 1], whole[:, :, 0], whole[:, :, 1], ALU.mult))
                    if h == 32:
                        pool.tensor_tensor(ko, ks, sv[:, :, 0, :], ALU.mult).then_inc(s_klev, 1)
                    else:
                        c.step(pool.tensor_tensor(ko, ks, sv[:, :, 0, :], ALU.mult))
                        c.wait()
                        total = rk[:].rearrange("p (n two h) -> p n two h", two=2, h=h)[:, :, 1, h - 1]
                        c.step(pool.tensor_tensor(sv[:, :, 0, :], sv[:, :, 0, :], spread(total, 2, h), ALU.mult))
                        c.wait()
                return c.n

            pool.wait_ge(s_pads, 3)
            def values(g, half):
                kind = "VB" if half else "VA"
                for k in range(4):
                    if isfirst(g) and not half:
                        count = ahead_index("VA", 0, k) + 1
                    elif half:
                        count = fill_index(g, kind, k) + 1
                    elif isinstance(g, int):
                        count = fill_index(g - 1, kind, k) + 1
                    else:
                        count = fills_before(g, False) - 6 - (3 - k)
                    pool.wait_ge(s_pevac, 2 * count)
                    part = v1[:, 2 * k:2 * k + 2, 256 * half:256 * half + 256]
                    pool.tensor_tensor(part, part, spread(bv[:, 256 * half:256 * half + 256], 1, 2), ALU.add).then_inc(s_v, 1)

            silu(0, uT[:, :, 0:TIME])
            pool.wait_ge(s_load, 16 * 9)
            for kind in (0, 3):
                w = wqk[:, kind].rearrange("p a (hh r d) -> p a hh r d", hh=2, r=2)[:, :, :, 1, :]
                pool.tensor_scalar(w, w, -1.0, None, ALU.mult).then_inc(s_signs, 1)
                b = bqk[:, 4 * kind:4 * kind + 4]
                pool.tensor_scalar(b, b, sign, None, ALU.mult).then_inc(s_signs, 1)
            pool.wait_ge(s_h0in, 16 * 8)
            h0im = h0[:].rearrange("p a (hh r e) -> p a hh r e", hh=2, r=2)[:, :, :, 1, :]
            pool.tensor_scalar(h0im, h0im, sign, None, ALU.mult).then_inc(s_h0sign, 1)
            pool.tensor_scalar(wy[:, 1, :, :], wy[:, 1, :, :], sign, None, ALU.mult).then_inc(s_h0sign, 1)
            n = rho(0, 0)
            pool.wait_ge(s_pfill, ahead_index("QB", 0, 3) + 1)
            pool.wait_ge(s_us, 8)
            silu(ahead_index("U", 1, 0), uT[:, :, 0:TIME])
            n += turn_k(0, 0, n)
            n += levels_k(0, 0, n)
            values(0, 0)
            n += rho(1, n)
            pool.wait_ge(s_load, 16 * 9)
            pool.wait_ge(s_xt_ps, 4)
            pool.tensor_tensor(x1[:], x1[:], spread(bout[0:ROWS, :], 1, TILES), ALU.add).then_inc(s_bout, 1)
            START, STEPS = n, 2 * (2 + 12) + 1

            def body(g):
                n = START + STEPS * g - isfinal(g)
                n += turn_k(g, 1, n)
                n += levels_k(g, 1, n)
                values(g, 1)
                if has("Z", g):
                    pool.wait_ge(s_vfill, fills_before(g, True)) if not (isinstance(g, int) and g == 1) else None
                    silu(fill_index(g, "Z", 0), z2[:].rearrange("p (b t) -> p b t", b=GB))
                if has("U", g):
                    pool.wait_ge(s_pfill, fill_index(g, "QB", 3) + 1)
                    pool.wait_ge(s_us, 8 * g + 16)
                    silu(fill_index(g, "U", 0), uT[:, :, 0:TIME])
                if not isfinal(g):
                    n += turn_k(g + 1, 0, n)
                    n += levels_k(g + 1, 0, n)
                    values(g + 1, 0)
                if has("U", g):
                    n += rho(g + 2, n)

            body(0)
            with pool.Fori(1, GROUPS - 2) as g:
                body(g)
            body(GROUPS - 2)
            body(LAST)
            pool.wait_ge(s_vfill, fills_before(LAST, True) + 2)
            silu(fills_before(LAST, False) + 5, z2[:].rearrange("p (b t) -> p b t", b=GB))

        @block.vector
        def _(dve):
            dve.memset(psum[:, 1024:2048], 0.0).then_inc(s_mask, 1)
            def cmul_split(c, t, out0, out1):
                c.step(dve.tensor_tensor(out0, t[0][0], t[1][1], ALU.subtract))
                c.step(dve.tensor_tensor(out1, t[0][1], t[1][0], ALU.add))

            def squares(g):
                dve.wait_ge(s_sq, 2 * g + 2)
                if not isfirst(g):
                    dve.wait_ge(s_rho, g)
                dve.tensor_tensor(mag[:], sq[:, 0, :], sq[:, 1, :], ALU.add).then_inc(s_mag, 1)

            def gates_1(c, g):
                dve.wait_ge(s_root, g + 1)
                c.step(dve.tensor_scalar(den[:], mag[:], 1.0, None, ALU.add))
                c.wait()
                c.step(dve.tensor_tensor(inv[:], root[:], den[:], ALU.mult))
                c.wait()
                c.step(dve.reciprocal(third[:], inv[:]))
                c.wait()
                dve.tensor_tensor(inv[:], third[:], den[:], ALU.mult).then_inc(s_inv, 1)
                dve.wait_ge(s_inv, g + 1)
                t = tmp[:, 1, 0:8 * TP]
                c.step(dve.tensor_tensor(t, inv[:], inv[:], ALU.mult))
                c.wait()
                c.step(dve.tensor_tensor(t, t, mag[:], ALU.mult))
                c.wait()
                c.step(dve.tensor_scalar(t, t, -0.5, 1.5, ALU.mult, ALU.add))
                c.wait()
                c.step(dve.tensor_tensor(inv[:], inv[:], t, ALU.mult))
                c.wait()
                dve.tensor_tensor(pp[:].rearrange("p r c t -> p r (c t)"), ag[:].rearrange("p r c t -> p r (c t)"),
                                  spread(inv[:], 1, 2), ALU.mult).then_inc(s_pp, 1)

            def eighths(t):
                return t.rearrange("p r c (n j) -> p r (c n) j", j=8)

            def gates_2(c, g):
                run, one = eighths(gx[:, 1:3]), eighths(pp[:])
                dve.wait_ge(s_pp, g + 1)
                if not isfirst(g):
                    for half in range(2):
                        dve.wait_ge(s_exp[half], 128 * g)
                c.step(dve.tensor_copy(run[:, :, :, 0], one[:, :, :, 0]))
                c.wait()
                ta, tb = tmp[:, :, 0:64], tmp[:, :, 64:128]
                for j in range(1, 8):
                    c.step(dve.tensor_tensor(ta, run[:, :, :, j - 1], spread(one[:, 0, :, j], 1, 2), ALU.mult))
                    c.step(dve.tensor_tensor(tb, run[:, :, :, j - 1], spread(one[:, 1, :, j], 1, 2), ALU.mult))
                    c.wait()
                    cmul_split(c, ((ta[:, 0], ta[:, 1]), (tb[:, 0], tb[:, 1])), run[:, 0, :, j], run[:, 1, :, j])
                    c.wait()

            def gates_3(c, g):
                run = gx[:, 1:3].rearrange("p r c (n j) -> p r c n j", j=8)
                c.step(dve.memset(bp[:, 0, :, 0], 1.0))
                c.step(dve.memset(bp[:, 1, :, 0], 0.0))
                c.wait()
                ta, tb = tmp[:, :, 0:8], tmp[:, :, 64:72]
                for n in range(1, 8):
                    c.step(dve.tensor_tensor(ta, bp[:, :, :, n - 1], spread(run[:, 0, :, n - 1, 7], 1, 2), ALU.mult))
                    c.step(dve.tensor_tensor(tb, bp[:, :, :, n - 1], spread(run[:, 1, :, n - 1, 7], 1, 2), ALU.mult))
                    c.wait()
                    cmul_split(c, ((ta[:, 0], ta[:, 1]), (tb[:, 0], tb[:, 1])), bp[:, 0, :, n], bp[:, 1, :, n])
                    c.wait()

            def gates_4(c, g):
                run, b = eighths(gx[:, 1:3]), bp[:].rearrange("p r c n -> p r (c n)")
                ta = tmp[:, :, 0:512].rearrange("p r (m j) -> p r m j", j=8)
                tb = tmp[:, :, 512:1024].rearrange("p r (m j) -> p r m j", j=8)
                for r in range(2):
                    c.step(dve.tensor_tensor(ta[:, r], run[:, r], spread(b[:, 0], 2, 8), ALU.mult))
                    c.step(dve.tensor_tensor(tb[:, r], run[:, r], spread(b[:, 1], 2, 8), ALU.mult))
                c.wait()
                c.step(dve.tensor_tensor(run[:, 0], ta[:, 0], tb[:, 1], ALU.subtract))
                c.wait()
                dve.tensor_tensor(run[:, 1], ta[:, 1], tb[:, 0], ALU.add).then_inc(s_gates, 1)

            def turn_q(c, g, half):
                k = 2 * g + half
                dve.wait_ge(s_exp[half], 128 * g + 128)
                if not (isfirst(g) and half == 0):
                    dve.wait_ge(s_klev, k)
                pre = gd[:, 0, HALF * half:HALF * half + HALF].rearrange("p a b t -> p (a b t)")
                two = suf[:].rearrange("p (n two) -> p n two", two=2)
                dve.tensor_copy(rk[:], pre).then_inc(s_rk, 1)
                dve.tensor_copy(two[:, :, 0], pre.rearrange("p (n two) -> p n two", two=2)[:, :, 1]).then_inc(s_rk, 1)
                dve.memset(two[:, :, 1], 1.0).then_inc(s_rk, 1)
                dve.wait_ge(s_pevac, qk_read(g, half))
                dve.wait_ge(s_gates, g + 1)
                q = qk[:, 0:2, HALF * half:HALF * half + HALF].rearrange("p k a b t -> p k (a b t)")
                cr, ci = (gd[:, i, HALF * half:HALF * half + HALF].rearrange("p a b t -> p (a b t)") for i in (1, 2))
                ta, tb = (tmp[:, i].rearrange("p (v x) -> p v x", v=2) for i in range(2))
                out = qv[:, :, HB * half:HB * half + HB].rearrange("p v c t -> p v (c t)")
                c.step(dve.tensor_tensor(ta, q, spread(cr, 1, 2), ALU.mult))
                c.step(dve.tensor_tensor(tb, q, spread(ci, 1, 2), ALU.mult))
                c.wait()
                if not isfirst(g):
                    dve.wait_ge(s_S, 8 * g - 4 + 4 * half)
                dve.tensor_tensor(out[:, 0], ta[:, 0], tb[:, 1], ALU.subtract).then_inc(s_turn, 1)
                dve.tensor_tensor(out[:, 1], ta[:, 1], tb[:, 0], ALU.add).then_inc(s_qv, 1)

            def levels(c, g, half, sizes):
                pre = gd[:, 0, HALF * half:HALF * half + HALF].rearrange("p a b t -> p (a b t)")
                if sizes[0] == 1:
                    dve.wait_ge(s_rk, 3 * (2 * g + half) + 3)
                    dve.wait_ge(s_turn, 2 * g + half + 1)
                    dve.wait_ge(s_qv, 2 * g + half + 1)
                for h in sizes:
                    slot = HALVES.index(h)
                    pv = pre.rearrange("p (n two h) -> p n two h", two=2, h=h)
                    for v in range(2):
                        qs = qv[:, v, HB * half:HB * half + HB].rearrange("p c (n two h) -> p (c n) two h", two=2, h=h)[:, :, 1, :]
                        qo = ql[:, slot, v, HB * half:HB * half + HB].rearrange("p c (n h) -> p (c n) h", h=h)
                        c.step(dve.tensor_tensor(qo, qs, pv[:, :, 1, :], ALU.mult))
                    c.wait()
                    c.step(dve.tensor_tensor(pv[:, :, 1, :], pv[:, :, 1, :], spread(pv[:, :, 0, h - 1], 2, h), ALU.mult))
                    c.wait()
                if sizes[-1] == 32:
                    dve.tensor_tensor(pre, qv[:, 0, HB * half:HB * half + HB].rearrange("p c t -> p (c t)"), pre, ALU.mult).then_inc(s_lev, 1)

            def masked(g, step):
                dve.wait_ge(s_S, 8 * g + step + 1)
                if not (isfirst(g) and step < 2):
                    dve.wait_ge(s_Y, 8 * g + step - 1)
                dve.tensor_tensor(sm[:, step % 2].rearrange("p u b v t -> p (u b v) t"),
                                  psum[:, 1024:2048].rearrange("p (n t) -> p n t", t=TP),
                                  spread(mask[:, step % 2, :], 1, 4 * GB), ALU.mult).then_inc(s_mask, 1)

            def residual(j0, index, banks):
                dve.wait_ge(s_bout, 1)
                for tl in range(2):
                    row = bass.ds(j0 + tl, 1)
                    tokens = x1[:, row, :].rearrange("p a d -> p (a d)")
                    dve.wait_ge(s_vfill, index + tl + 1)
                    dve.tensor_tensor(tokens, pb[banks[tl]][0:ROWS, 0:DM], tokens, ALU.add).then_inc(s_vevac, 1)
                    dve.wait_ge(s_vevac, index + tl + 1)
                    dve.bn_stats(stats[:, row, :].rearrange("p a d -> p (a d)"), tokens).then_inc(s_stats, 1)

            for i in range(4):
                dve.wait_ge(s_xt_ps, i + 1)
                dve.tensor_copy(xT[:, i * 4 * ROWS:(i + 1) * 4 * ROWS], pb[4 + i][:, 0:4 * ROWS]).then_inc(s_xt, 1)
            c = Chain(dve, s_dve, 0)
            squares(0)
            gates_1(c, 0)
            gates_2(c, 0)
            gates_3(c, 0)
            gates_4(c, 0)
            squares(1)
            gates_1(c, 1)
            turn_q(c, 0, 0)
            levels(c, 0, 0, [1, 2, 4, 8, 16, 32])
            gates_2(c, 1)
            START = c.n

            def body(g, base):
                c = Chain(dve, s_dve, base)
                masked(g, 0)
                turn_q(c, g, 1)
                levels(c, g, 1, [1, 2])
                masked(g, 1)
                levels(c, g, 1, [4, 8, 16, 32])
                masked(g, 2)
                if has("QB", g):
                    gates_3(c, g + 1)
                masked(g, 3)
                if has("QB", g):
                    gates_4(c, g + 1)
                masked(g, 4)
                masked(g, 5)
                if has("QB", g):
                    turn_q(c, g + 1, 0)
                    levels(c, g + 1, 0, [1, 2, 4])
                if has("A", g):
                    squares(g + 2)
                masked(g, 6)
                if has("QB", g):
                    levels(c, g + 1, 0, [8, 16, 32])
                if has("A", g):
                    gates_1(c, g + 2)
                masked(g, 7)
                if has("O", g):
                    residual(2 * g - 2, fill_index(g, "O", 0), [RING["O", k] for k in range(2)])
                if has("A", g):
                    gates_2(c, g + 2)
                return c.n

            STEPS = body(0, START)
            with dve.Fori(1, GROUPS - 2) as g:
                body(g, START + STEPS * g)
            n = START + STEPS * (GROUPS - 2)
            n += body(GROUPS - 2, n)
            body(LAST, n)
            residual(2 * LAST, fills_before(LAST, True) + 2, (0, 1))
            dve.wait_ge(s_stats, TILES)
            for j in range(TILES):
                dve.bn_aggr(mv[:, j, :], stats[:, j, :]).then_inc(s_ln, 1)
            dve.wait_ge(s_ln, TILES)
            dve.tensor_scalar(rstd[:], mv[:, :, 1], EPS, None, ALU.add).then_inc(s_ln, 1)
            dve.wait_ge(s_root1, 1)
            dve.reciprocal(rstd[:], rstd[:]).then_inc(s_ln, 1)
            dve.wait_ge(s_ln, TILES + 2)
            for j in range(TILES):
                dve.tensor_scalar(x1[:, j, :], x1[:, j, :], mv[:, j, 0:1], rstd[:, j:j + 1], ALU.subtract, ALU.mult).then_inc(s_x1, 1)
            for c in range(4):
                dve.wait_ge(s_x1T_ps, c + 1)
                dve.tensor_copy(x1T[:, c * 4 * ROWS:(c + 1) * 4 * ROWS], pb[4 + c][:, 0:4 * ROWS]).then_inc(s_x1T, 1)



def cross(nc, io, keep, early, late, psum, pb):
    x1, x1T = keep["x1"], keep["xT"]
    QN = 4
    HQ = XH // QN
    S_FILLS = 9
    with ExitStack() as ctx:
        def sb(name, shape, dt=F32):
            return ctx.enter_context(nc.sbuf_tensor("x_" + name, shape, dt))

        def sem(name):
            return ctx.enter_context(nc.semaphore("x_" + name))

        wq, wk, wvx, wo = (early["w"][n] for n in "qkvo")
        wom = sb("wom", [128, HQ, 128])
        wkh, wkl = sb("wkh", [128, 128], F32R), sb("wkl", [128, 128], F32R)
        qhi, qlo = late["q"]
        qr = sb("qr", [96, QN, TOKENS], F32R)
        qbd = [sb(f"qbd{i}", [96, QN, HQ, TIME], F32R) for i in range(2)]
        raw = early["raw"]
        ctxT = sb("ctxT", [128, CTX])
        chi, clo = sb("chi", [128, CTX], F32R), sb("clo", [128, CTX], F32R)
        khi, klo = sb("khi", [128, CTX], F32R), sb("klo", [128, CTX], F32R)
        k3 = [sb(f"k3_{i}", [96, QN, CTX], F32R) for i in range(2)]
        vx = [sb(f"v{i}", [KP, KT_N, 128]) for i in range(2)]
        probs = [sb(f"probs{i}", [KP, QN * QC]) for i in range(3)]
        o_sb = sb("o", [128, HQ, 2, TIME])
        stats, mv, rstd = sb("stats", [ROWS, TILES, 6]), sb("mv", [ROWS, TILES, 2]), sb("rstd", [ROWS, TILES])

        s_w, s_wom, s_wkh, s_wkl = early["sem"], sem("wo_masked"), sem("wk_hi"), sem("wk_lo")
        s_ctx, s_chi, s_clo, s_q3 = early["ctx"], sem("ctx_hi"), sem("ctx_lo"), sem("q_stacked")
        s_qf, s_qhi, s_qlo, s_qbd = sem("q_filled"), sem("q_hi"), sem("q_split"), sem("q_blocks")
        s_stage, s_read, s_khi = sem("staged"), sem("stage_read"), sem("k_hi")
        s_k3 = [sem("k_stacked0"), sem("k_stacked1")]
        s_qk, s_act, s_pv = sem("scores_made"), sem("probs_made"), sem("pv_done")
        s_oev, s_out, s_res, s_stats = sem("o_read"), sem("out_made"), sem("residual_added"), sem("stats_ready")
        s_ln, s_root, s_norm, s_x2 = sem("ln_chain"), sem("rstd_root"), sem("normed"), sem("x2_stored")

        bank_stage = [pb[5], pb[6]]

        def sfill(n):
            return 15 + S_FILLS * n

        def stacked(n, par):
            return 96 * (n - par) + 192

        block = ctx.enter_context(nc.Block())

        @block.sync
        def _(sp):
            def context(m, par):
                sp.dma_start(raw[par][:], io["ctx"][m].rearrange("(p k) d -> p k d", k=KT_N) if isinstance(m, int) else
                             io["ctx"][bass.ds(m, 1)].rearrange("a (p k) d -> p (a k) d", k=KT_N)).then_inc(s_ctx[par], 16)

            def stack(par):
                for part, half in enumerate((khi, khi, klo)):
                    for q in range(QN):
                        sp.dma_start(k3[par][32 * part:32 * part + 32, q, :].bitcast(F32), half[32 * q:32 * q + 32, :].bitcast(F32)).then_inc(s_k3[par], 16)

            sp.wait_ge(s_qlo, 4)
            for part, half in enumerate((qhi, qlo, qhi)):
                for q in range(QN):
                    sp.dma_start(qr[32 * part:32 * part + 32, q, :].bitcast(F32), half[32 * q:32 * q + 32, :].bitcast(F32)).then_inc(s_q3, 16)
            for m in range(2):
                sp.wait_ge(s_read, 2 + 9 * m + 6)
                stack(m)
                sp.wait_ge(s_stage, 9 * m + 3)
                context(m + 2, m)
            sp.wait_ge(s_q3, 192)
            for (dst, src) in late["loads"]:
                sp.dma_start(dst, src).then_inc(late["sem"], 16)

            def pair(i, last):
                for par in range(2):
                    m = 2 * i + par
                    sp.wait_ge(s_read, 2 + 9 * m + 6)
                    sp.wait_ge(s_qk, 12 * m - 12)
                    stack(par)
                    if not last:
                        sp.wait_ge(s_stage, 9 * m + 3)
                        context(m + 2, par)

            with sp.Fori(1, TILES - 1) as i:
                pair(i, False)
            pair(TILES - 1, True)
            sp.wait_ge(s_norm, TILES)
            sp.dma_start(late["x2d"].rearrange("(j r) d -> r j d", r=ROWS), x1[:]).then_inc(s_x2, 16)
            sp.wait_ge(s_x2, 16)
            sp.wait_ge(late["sem"], 16 * len(late["loads"]))

        @block.tensor
        def _(pe):
            pe.wait_ge(s_w, 64)
            for c in range(4):
                pe.matmul(pb[c][:, 0:4 * ROWS], wq[:], x1T[:, c * 4 * ROWS:(c + 1) * 4 * ROWS],
                          start=True, stop=True).then_inc(s_qf, 1)
            pe.sem_inc(s_pv, 3)

            def transposes(m, par, c, f):
                if c == 0:
                    pe.wait_ge(s_ctx[par], 16 * (m // 2 + 1) if isinstance(m, int) else 8 * (m - par) + 16)
                pe.wait_ge(s_read, f + 1)
                for t in range(4):
                    i = pe.transpose(bank_stage[fpar(f)][:, t * KP:(t + 1) * KP], raw[par][:, 4 * c + t, :], keep["ident"][0:KP, 0:KP])
                i.then_inc(s_stage, 1)

            parity = [0]

            def fpar(f):
                return parity[0] % 2

            def keys(m, c, f):
                pe.wait_ge(s_clo, 3 * m + c + 1)
                pe.wait_ge(s_read, f + 1)
                for i, (w, x) in enumerate(((wkh, chi), (wkl, chi), (wkh, clo))):
                    t = pe.matmul(bank_stage[fpar(f)][:, 0:CH], w[:], x[:, c * CH:(c + 1) * CH], start=(i == 0), stop=(i == 2))
                t.then_inc(s_stage, 1)

            def vals(par, c, f):
                pe.wait_ge(s_read, f + 1)
                for t in range(4):
                    col = (4 * c + t) * KP
                    i = pe.matmul(bank_stage[fpar(f)][0:KP, t * 128:(t + 1) * 128], ctxT[:, col:col + KP], wvx[:],
                                  start=True, stop=True, skip_group_check=True)
                i.then_inc(s_stage, 1)

            def piece(n, par, k, f, has_v, has_tk):
                if k < 3 and has_v:
                    vals(1 - par, k, f)
                elif k >= 3 and has_tk:
                    if k < 6:
                        transposes(n + 2, par, k - 3, f)
                    else:
                        keys(n + 2, k - 6, f)
                parity[0] += 1

            f = 0
            for m in range(2):
                for k in range(3, 9):
                    piece(m - 2, m, k, f, True, True)
                    f += 1
                if m == 0:
                    for k in range(3):
                        piece(-1, 1, k, f, True, True)
                        f += 1

            def out_proj(i):
                pe.wait_ge(s_oev, 2 * i + 2)
                pe.wait_ge(s_res, i)
                for h in range(HQ):
                    m = pe.matmul(pb[7][0:ROWS, 0:DM], o_sb[:, h, :, :].rearrange("p b t -> p (b t)"), wom[:, h, :],
                                  start=(h == 0), stop=(h == HQ - 1))
                m.then_inc(s_out, 1)

            def pv(n, par, k):
                T = 12 * n + k
                pe.wait_ge(s_act, T + 3)
                if k == 0:
                    pe.wait_ge(s_oev, n)
                for q in range(QN):
                    m = pe.matmul(pb[4][32 * q:32 * q + 32, 0:QC], vx[par][:, k, 32 * q:32 * q + 32],
                                  probs[k % 3][:, q * QC:(q + 1) * QC], start=(k == 0), stop=(k == KT_N - 1))
                m.then_inc(s_pv, 1)

            def batch(n, par, first, has_v, has_tk):
                parity[0] = 1 + par
                pe.wait_ge(s_qbd, n + 1)
                pe.wait_ge(s_k3[par], stacked(n, par))
                for k in range(KT_N):
                    T = 12 * n + k
                    pe.wait_ge(s_act, T + 1)
                    for q in range(QN):
                        m = pe.matmul(pb[2 * (k % 2) + q // 2][0:KP, (q % 2) * QC:(q % 2 + 1) * QC],
                                      k3[par][:, q, k * KP:(k + 1) * KP], qbd[par][:, q, :, :].rearrange("p h t -> p (h t)"),
                                      start=(q % 2 == 0), stop=True, skip_group_check=True)
                    m.then_inc(s_qk, 1)
                    if k < 9:
                        piece(n, par, k, sfill(n) + k, has_v, has_tk)
                    if k == 2 and par == 0 and not first:
                        out_proj((n - 1) // 2 if isinstance(n, int) else pair_of[0] - 1)
                    if k == 1:
                        pe.wait_ge(s_read, 2 + (sfill(n) - 6 if not (isinstance(n, int) and n == 0) else 9))
                    if k >= 1:
                        pv(n, par, k - 1)
                    elif not (isinstance(n, int) and n == 0):
                        pv(n - 1, 1 - par, KT_N - 1)

            pair_of = [0]

            def pair(i, first, last):
                pair_of[0] = i
                batch(2 * i, 0, first, True, not last)
                batch(2 * i + 1, 1, first, not last, not last)

            pair(0, True, False)
            with pe.Fori(1, TILES - 1) as i:
                pair(i, False, False)
            pair(TILES - 1, False, True)
            pv(BATCH - 1, 1, KT_N - 1)
            out_proj(TILES - 1)

        @block.scalar
        def _(act):
            act.sem_inc(s_act, 2)
            for c in range(4):
                act.wait_ge(s_qf, c + 1)
                act.activation(qhi[:, c * 4 * ROWS:(c + 1) * 4 * ROWS], pb[c][:, 0:4 * ROWS], ACT.Copy).then_inc(s_qhi, 1)
            act.wait_ge(s_w, 64)
            act.activation(wkh[:], wk[:], ACT.Copy).then_inc(s_wkh, 1)

            def c_hi(c, f):
                act.wait_ge(s_read, 2 + f + 1)
                act.activation(chi[:, c * CH:(c + 1) * CH], ctxT[:, c * CH:(c + 1) * CH], ACT.Copy).then_inc(s_chi, 1)

            def k_hi(c, f, bank):
                act.wait_ge(s_stage, f + 1)
                act.activation(khi[:, c * CH:(c + 1) * CH], bank[:, 0:CH], ACT.Copy).then_inc(s_khi, 1)

            for m in range(2):
                for c in range(3):
                    c_hi(c, 9 * m + c)
                if m == 1:
                    act.wait_ge(s_k3[0], 192)
                for c in range(3):
                    f = 9 * m + 3 + c
                    k_hi(c, f, bank_stage[f % 2])

            def batch(n, par, has_tk):
                for k in range(KT_N):
                    T = 12 * n + k
                    act.wait_ge(s_qk, T + 1)
                    act.wait_ge(s_pv, T + 1)
                    src = psum[0:KP, 1024 * (k % 2):1024 * (k % 2) + 1024].rearrange("p (a c) -> p a c", a=2)[:, :, 0:2 * QC]
                    act.activation(probs[k % 3][:].rearrange("p (a c) -> p a c", a=2), src, ACT.Sigmoid, scale=XSCALE).then_inc(s_act, 1)
                    if has_tk and 3 <= k < 6:
                        c_hi(k - 3, sfill(n) + k)
                    if has_tk and 6 <= k < 9:
                        if k == 6:
                            act.wait_ge(s_k3[1 - par], stacked(n + 1, 1 - par))
                        k_hi(k - 6, sfill(n) + k, bank_stage[(1 + par + k) % 2])

            with act.Fori(0, TILES - 1) as i:
                batch(2 * i, 0, True)
                batch(2 * i + 1, 1, True)
            batch(2 * TILES - 2, 0, False)
            batch(2 * TILES - 1, 1, False)
            act.wait_ge(s_ln, TILES + 1)
            act.activation(rstd[:], rstd[:], ACT.Sqrt).then_inc(s_root, 1)

        @block.gpsimd
        def _(pool):
            def c_lo(m, c):
                pool.wait_ge(s_chi, 3 * m + c + 1)
                cols = slice(c * CH, (c + 1) * CH)
                pool.tensor_tensor(clo[:, cols], ctxT[:, cols], chi[:, cols].bitcast(F32), ALU.subtract).then_inc(s_clo, 1)

            pool.wait_ge(s_wkh, 1)
            pool.tensor_tensor(wkl[:], wk[:], wkh[:].bitcast(F32), ALU.subtract).then_inc(s_wkl, 1)
            for c in range(3):
                c_lo(0, c)
            with pool.Fori(1, BATCH) as m:
                for c in range(3):
                    c_lo(m, c)

        @block.vector
        def _(dve):
            dve.sem_inc(s_read, 2)
            for c in range(4):
                cols = slice(c * 4 * ROWS, (c + 1) * 4 * ROWS)
                dve.wait_ge(s_qhi, c + 1)
                dve.tensor_tensor(qlo[:, cols], pb[c][:, 0:4 * ROWS], qhi[:, cols].bitcast(F32), ALU.subtract).then_inc(s_qlo, 1)
            dve.wait_ge(s_w, 64)
            for h in range(HQ):
                dve.tensor_scalar(wom[:, h, :], wo[:], keep["hmask"][:, h:h + 1], None, ALU.mult).then_inc(s_wom, 1)

            def blocks(n, par):
                src = qr[:, :, bass.ds(n * TIME, TIME)].bitcast(F32)
                dve.tensor_tensor(qbd[par][:], spread(src, 2, HQ),
                                  keep["hmask"][0:96, 0:HQ].unsqueeze(1).unsqueeze(3).broadcast_to([96, QN, HQ, TIME]), ALU.mult).then_inc(s_qbd, 1)

            def t_read(c, f, bank):
                dve.wait_ge(s_stage, f + 1)
                dve.tensor_copy(ctxT[:, c * CH:(c + 1) * CH], bank[:, 0:CH]).then_inc(s_read, 1)

            def k_lo(c, f, bank, khis):
                dve.wait_ge(s_khi, khis)
                dve.tensor_tensor(klo[:, c * CH:(c + 1) * CH], bank[:, 0:CH],
                                  khi[:, c * CH:(c + 1) * CH].bitcast(F32), ALU.subtract).then_inc(s_read, 1)

            def v_read(par, c, f, bank):
                dve.wait_ge(s_stage, f + 1)
                dve.tensor_copy(vx[par][:, 4 * c:4 * c + 4, :], bank[0:KP, :].rearrange("p (t d) -> p t d", t=4)).then_inc(s_read, 1)

            def tk(m, f, p):
                for k in range(6):
                    if k == 3 and not (isinstance(m, int) and m == 0):
                        dve.wait_ge(s_k3[(p + 1) % 2], stacked(m - 1, (p + 1) % 2))
                    bank = bank_stage[(p + k) % 2]
                    if k < 3:
                        t_read(k, f + k, bank)
                    else:
                        k_lo(k - 3, f + k, bank, 3 * m + k - 3 + 1)

            tk(0, 0, 0)
            for c in range(3):
                v_read(0, c, 6 + c, bank_stage[(6 + c) % 2])
            tk(1, 9, 1)
            dve.wait_ge(s_q3, 192)
            blocks(0, 0)

            def o_read(n, par, i):
                if par == 0 and not (isinstance(i, int) and i == 0):
                    dve.wait_ge(s_out, i)
                dve.wait_ge(s_pv, 3 + 12 * n + 12)
                dve.tensor_copy(o_sb[:, :, par, :], pb[4][:, 0:QC].rearrange("p (h t) -> p h t", h=HQ)).then_inc(s_oev, 1)

            def batch(n, par, has_next, has_tk, i):
                if par == 1:
                    o_read(n - 1, 0, i)
                elif not (isinstance(i, int) and i == 0):
                    o_read(n - 1, 1, i)
                if has_next:
                    dve.wait_ge(s_qk, 12 * n)
                    blocks(n + 1, 1 - par)
                    for c in range(3):
                        v_read(1 - par, c, sfill(n) + c, bank_stage[(1 + par + c) % 2])
                if has_tk:
                    tk(n + 2, sfill(n) + 3, par)

            def residual(i):
                row = bass.ds(i, 1)
                dve.wait_ge(s_out, i + 1)
                dve.tensor_tensor(x1[:, row, :].rearrange("p a d -> p (a d)"), pb[7][0:ROWS, 0:DM],
                                  x1[:, row, :].rearrange("p a d -> p (a d)"), ALU.add).then_inc(s_res, 1)
                dve.wait_ge(s_res, i + 1)
                dve.bn_stats(stats[:, row, :].rearrange("p a d -> p (a d)"), x1[:, row, :].rearrange("p a d -> p (a d)")).then_inc(s_stats, 1)

            def pair(i, last):
                batch(2 * i, 0, True, not last, i)
                if not (isinstance(i, int) and i == 0):
                    residual(i - 1)
                batch(2 * i + 1, 1, not last, not last, i)

            pair(0, False)
            with dve.Fori(1, TILES - 1) as i:
                pair(i, False)
            pair(TILES - 1, True)
            o_read(BATCH - 1, 1, TILES - 1)
            residual(TILES - 1)
            dve.wait_ge(s_stats, TILES)
            for j in range(TILES):
                dve.bn_aggr(mv[:, j, :], stats[:, j, :]).then_inc(s_ln, 1)
            dve.wait_ge(s_ln, TILES)
            dve.tensor_scalar(rstd[:], mv[:, :, 1], EPS, None, ALU.add).then_inc(s_ln, 1)
            dve.wait_ge(s_root, 1)
            dve.reciprocal(rstd[:], rstd[:]).then_inc(s_ln, 1)
            dve.wait_ge(s_ln, TILES + 2)
            for j in range(TILES):
                dve.tensor_scalar(x1[:, j, :], x1[:, j, :], mv[:, j, 0:1], rstd[:, j:j + 1], ALU.subtract, ALU.mult).then_inc(s_norm, 1)



def experts(nc, io, keep, late, psum, pb):
    CE = CAP * EX
    KK = 4
    w = late["t"]
    with ExitStack() as ctx:
        def sb(name, shape, dt=F32):
            return ctx.enter_context(nc.sbuf_tensor("e_" + name, shape, dt))

        def sem(name):
            return ctx.enter_context(nc.semaphore("e_" + name))

        ident = keep["ident"]
        X2 = sb("x2", [128, KL, DM])
        X2T = sb("x2T", [128, KL, 128])
        lg = sb("lg", [128, KL, EX])
        red = sb("red", [128, KL])
        pr = sb("pr", [128, 16, CAP, EX])
        sc = sb("sc", [128, 16, BATCH])
        oh = sb("oh", [128, 16, BATCH])
        t1 = sb("t1", [128, 16, BATCH])
        i1, i2, m1 = sb("i1", [128, 16]), sb("i2", [128, 16]), sb("m1", [128, 16])
        ohn = sb("ohn", [128, 16, CE])
        hg = sb("hg", [128, CE, TIME])
        qkv = sb("qkv", [TIME, EX, CAP, 3 * EDH])
        ta, tb = sb("ta", [TIME, EX, EDH]), sb("tb", [TIME, EX, EDH])
        att = sb("att", [TIME, EX, CAP, CAP])
        attT = sb("attT", [64, TIME])
        am, asum = sb("am", [64, 1]), sb("asum", [64, 1])
        pT = sb("pT", [TIME, EX, CAP, CAP])
        av = sb("av", [TIME, CAP, EX, EDH])
        avT = sb("avT", [128, CAP, EX // 2, TIME])
        ao = sb("ao", [TIME, CE, DM])
        aoT = sb("aoT", [128, KK, 4, DM])
        y = sb("y", [128, KL, DM])
        stats, mv, rstd = sb("stats", [128, KL, 6]), sb("mv", [128, KL, 2]), sb("rstd", [128, KL])

        s_x2, s_x2T_ps, s_x2T = sem("x2_loaded"), sem("x2T_in_psum"), sem("x2T_ready")
        s_lg, s_sub, s_exp, s_pr, s_sc_ps, s_oh, s_ohn_ps, s_ohn = (sem(n) for n in (
            "logits", "logits_less_max", "exps", "probs", "probs_turned", "one_hot", "one_hot_turned", "one_hot_read"))
        s_hg_ps, s_hg, s_qkv_ps, s_qkv, s_att = (sem(n) for n in ("gathered", "gathered_read", "qkv_filled", "qkv_read", "att_ready"))
        s_attT, s_amax, s_aexp, s_asum, s_pn, s_pT_ps, s_pT = (sem(n) for n in (
            "att_turned", "att_max", "att_exp", "att_sum", "att_normed", "p_turned", "p_ready"))
        s_av, s_avT_ps, s_avT, s_ao_ps, s_ao, s_aod, s_aoT = (sem(n) for n in (
            "av_ready", "av_turned", "avT_ready", "ao_filled", "ao_read", "ao_stored", "ao_loaded"))
        s_y_ps, s_var, s_root, s_res, s_outn, s_fin = (sem(n) for n in ("scattered", "variance", "root", "residual", "out_normed", "out_stored"))
        s_dve = sem("dve_chain")
        s_pad = sem("pad_set")

        block = ctx.enter_context(nc.Block())

        @block.sync
        def _(sp):
            src = late["x2d"].rearrange("(n k q) d -> q n k d", k=KL, q=4)
            for q in range(4):
                sp.dma_start(X2[32 * q:32 * q + 32, :, :], src[q]).then_inc(s_x2, 16)
            sp.wait_ge(s_ao, 8)
            sp.dma_start(late["aod"][0:TIME].rearrange("l c d -> l (c d)"), ao[:].rearrange("l c d -> l (c d)")).then_inc(s_aod, 16)
            sp.wait_ge(s_aod, 16)
            src = late["aod"].rearrange("(kk k4 q) c d -> k4 c kk q d", kk=KK, k4=4)
            for k4 in range(4):
                n = KK if k4 < 2 else KK - 1
                for kk in range(n):
                    sp.dma_start(aoT[32 * k4:32 * k4 + 32, kk, :, :], src[k4][:, kk, :, :]).then_inc(s_aoT, 16)
            dst = io["out"].rearrange("n (k q) d -> q n k d", q=4)
            sp.wait_ge(s_outn, KL)
            for q in range(4):
                sp.dma_start(dst[q], y[32 * q:32 * q + 32, :, :]).then_inc(s_fin, 16)
            sp.wait_ge(s_fin, 64)

        @block.tensor
        def _(pe):
            pe.wait_ge(s_x2, 64)
            for k in range(KL):
                t = pe.transpose(pb[k // 4][:, (k % 4) * 128:(k % 4 + 1) * 128], X2[:, k, :], ident[:])
                if k % 4 == 3 or k == KL - 1:
                    t.then_inc(s_x2T_ps, 1)
            for k in range(KL):
                if k % 4 == 0:
                    pe.wait_ge(s_x2T, k // 4 + 1)
                m = pe.matmul(pb[4][:, k * EX:(k + 1) * EX], X2T[:, k, :], w["wg"], start=True, stop=True, skip_group_check=True)
            m.then_inc(s_lg, 1)
            pe.wait_ge(s_pr, 2)
            for kk in range(KK):
                t = pe.transpose(pb[5][:, kk * 128:(kk + 1) * 128], pr[:, 4 * kk:4 * kk + 4, :, :].rearrange("p k c e -> p (k c e)"), ident[:])
            t.then_inc(s_sc_ps, 1)
            pe.wait_ge(s_oh, 1)
            for kk in range(KK):
                t = pe.transpose(pb[6][:, kk * 128:(kk + 1) * 128], oh[:, 4 * kk:4 * kk + 4, :].rearrange("p q n -> p (q n)"), ident[:])
            t.then_inc(s_ohn_ps, 1)
            pe.wait_ge(s_ohn, 1)
            for k in range(KL):
                for q in range(4):
                    rows = slice(32 * q, 32 * q + 32)
                    m = pe.matmul(pb[q][:, k * CE:(k + 1) * CE], X2[rows, k, :], ohn[rows, k, :], start=True, stop=True, skip_group_check=True)
                    if k == KL - 1:
                        m.then_inc(s_hg_ps, 1)
            pe.wait_ge(s_hg, 4)
            for e in range(EX):
                if e >= 4:
                    pe.wait_ge(s_qkv, e - 3)
                for c in range(CAP):
                    m = pe.matmul(pb[4 + e % 4][0:TIME, c * 192:(c + 1) * 192], hg[:, c * EX + e, :], w["wqkv"][:, e, :],
                                  start=(c == 0), stop=True, skip_group_check=True)
                m.then_inc(s_qkv_ps, 1)
            pe.wait_ge(s_att, 4)
            pe.transpose(pb[0][0:64, 0:TIME], att[:].rearrange("l e i j -> l (e i j)"), ident[0:TIME, 0:TIME]).then_inc(s_attT, 1)
            pe.wait_ge(s_pn, 1)
            pe.transpose(pb[1][0:TIME, 0:64], attT[:], ident[0:64, 0:64]).then_inc(s_pT_ps, 1)
            for i in range(CAP):
                pe.wait_ge(s_av, i + 1)
                for hp in range(EX // 2):
                    t = pe.transpose(pb[2 + i][:, hp * TIME:(hp + 1) * TIME], av[:, i, 2 * hp:2 * hp + 2, :].rearrange("l e d -> l (e d)"), ident[0:TIME, 0:TIME])
                t.then_inc(s_avT_ps, 1)
            for f in range(8):
                i, half, odd = f // 4, f // 2 % 2, f % 2
                if f % 4 == 0:
                    pe.wait_ge(s_avT, i + 1)
                if f >= 4:
                    pe.wait_ge(s_ao, f - 3)
                rows = slice(64 * odd, 64 * odd + 64)
                for s in range(4):
                    hp = 4 * half + s
                    m = pe.matmul(pb[4 + f % 4][0:TIME, s * DM:(s + 1) * DM], avT[rows, i, hp, :], w["woP"][rows, hp, :],
                                  start=True, stop=True, skip_group_check=True)
                m.then_inc(s_ao_ps, 1)
            pe.wait_ge(s_aoT, 16 * KL)
            for k4 in range(4):
                for kk in range(KK if k4 < 2 else KK - 1):
                    for q in range(4):
                        rows = slice(32 * k4, 32 * k4 + 32)
                        m = pe.matmul(pb[k4][32 * q:32 * q + 32, kk * DM:(kk + 1) * DM], oh[rows, 4 * kk + q, :], aoT[rows, kk, q, :],
                                      start=True, stop=True, skip_group_check=True)
                m.then_inc(s_y_ps, 1)

        @block.scalar
        def _(act):
            act.wait_ge(s_sub, 1)
            act.activation(lg[:], lg[:], ACT.Exp).then_inc(s_exp, 1)
            act.wait_ge(s_amax, 1)
            act.activation(attT[:], pb[0][0:64, 0:TIME], ACT.Exp, bias=am[:, 0:1], scale=float(EDH) ** -0.5, accum_out=asum[:, 0:1]).then_inc(s_aexp, 1)
            for r in range(2):
                act.wait_ge(s_var, r + 1)
                act.activation(rstd[:], rstd[:], ACT.Sqrt).then_inc(s_root, 1)

        @block.gpsimd
        def _(pool):
            pool.memset(pr[:, KL:16, :, :], 0.0).then_inc(s_pad, 1)

        @block.vector
        def _(dve):
            c = Chain(dve, s_dve, 0)
            for b in range(4):
                n = 4 if b < 3 else KL - 12
                dve.wait_ge(s_x2T_ps, b + 1)
                dve.tensor_copy(X2T[:, 4 * b:4 * b + n, :], pb[b][:, 0:n * 128].rearrange("p (k t) -> p k t", t=128)).then_inc(s_x2T, 1)
            dve.wait_ge(s_lg, 1)
            L = pb[4][:, 0:KL * EX].rearrange("p (k e) -> p k e", e=EX)
            c.step(dve.tensor_reduce(red[:], L, AX.X, ALU.max))
            c.wait()
            dve.tensor_tensor(lg[:], L, spread(red[:], 2, EX), ALU.subtract).then_inc(s_sub, 1)
            dve.wait_ge(s_exp, 1)
            c.step(dve.tensor_reduce(red[:], lg[:], AX.X, ALU.add))
            c.wait()
            c.step(dve.reciprocal(red[:], red[:]))
            c.wait()
            dve.wait_ge(s_pad, 1)
            for h in range(CAP):
                dve.tensor_tensor(pr[:, 0:KL, h, :], lg[:], spread(red[:], 2, EX), ALU.mult).then_inc(s_pr, 1)
            iota = spread(w["iota"], 1, 16)
            dve.wait_ge(s_sc_ps, 1)
            c.step(dve.tensor_copy(sc[:], pb[5][:, :].rearrange("p (l n) -> p l n", n=BATCH)))
            c.wait()
            for rnd, idx in enumerate((i1, i2)):
                c.step(dve.tensor_reduce(m1[:], sc[:], AX.X, ALU.max))
                c.wait()
                c.step(dve.tensor_tensor(t1[:], sc[:], spread(m1[:], 2, BATCH), ALU.is_equal))
                c.wait()
                c.step(dve.tensor_tensor(t1[:], t1[:], iota, ALU.mult))
                c.wait()
                c.step(dve.tensor_reduce(idx[:], t1[:], AX.X, ALU.max))
                c.wait()
                if rnd == 0:
                    c.step(dve.tensor_tensor(t1[:], iota, spread(idx[:], 2, BATCH), ALU.is_equal))
                    c.wait()
                    c.step(dve.scalar_tensor_tensor(sc[:], t1[:], -4.0, sc[:], ALU.mult, ALU.add))
                    c.wait()
            c.step(dve.tensor_tensor(m1[:], i1[:], i2[:], ALU.max))
            c.step(dve.tensor_tensor(i1[:], i1[:], i2[:], ALU.min))
            c.wait()
            c.step(dve.tensor_tensor(m1[:], m1[:], i1[:], ALU.subtract))
            c.wait()
            c.step(dve.tensor_scalar(m1[:], m1[:], w["first"][:, 0:1], None, ALU.mult))
            c.wait()
            c.step(dve.tensor_tensor(i1[:], i1[:], m1[:], ALU.add))
            c.wait()
            dve.tensor_tensor(oh[:], iota, spread(i1[:], 2, BATCH), ALU.is_equal).then_inc(s_oh, 1)
            dve.wait_ge(s_ohn_ps, 1)
            dve.tensor_copy(ohn[:], pb[6][:, :].rearrange("p (k c) -> p k c", c=CE)).then_inc(s_ohn, 1)
            hgv = hg[:].rearrange("p c (k q) -> p q k c", q=4)
            for q in range(4):
                dve.wait_ge(s_hg_ps, q + 1)
                dve.tensor_copy(hgv[:, q], pb[q][:, 0:KL * CE].rearrange("p (k c) -> p k c", c=CE)).then_inc(s_hg, 1)
            for e in range(EX):
                dve.wait_ge(s_qkv_ps, e + 1)
                dve.tensor_tensor(qkv[:, e, :, :], pb[4 + e % 4][0:TIME, 0:CAP * 192].rearrange("l (c x) -> l c x", c=CAP),
                                  spread(w["bqkv"][:, e, :], 1, CAP), ALU.add).then_inc(s_qkv, 1)
            dve.wait_ge(s_qkv, EX)
            for i in range(CAP):
                for j in range(CAP):
                    c.step(dve.tensor_tensor(ta[:], qkv[:, :, i, 0:EDH], qkv[:, :, j, EDH:2 * EDH], ALU.mult))
                    c.wait()
                    dve.tensor_reduce(att[:, :, i, j], ta[:], AX.X, ALU.add).then_inc(s_att, 1)
                    dve.wait_ge(s_att, 2 * i + j + 1)
            dve.wait_ge(s_attT, 1)
            c.step(dve.tensor_reduce(am[:], pb[0][0:64, 0:TIME], AX.X, ALU.max))
            c.wait()
            dve.tensor_scalar(am[:], am[:], -float(EDH) ** -0.5, None, ALU.mult).then_inc(s_amax, 1)
            dve.wait_ge(s_aexp, 1)
            c.step(dve.reciprocal(asum[:], asum[:]))
            c.wait()
            dve.tensor_scalar(attT[:], attT[:], asum[:, 0:1], None, ALU.mult).then_inc(s_pn, 1)
            dve.wait_ge(s_pT_ps, 1)
            dve.tensor_copy(pT[:].rearrange("l e i j -> l (e i j)"), pb[1][0:TIME, 0:64]).then_inc(s_pT, 1)
            dve.wait_ge(s_pT, 1)
            for i in range(CAP):
                c.step(dve.tensor_tensor(ta[:], qkv[:, :, 0, 2 * EDH:], spread(pT[:, :, i, 0], 2, EDH), ALU.mult))
                c.step(dve.tensor_tensor(tb[:], qkv[:, :, 1, 2 * EDH:], spread(pT[:, :, i, 1], 2, EDH), ALU.mult))
                c.wait()
                dve.tensor_tensor(av[:, i, :, :], ta[:], tb[:], ALU.add).then_inc(s_av, 1)
                dve.wait_ge(s_av, i + 1)
            for i in range(CAP):
                dve.wait_ge(s_avT_ps, i + 1)
                dve.tensor_copy(avT[:, i, :, :].rearrange("p a t -> p (a t)"), pb[2 + i][:, 0:EX // 2 * TIME]).then_inc(s_avT, 1)
            for f in range(8):
                i, half, odd = f // 4, f // 2 % 2, f % 2
                c0 = i * EX + 8 * half + odd
                dve.wait_ge(s_ao_ps, f + 1)
                dve.tensor_tensor(ao[:, c0:c0 + 7:2, :], pb[4 + f % 4][0:TIME, :].rearrange("l (s d) -> l s d", s=4),
                                  spread(w["bo"][0:TIME, :], 1, 4), ALU.add).then_inc(s_ao, 1)
            for k4 in range(4):
                n = KK if k4 < 2 else KK - 1
                dve.wait_ge(s_y_ps, k4 + 1)
                c.step(dve.tensor_tensor(y[:, k4::4, :], pb[k4][:, 0:n * DM].rearrange("p (k d) -> p k d", d=DM), X2[:, k4::4, :], ALU.add))
            for r in range(2):
                c.wait()
                for k in range(KL):
                    c.step(dve.bn_stats(stats[:, k, :], y[:, k, :]))
                c.wait()
                for k in range(KL):
                    c.step(dve.bn_aggr(mv[:, k, :], stats[:, k, :]))
                c.wait()
                dve.tensor_scalar(rstd[:], mv[:, :, 1], EPS, None, ALU.add).then_inc(s_var, 1)
                dve.wait_ge(s_root, r + 1)
                c.step(dve.reciprocal(rstd[:], rstd[:]))
                c.wait()
                for k in range(KL):
                    i = dve.tensor_scalar(y[:, k, :], y[:, k, :], mv[:, k, 0:1], rstd[:, k:k + 1], ALU.subtract, ALU.mult)
                    if r == 0:
                        c.step(i)
                    else:
                        i.then_inc(s_outn, 1)
                if r == 0:
                    c.wait()
                    c.step(dve.tensor_tensor(y[:], y[:], spread(w["lng"], 1, KL), ALU.mult))
                    c.wait()
                    c.step(dve.tensor_tensor(y[:], y[:], spread(w["lnb"], 1, KL), ALU.add))
                    c.wait()
                    c.step(dve.tensor_tensor(y[:], y[:], X2[:], ALU.add))



def program(nc, io):
    with ExitStack() as ctx:
        def sb(name, shape):
            return ctx.enter_context(nc.sbuf_tensor(name, shape, F32))

        psum = ctx.enter_context(nc.psum_tensor("psum", [128, 8 * 512], F32))
        pb = [psum[:, 512 * i:512 * i + 512] for i in range(8)]
        keep = {"ident": sb("ident", [128, 128]), "hmask": sb("hmask", [128, 5]),
                "x1": sb("x1", [ROWS, TILES, DM]), "xT": sb("xT", [128, TOKENS])}
        x = {n: sb("x_w" + n, [128, 128]) for n in ("q", "k", "v", "o")}
        raw = [sb(f"x_ctx{i}", [KP, KT_N, DM]) for i in range(2)]
        early = {"w": x, "raw": raw, "sem": ctx.enter_context(nc.semaphore("x_weights_loaded")),
                 "ctx": [ctx.enter_context(nc.semaphore(f"x_ctx_loaded{i}")) for i in range(2)]}
        mixer(nc, io, keep, early, psum, pb)
        space = sb("late", [128, 2 * 3 * EX * EDH + EX // 2 * DM])
        wide = 3 * EX * EDH
        t = {"wqkv": space[:, 0:wide].rearrange("p (e x) -> p e x", e=EX),
             "bqkv": space[0:TIME, wide:2 * wide].rearrange("p (e x) -> p e x", e=EX),
             "woP": space[:, 2 * wide:].rearrange("p (e x) -> p e x", e=EX // 2)}
        for n, shape in (("wg", [128, EX]), ("bo", [128, DM]), ("lng", [128, DM]), ("lnb", [128, DM]), ("iota", [128, BATCH]), ("first", [128, 1])):
            t[n] = sb(n, shape)[:]
        late = {"t": t, "sem": ctx.enter_context(nc.semaphore("late_loads")),
                "q": [space[:, TOKENS * i:TOKENS * (i + 1)].bitcast(F32R) for i in range(2)],
                "loads": [(t[n], io["e_" + n].partition_broadcast(t[n].shape[0]) if n in ("bqkv", "bo", "lng", "lnb", "iota")
                           else io["e_" + n]) for n in t],
                "x2d": nc.dram_tensor("x2_scratch", (TOKENS, DM), F32, kind="Internal").ap(),
                "aod": nc.dram_tensor("ao_scratch", (64, CAP * EX, DM), F32, kind="Internal").ap()}
        cross(nc, io, keep, early, late, psum, pb)
        experts(nc, io, keep, late, psum, pb)


def layouts(inputs):
    a = {k: np.ascontiguousarray(v) for k, v in inputs.items()}
    out = {"x": a["x"], "ctx": a["ctx_1024"]}
    out["w_inT"] = a["L0_attn_W_in"].T
    out["w_outT"] = a["L0_attn_W_out"].T
    w = a["L0_attn_W_qkva"].reshape(PAIRS, 2, DH, 4, 2, DM)
    b = a["L0_attn_b_qkva"].reshape(PAIRS, 2, DH, 4, 2)
    kinds = [(0, (0, 1)), (0, (1, 0)), (1, (0, 1)), (1, (1, 0))]
    out["w_qk"] = np.stack([w[:, :, :, c][:, :, :, list(r)].transpose(4, 0, 1, 3, 2).reshape(DM, PAIRS, 128) for c, r in kinds], 1)
    out["b_qk"] = np.stack([b[:, :, :, c][:, :, :, list(r)].transpose(1, 3, 2, 0).reshape(128, PAIRS) for c, r in kinds], 1).reshape(128, 16)
    wa = w[:, :, :, 3].reshape(2, 2, 2, DH, 2, DM)
    out["w_gate"] = wa.transpose(5, 4, 0, 2, 1, 3).reshape(DM, 2, 2, 128)
    out["b_gate"] = b[:, :, :, 3].reshape(2, 2, 2, DH, 2).transpose(2, 1, 3, 4, 0).reshape(128, 4)
    out["w_v"] = w[:, :, :, 2].transpose(4, 0, 1, 3, 2).reshape(DM, 512)
    out["b_v"] = b[:, :, :, 2].transpose(0, 1, 3, 2).reshape(512)
    out["b_col"] = np.stack([a["L0_attn_b_in"], a["L0_attn_b_y"]], 1)
    out["b_out"] = a["L0_attn_b_out"]
    wy = a["L0_attn_W_y"].reshape(DM, PAIRS, 2, DH, 2)
    out["w_yT"] = np.stack([wy[..., r].transpose(2, 4, 3, 1, 0).reshape(128, PAIRS, DM) for r in ([0, 1], [1, 0])], 1)
    out["h0_re"], out["h0_im"] = a["L0_attn_h0_re"], a["L0_attn_h0_im"]
    for n in "qkvo":
        out["x_w" + n] = a["L0_xattn_W" + n].T
    out["e_wg"] = a["L0_ffn_Wg"]
    out["e_wqkv"] = np.concatenate([a["L0_ffn_Wq"], a["L0_ffn_Wkv"]], 2).transpose(1, 0, 2)
    out["e_bqkv"] = np.concatenate([a["L0_ffn_bq"], a["L0_ffn_bkv"]], 1)
    out["e_woP"] = a["L0_ffn_Wo"].reshape(EX // 2, 2 * EDH, DM).transpose(1, 0, 2)
    out["e_bo"], out["e_lng"], out["e_lnb"] = a["L0_ffn_bo"], a["L0_ffn_ln_g"], a["L0_ffn_ln_b"]
    out["e_iota"] = np.arange(BATCH, 0, -1).astype(np.float32)
    out["e_first"] = (np.arange(128) // EX % CAP == 0).astype(np.float32)[:, None]
    out["ident"] = np.eye(128, dtype=np.float32)
    mask = np.zeros((2, 4, 32, TP), np.float32)
    for slot in range(SLOTS):
        for i in range(32):
            if slot < 6:
                h = HALVES[slot]
                s = i // h * 2 * h + i % h
                t = [t for t in range(TP) if t // (2 * h) == s // (2 * h) and t // h % 2]
            else:
                s = 32 * (slot - 6) + i
                t = [s]
            if s < TIME:
                mask[slot // 4, slot % 4, i, t] = 1
    out["mask"] = mask.transpose(1, 2, 0, 3).reshape(128, 2, TP)
    head = np.arange(128) // XD
    rows = np.arange(128)[:, None]
    out["hmask"] = np.concatenate([head[:, None] % 4 == np.arange(4), 1 - 2 * (rows // DH % 2)], 1).astype(np.float32)
    return {k: np.ascontiguousarray(v) for k, v in out.items()}


def kernel(**inputs):
    import concourse.bacc as bacc
    from concourse.bass_utils import run_bass_kernel_spmd

    arrays = layouts(inputs)
    nc = bacc.Bacc("TRN2", target_bir_lowering=False, num_devices=1)
    io = {n: nc.dram_tensor(f"in_{n}", a.shape, mybir.dt.from_np(a.dtype), kind="ExternalInput").ap() for n, a in arrays.items()}
    io["out"] = nc.dram_tensor("out", (BATCH, TIME, DM), F32, kind="ExternalOutput").ap()
    program(nc, io)
    r = run_bass_kernel_spmd(nc, [{f"in_{n}": a for n, a in arrays.items()}], core_ids=[0])
    return r.results[0]["out"]
```

```python
from contextlib import ExitStack

import numpy as np

import concourse.bass as bass
from concourse import mybir

F32 = mybir.dt.float32
F32R = mybir.dt.float32r
ACT = mybir.ActivationFunctionType
ALU = mybir.AluOpType
AX = mybir.AxisListType

BATCH, TIME, DM = 32, 56, 128
HEADS, DH = 8, 32
PAIRS = HEADS // 2
TP = 64
GB = 4
GROUPS = BATCH // GB
PB = PAIRS * GB
GT = GB * TIME
TOKENS = BATCH * TIME
ROWS = 2 * TIME
TILES = BATCH // 2
HALVES = [32, 16, 8, 4, 2, 1]
SLOTS = len(HALVES) + 2
CTX = 1500
KT_N = 12
KP = CTX // KT_N
XH, XD = 16, 8
XSCALE = float(XD) ** -0.5
CH = 500
QC = XH // 4 * TIME
EX, EDH = 16, 64
CAP = BATCH // EX
KL = TIME // 4
EPS = 1e-5


def spread(ap, axis, count):
    ap = ap.unsqueeze(axis)
    shape = list(ap.shape)
    shape[axis] = count
    return ap.broadcast_to(shape)


class Chain:

    def __init__(self, eng, sem, base):
        self.eng, self.sem, self.base, self.n = eng, sem, base, 0

    def step(self, ins):
        ins.then_inc(self.sem, 1)
        self.n += 1

    def wait(self, upto=None):
        self.eng.wait_ge(self.sem, self.base + (self.n if upto is None else upto))


def in_turns(c, chains, rounds=None):
    chains = list(chains)
    while chains and rounds != 0:
        for link in list(chains):
            if link[1] is not None:
                c.wait(link[1])
            if next(link[0], "end") == "end":
                chains.remove(link)
            link[1] = c.n
        rounds = None if rounds is None else rounds - 1
    if not chains:
        c.wait()



FILLS = [(0, "VB", 0), (0, "VB", 1), (0, "VB", 2), (0, "VB", 3), (0, "Z", 0), (1, "QB", 0), (2, "QB", 1), (2, "QB", 2),
         (2, "QB", 3), (2, "U", 0), (3, "A", 0), (3, "A", 1), (3, "VA", 0), (4, "VA", 1), (5, "VA", 2), (6, "VA", 3),
         (7, "QA", 0), (7, "QA", 1), (7, "O", 0), (7, "O", 1), (7, "QA", 2), (7, "QA", 3)]
RING = {(kind, k): i % 2 for i, (_, kind, k) in enumerate(FILLS)}
AHEAD = [("U", 0, 0), ("A", 0, 0), ("A", 0, 1), ("QA", 0, 0), ("QA", 0, 1), ("QA", 0, 2), ("QA", 0, 3),
         ("QB", 0, 0), ("QB", 0, 1), ("QB", 0, 2), ("QB", 0, 3), ("VA", 0, 0), ("VA", 0, 1), ("VA", 0, 2), ("VA", 0, 3),
         ("U", 1, 0), ("A", 1, 0), ("A", 1, 1), ("QA", 1, 0), ("QA", 1, 1), ("QA", 1, 2), ("QA", 1, 3)]
TO_DVE = ("O",)


def mixer(nc, io, keep, early, psum, pb):
    x1, xT = keep["x1"], keep["xT"]
    ident = keep["ident"]
    HALF = PAIRS // 2
    HB = HALF * GB
    LAST = GROUPS - 1
    with ExitStack() as ctx:
        def sb(name, shape):
            return ctx.enter_context(nc.sbuf_tensor("m_" + name, shape, F32))

        def sem(name):
            return ctx.enter_context(nc.semaphore("m_" + name))

        win, wout = sb("win", [128, 128]), sb("wout", [128, 128])
        wy = sb("wy", [128, 2, PAIRS, 128])
        wgate = sb("wgate", [128, 2, 2, 128])
        wqk = sb("wqk", [128, 4, PAIRS, 128])
        bgate, bqk = sb("bgate", [128, 4]), sb("bqk", [128, 16])
        bcol = sb("bcol", [128, 2])
        wv, bv = sb("wv", [128, 512]), sb("bv", [128, 512])
        bout = sb("bout", [128, 128])
        h0 = sb("h0", [128, PAIRS, 128])
        mask = sb("mask", [128, 2, TP])
        silu_a, silu_b = sb("silu_a", [128, GT]), sb("silu_b", [128, GT])
        uT = sb("uT", [128, GB, TP])
        uS = sb("uS", [128, GB, SLOTS, 32])
        ag = sb("ag", [128, 2, 8, TP])
        mag, root = sb("mag", [128, 8 * TP]), sb("root", [128, 8 * TP])
        qk = sb("qk", [128, 4, PAIRS, GB, TP])
        tmp = sb("tmp", [128, 2, PB * TP])
        den, inv, third = sb("den", [128, 8 * TP]), sb("inv", [128, 8 * TP]), sb("third", [128, 8 * TP])
        pp = sb("pp", [128, 2, 8, TP])
        sq = pp[:].rearrange("p r c t -> p r (c t)")
        gx = sb("gx", [128, 3, 8, TP])
        bp = sb("bp", [128, 2, 8, 8])
        small = sb("small", [128, 256])
        gd = sb("gd", [128, 3, PAIRS, GB, TP])
        rk = sb("rk", [128, HB * TP])
        suf = sb("suf", [128, HB * TP])
        qv = sb("qv", [128, 2, PB, TP])
        kv = sb("kv", [128, PB, TP])
        ql = sb("ql", [128, 6, 2, PB, 32])
        kl = sb("kl", [128, 6, PB, 32])
        qf = gd[:, 0]
        v1 = sb("v1", [128, GB * 2, 512])
        sm = sb("sm", [128, 2, 2, GB, 2, TP])
        ysb = sb("ysb", [128, PAIRS, GB, 2, TIME])
        z2 = sb("z2", [128, GT])
        stats = keep["stats"]
        sign = keep["hmask"][:, 4:5]

        s_x, s_ident, s_front, s_load = sem("x_loaded"), sem("ident_loaded"), sem("front_loaded"), sem("rest_loaded")
        s_x0 = sem("first_x_loaded")
        s_h0in = sem("h0_loaded")
        s_xt_ps, s_xt = sem("xT_in_psum"), sem("xT_ready")
        s_pfill, s_pevac = sem("fills_for_act"), sem("fills_read_by_act")
        s_vfill, s_vevac = sem("fills_for_dve"), sem("fills_read_by_dve")
        s_silu, s_us = sem("silu_ready"), sem("slot_u_ready")
        s_sq, s_mag, s_root, s_inv, s_rho = sem("squares"), sem("mag2_ready"), sem("root_ready"), sem("inv_ready"), sem("rho_ready")
        s_pp, s_gates = sem("phases_ready"), sem("gates_ready")
        s_exp = [sem("gates_spread0"), sem("gates_spread1")]
        s_rk = sem("rho_for_pool")
        s_turn = sem("q_turned_first")
        s_v = sem("v_ready")
        s_qv, s_kv, s_lev, s_klev = sem("q_turned"), sem("k_turned"), sem("q_levels"), sem("k_levels")
        s_S, s_mask, s_Y, s_yev = sem("scores_filled"), sem("scores_masked"), sem("y_step_done"), sem("y_read")
        s_h0 = sem("h0_added")
        s_dve, s_pool = sem("dve_chain"), sem("pool_chain")
        s_bout = sem("bout_added")
        s_pads, s_h0pad, s_signs, s_h0sign = sem("pads_set"), sem("h0_zeroed"), sem("signs_set"), sem("h0_signed")
        s_stats = sem("stats_ready")

        def isfirst(g):
            return isinstance(g, int) and g == 0

        def isfinal(g):
            return isinstance(g, int) and g == LAST

        def has(kind, g):
            if kind in ("Z", "O"):
                return not isfirst(g)
            ahead = {"VB": 0, "QB": 1, "VA": 1, "U": 2, "A": 2, "QA": 2}[kind]
            return not (isinstance(g, int) and g + ahead > LAST)

        def fills_before(g, dve):
            if dve:
                return 0 if isfirst(g) else 2 * g - 2
            return len(AHEAD) if isfirst(g) else 21 + 20 * g if not isfinal(g) else 21 + 20 * (g - 1) + 13

        def fill_index(g, kind, k):
            dve = kind in TO_DVE
            n = 0
            for _, other, j in FILLS:
                if (other, j) == (kind, k):
                    return fills_before(g, dve) + n
                n += (other in TO_DVE) == dve and has(other, g)

        def ahead_index(kind, g, k):
            dve = kind in TO_DVE
            return sum((other in TO_DVE) == dve for other, _, _ in AHEAD[:AHEAD.index((kind, g, k))])

        def silu_index(g, kind):
            if isinstance(g, int) and g == LAST:
                return 14
            return 1 + 2 * g if kind == "Z" else 2 + 2 * g

        def qk_read(g, half):
            if isinstance(g, int) and (g == 0 or (g == 1 and half == 0)):
                return 2 * ahead_index("QB" if half else "QA", g, 3) + 2
            if half == 0:
                return 2 * (fills_before(g - 1, False) if not isinstance(g, int) else fill_index(g - 2, "QA", 3) + 1)
            return 2 * (fill_index(g - 1, "QB", 3) + 1 if isinstance(g, int) else fills_before(g, False) - 11)
        block = ctx.enter_context(nc.Block())

        @block.sync
        def _(sp):
            x_v = io["x"].rearrange("(j two) t d -> (two t) j d", two=2)
            sp.dma_start(x1[:, 0:4, :], x_v[:, 0:4, :]).then_inc(s_x0, 16)
            sp.dma_start(win[:], io["w_inT"]).then_inc(s_front, 16)
            sp.dma_start(bcol[:], io["b_col"]).then_inc(s_front, 16)
            sp.dma_start(wgate[:], io["w_gate"]).then_inc(s_front, 16)
            sp.dma_start(bgate[:], io["b_gate"]).then_inc(s_front, 16)
            sp.dma_start(wqk[:], io["w_qk"]).then_inc(s_load, 16)
            sp.dma_start(bqk[:], io["b_qk"]).then_inc(s_load, 16)
            sp.dma_start(wv[:], io["w_v"]).then_inc(s_load, 16)
            sp.dma_start(bv[:], io["b_v"].partition_broadcast(128)).then_inc(s_load, 16)
            sp.dma_start(mask[:], io["mask"]).then_inc(s_load, 16)
            sp.wait_ge(s_h0pad, 1)
            for hh in range(2):
                for r, (left, right) in enumerate((("h0_re", "h0_im"), ("h0_im", "h0_re"))):
                    rows = slice(64 * hh + 32 * r, 64 * hh + 32 * r + 32)
                    for c, name in enumerate((left, right)):
                        sp.dma_start(h0[rows, :, 64 * hh + 32 * c:64 * hh + 32 * c + 32],
                                     io[name].rearrange("(p hh) d e -> hh d p e", hh=2)[hh]).then_inc(s_h0in, 16)

            for n in early["w"]:
                sp.dma_start(early["w"][n][:], io["x_w" + n]).then_inc(early["sem"], 16)
            for i in range(2):
                sp.dma_start(early["raw"][i][:], io["ctx"][i].rearrange("(p k) d -> p k d", k=KT_N)).then_inc(early["ctx"][i], 16)

            def spread_gates(j, half):
                for hh in range(2):
                    for odd in range(2):
                        for r in range(2):
                            rows = slice(64 * hh + 32 * r, 64 * hh + 32 * r + 32)
                            sp.dma_start(gd[rows, :, 2 * half + odd, :, :].rearrange("p g b t -> p g (b t)"),
                                         gx[64 * hh + 32 * odd:64 * hh + 32 * odd + 32, :, GB * half:GB * half + GB, :].rearrange(
                                             "p g b t -> p g (b t)")).then_inc(s_exp[half], 16)

            def spread_group(j):
                sp.wait_ge(s_gates, j + 1)
                sp.wait_ge(s_rho, j + 1)
                for half in range(2):
                    if not isfirst(j):
                        sp.wait_ge(s_h0, 2 * j + half - 1)
                    spread_gates(j, half)

            spread_group(0)
            with sp.Fori(1, GROUPS) as j:
                spread_group(j)

        @block.tensor
        def _(pe):
            held = {0: None, 1: None}

            def fill(kind, g, k, index, bank):
                if held[bank] is not None:
                    pe.wait_ge(*held[bank])
                out = pb[bank]
                if kind == "U":
                    pe.matmul(out[:, 0:GT], win[:], xT[:, bass.ds(g * GT, GT)], start=True, stop=True).then_inc(s_pfill, 1)
                if kind == "A":
                    for c in range(2):
                        m = pe.matmul(out[:, c * GT:(c + 1) * GT], wgate[:, k, c, :], uT[:, :, 0:TIME], start=(c == 0), stop=(c == 1),
                                      skip_group_check=True)
                    m.then_inc(s_pfill, 1)
                if kind in ("QA", "QB"):
                    for c in range(2):
                        m = pe.matmul(out[:, c * GT:(c + 1) * GT], wqk[:, k, 2 * (kind == "QB") + c, :], uT[:, :, 0:TIME],
                                      start=(c == 0), stop=(c == 1), skip_group_check=True)
                    m.then_inc(s_pfill, 1)
                if kind in ("VA", "VB"):
                    cols = slice(256 * (kind == "VB"), 256 * (kind == "VB") + 256)
                    for tile in range(2):
                        m = pe.matmul(out[:, 256 * tile:256 * tile + 256], uS[:, k, 4 * tile:4 * tile + 4, :], wv[:, cols],
                                      start=(tile == 0), stop=(tile == 1), skip_group_check=True)
                    m.then_inc(s_pfill, 1)
                if kind == "Z":
                    for i in range(2 * PAIRS):
                        m = pe.matmul(out[:, 0:GT], wy[:, i % 2, i // 2, :], ysb[:, i // 2, :, i % 2, :],
                                      start=(i == 0), stop=(i == 2 * PAIRS - 1))
                    m.then_inc(s_pfill, 1)
                if kind == "O":
                    pe.matmul(out[0:ROWS, 0:DM], z2[:, k * ROWS:(k + 1) * ROWS], wout[:], start=True, stop=True).then_inc(s_vfill, 1)
                held[bank] = (s_vevac, index + 1) if kind in TO_DVE else (s_pevac, 2 * index + 2)

            def scores(step):
                pair, tile = step // 2, step % 2
                for b in range(GB):
                    pbi = pair * GB + b
                    for hh in range(2):
                        rows = slice(64 * hh, 64 * hh + 64)
                        bank = pb[2 + hh][:, :].rearrange("p (b v t) -> p b v t", b=GB, v=2)
                        for q in range(4):
                            slot, prt = 4 * tile + q, slice(32 * q, 32 * q + 32)
                            if slot < 6:
                                h = HALVES[slot]
                                out = bank[prt, b, :, :].rearrange("p v (n two h) -> p v n two h", two=2, h=h)[:, :, :, 1, :]
                                lhs = kl[rows, slot, pbi, :] if h > 1 else kv[rows, pbi, 0:TP:2]
                                rhs = ql[rows, slot, :, pbi, :].rearrange("p v (n h) -> p v n h", h=h)
                            else:
                                d = slice(32 * (slot - 6), 32 * (slot - 6) + 32)
                                out, lhs, rhs = bank[prt, b, :, d], kv[rows, pbi, d], qv[rows, :, pbi, d]
                            m = pe.matmul(out, lhs, rhs, start=True, stop=True, skip_group_check=True)
                m.then_inc(s_S, 1)

            def mix(g, step, head, part):
                pair, tile = step // 2, step % 2
                if head:
                    pe.wait_ge(s_mask, 8 * g + step + 2)
                for b in range(GB):
                    for hh in range(2):
                        if (b == 0 and hh == 0) != head and not (part == "all"):
                            continue
                        u = 2 * pair + hh
                        m = pe.matmul(pb[4 + pair][64 * hh:64 * hh + 64, b * 2 * TIME:(b + 1) * 2 * TIME].rearrange("p (v t) -> p v t", v=2),
                                      v1[:, 2 * b + tile, 64 * u:64 * u + 64], sm[:, step % 2, hh, b, :, 0:TIME],
                                      start=False, stop=True, skip_group_check=True)
                if not head or part == "all":
                    m.then_inc(s_Y, 1)

            def initial(g, half):
                pe.wait_ge(s_lev, 2 * g + half + 1)
                pe.wait_ge(s_klev, 2 * g + half + 1)
                if not isfirst(g):
                    pe.wait_ge(s_yev, 4 * g - 2 + 2 * half)
                for pair in range(HALF * half, HALF * half + HALF):
                    m = pe.matmul(pb[4 + pair][:, 0:2 * GT].rearrange("p (b v t) -> p b v t", b=GB, v=2)[:, :, 0, :], h0[:, pair, :],
                                  qf[:, pair, :, 0:TIME], start=True, stop=True, skip_group_check=True)
                m.then_inc(s_h0, 1)

            def body(g):
                initial(g, 0)
                scores(0)
                for step in range(8):
                    if step == 0:
                        pe.wait_ge(s_v, 8 * g + 4)
                    if step == 4:
                        pe.wait_ge(s_v, 8 * g + 8)
                    if step in (3, 7):
                        mix(g, step, True, "all")
                    else:
                        mix(g, step, True, "head")
                        scores(step + 1)
                        mix(g, step, False, "rest")
                    if step == 3:
                        initial(g, 1)
                        scores(4)
                    for at, kind, k in FILLS:
                        if at != step or not has(kind, g):
                            continue
                        if kind == "Z":
                            pe.wait_ge(s_yev, 4 * g)
                        if (kind, k) == ("VA", 0):
                            pe.wait_ge(s_us, 8 * g + 16)
                        if (kind, k) == ("A", 0):
                            pe.wait_ge(s_silu, silu_index(g, "U") + 1)
                        if (kind, k) == ("O", 0):
                            pe.wait_ge(s_silu, silu_index(g, "Z") + 1)
                        fill(kind, g + 2 if kind == "U" else g, k, fill_index(g, kind, k), RING[kind, k])

            pe.wait_ge(s_ident, 16)
            pe.wait_ge(s_x0, 16)
            for j in range(TILES):
                if j == 4:
                    pe.wait_ge(s_x, 16)
                t = pe.transpose(pb[4 + j // 4][:, (j % 4) * ROWS:(j % 4 + 1) * ROWS], x1[:, j, :], ident[0:ROWS, 0:ROWS])
                if j % 4 == 3:
                    t.then_inc(s_xt_ps, 1)
                if j == 3:
                    pe.wait_ge(s_front, 64)
                    pe.wait_ge(s_xt, 1)
                    fill("U", 0, 0, 0, 0)
            pe.wait_ge(s_silu, 1)
            pe.wait_ge(s_xt, 4)
            for i, (kind, g, k) in enumerate(AHEAD):
                if i == 0:
                    continue
                if (kind, g, k) == ("QA", 0, 0):
                    pe.wait_ge(s_signs, 4)
                if (kind, k) == ("VA", 0):
                    pe.wait_ge(s_load, 144)
                    pe.wait_ge(s_us, 8)
                if (kind, g, k) == ("A", 1, 0):
                    pe.wait_ge(s_silu, 2)
                fill(kind, g, k, ahead_index(kind, g, k), i % 2)
            pe.wait_ge(s_h0sign, 2)
            body(0)
            with pe.Fori(1, GROUPS - 2) as g:
                for i, k in ((0, 2), (1, 3)):
                    held[i] = (s_pevac, 2 * fills_before(g, False) - 2 + 2 * i)
                body(g)
            for i in range(2):
                held[i] = (s_pevac, 2 * fills_before(GROUPS - 2, False) - 2 + 2 * i)
            body(GROUPS - 2)
            body(LAST)
            pe.wait_ge(s_yev, 4 * GROUPS)
            fill("Z", LAST, 0, fills_before(LAST, False) + 5, 0)
            pe.wait_ge(s_silu, 16)
            for k in range(2):
                fill("O", LAST, k, fills_before(LAST, True) + 2 + k, k)

        @block.scalar
        def _(act):
            x_v = io["x"].rearrange("(j two) t d -> (two t) j d", two=2)
            act.dma_start(ident[:], io["ident"]).then_inc(s_ident, 16)
            act.dma_start(x1[:, 4:16, :], x_v[:, 4:16, :]).then_inc(s_x, 16)
            act.dma_start(bout[:], io["b_out"].partition_broadcast(128)).then_inc(s_load, 16)
            act.dma_start(wout[:], io["w_outT"]).then_inc(s_load, 16)
            act.dma_start(wy[:], io["w_yT"]).then_inc(s_load, 16)
            act.dma_start(keep["hmask"][:], io["hmask"]).then_inc(s_load, 16)

            def silu(idx, count, bank, bias):
                act.wait_ge(s_pfill, count + 1)
                if not (isinstance(idx, int) and idx == 0):
                    act.wait_ge(s_silu, idx)
                act.activation(silu_a[:], bank[:, 0:GT], ACT.Sigmoid, bias=bias).then_inc(s_pevac, 1)
                act.activation(silu_b[:], bank[:, 0:GT], ACT.Identity, bias=bias).then_inc(s_pevac, 1)

            def read(kind, g, k, index, bank):
                act.wait_ge(s_pfill, index + 1)
                for c in range(2):
                    src = pb[bank][:, c * GT:(c + 1) * GT].rearrange("p (b t) -> p b t", b=GB)
                    if kind in ("VA", "VB"):
                        half = kind == "VB"
                        i = act.activation(v1[:, 2 * k + c, 256 * half:256 * half + 256], pb[bank][:, 256 * c:256 * c + 256], ACT.Copy)
                    elif kind == "A":
                        i = act.activation(ag[:, k, c * GB:(c + 1) * GB, 0:TIME], src, ACT.Identity,
                                           bias=bgate[:, 2 * k + c:2 * k + c + 1])
                    else:
                        pair = HALF * (kind == "QB") + c
                        i = act.activation(qk[:, k, pair, :, 0:TIME], src, ACT.Identity,
                                           bias=bqk[:, 4 * k + pair:4 * k + pair + 1])
                    i.then_inc(s_pevac, 1)

            def slot_tokens(g, idx):
                act.wait_ge(s_silu, idx + 1)
                for slot in range(SLOTS):
                    if slot < 6:
                        h = HALVES[slot]
                        src = uT[:].rearrange("p b (n two h) -> p b n two h", two=2, h=h)[:, :, :, 0, :]
                        dst = uS[:, :, slot, :].rearrange("p b (n h) -> p b n h", h=h)
                    else:
                        src, dst = uT[:, :, 32 * (slot - 6):32 * (slot - 6) + 32], uS[:, :, slot, :]
                    act.activation(dst, src, ACT.Copy).then_inc(s_us, 1)

            def squares(g, gates_read):
                act.wait_ge(s_pevac, gates_read)
                for r in range(2):
                    act.activation(sq[:, r, :], ag[:, r, :, :].rearrange("p c t -> p (c t)"), ACT.Square).then_inc(s_sq, 1)

            def roots(g):
                act.wait_ge(s_mag, g + 1)
                act.activation(root[:], mag[:], ACT.Sqrt).then_inc(s_root, 1)

            def y_out(g, pair):
                act.wait_ge(s_Y, 8 * g + 2 * pair + 2)
                act.activation(ysb[:, pair, :, :, :].rearrange("p b v t -> p (b v t)"), pb[4 + pair][:, 0:2 * GT], ACT.Copy).then_inc(s_yev, 1)

            def body(g):
                if not isfirst(g):
                    act.wait_ge(s_Y, 8 * g)
                for k in range(4):
                    read("VB", g, k, fill_index(g, "VB", k), RING["VB", k])
                if has("Z", g):
                    silu(silu_index(g, "Z"), fill_index(g, "Z", 0), pb[RING["Z", 0]], bcol[:, 1:2])
                y_out(g, 0)
                if has("QB", g):
                    act.wait_ge(s_pfill, fill_index(g, "VB", 3) + 1)
                    slot_tokens(g + 1, 1 if isfirst(g) else silu_index(g - 1, "U") if isinstance(g, int) else 2 * g)
                    act.wait_ge(s_qv, 2 * g + 2)
                    act.wait_ge(s_kv, 2 * g + 2)
                    for k in range(4):
                        read("QB", g + 1, k, fill_index(g, "QB", k), RING["QB", k])
                if has("U", g):
                    silu(silu_index(g, "U"), fill_index(g, "U", 0), pb[RING["U", 0]], bcol[:, 0:1])
                y_out(g, 1)
                if has("A", g):
                    act.wait_ge(s_pp, g + 2)
                    for k in range(2):
                        read("A", g + 2, k, fill_index(g, "A", k), RING["A", k])
                    act.wait_ge(s_gates, g + 2)
                    act.wait_ge(s_rho, g + 2)
                    squares(g + 2, 2 * fill_index(g, "A", 1) + 2)
                    roots(g + 2)
                if has("VA", g):
                    for k in range(4):
                        read("VA", g + 1, k, fill_index(g, "VA", k), RING["VA", k])
                y_out(g, 2)
                if has("A", g):
                    act.wait_ge(s_qv, 2 * g + 3)
                    act.wait_ge(s_kv, 2 * g + 3)
                    for k in range(4):
                        read("QA", g + 2, k, fill_index(g, "QA", k), RING["QA", k])
                y_out(g, 3)

            for i, (kind, g, k) in enumerate(AHEAD):
                index = ahead_index(kind, g, k)
                if kind == "U":
                    act.wait_ge(s_front, 64)
                    silu(g, index, pb[i % 2], bcol[:, 0:1])
                    if g == 0:
                        act.wait_ge(s_pads, 3)
                        slot_tokens(0, 0)
                else:
                    if (kind, g, k) == ("QA", 0, 0):
                        act.wait_ge(s_signs, 4)
                    if (kind, g, k) == ("A", 1, 0):
                        act.wait_ge(s_pp, 1)
                    if (kind, g, k) == ("QA", 1, 0):
                        act.wait_ge(s_qv, 1)
                        act.wait_ge(s_kv, 1)
                    read(kind, g, k, index, i % 2)
                if (kind, k) == ("A", 1):
                    if g > 0:
                        act.wait_ge(s_gates, g)
                        act.wait_ge(s_rho, g)
                    squares(g, 2 * index + 2)
                    roots(g)
            body(0)
            with act.Fori(1, GROUPS - 2) as g:
                body(g)
            body(GROUPS - 2)
            body(LAST)
            silu(15, fills_before(LAST, False) + 5, pb[0], bcol[:, 1:2])

        @block.gpsimd
        def _(pool):
            pool.memset(uT[:], 0.0).then_inc(s_pads, 1)
            pool.memset(ag[:], 1.0).then_inc(s_pads, 1)
            pool.memset(h0[:], 0.0).then_inc(s_h0pad, 1)
            pool.memset(qk[:], 0.0).then_inc(s_pads, 1)

            def silu(count, out):
                pool.wait_ge(s_pevac, 2 * count + 2)
                pool.tensor_tensor(out, silu_a[:].rearrange("p (b t) -> p b t", b=GB),
                                   silu_b[:].rearrange("p (b t) -> p b t", b=GB), ALU.mult).then_inc(s_silu, 1)

            def half_of(a, half):
                return a[:, HALF * half:HALF * half + HALF].rearrange("p a b t -> p (a b t)")

            def rho(g, base):
                c = Chain(pool, s_pool, base)
                pool.wait_ge(s_inv, g + 1)
                if not isfirst(g):
                    for half in range(2):
                        pool.wait_ge(s_exp[half], 128 * g)
                c.step(pool.tensor_tensor(third[:], third[:], root[:], ALU.mult))
                c.wait()
                pool.tensor_tensor(gx[:, 0].rearrange("p c t -> p (c t)"), mag[:], third[:], ALU.mult).then_inc(s_rho, 1)
                return c.n

            def turn_k(g, half, base):
                c = Chain(pool, s_pool, base)
                n = 128 * g + 128
                pool.wait_ge(s_exp[half], n)
                pool.wait_ge(s_pevac, qk_read(g, half))
                ka, kb = half_of(qk[:, 2], half), half_of(qk[:, 3], half)
                c.step(pool.tensor_tensor(ka, ka, half_of(gd[:, 1], half), ALU.mult))
                c.step(pool.tensor_tensor(kb, kb, half_of(gd[:, 2], half), ALU.mult))
                c.wait()
                if not isfirst(g):
                    pool.wait_ge(s_S, 8 * g - 4 + 4 * half)
                pool.tensor_tensor(kv[:, HB * half:HB * half + HB].rearrange("p c t -> p (c t)"), ka, kb, ALU.add).then_inc(s_kv, 1)
                return c.n

            def levels_k(g, half, base):
                c = Chain(pool, s_pool, base)
                pool.wait_ge(s_rk, 3 * (2 * g + half) + 3)
                pool.wait_ge(s_kv, 2 * g + half + 1)
                kvh = kv[:, HB * half:HB * half + HB]
                for h in HALVES[::-1][1:]:
                    slot = HALVES.index(h)
                    sv = suf[:].rearrange("p (n two h) -> p n two h", two=2, h=h)
                    ks = kvh.rearrange("p c (n two h) -> p (c n) two h", two=2, h=h)[:, :, 0, :]
                    ko = kl[:, slot, HB * half:HB * half + HB].rearrange("p c (n h) -> p (c n) h", h=h)
                    whole = rk[:].rearrange("p (n two j) -> p n two j", two=2, j=h // 2)[:, :, :, h // 2 - 1]
                    if h < 32:
                        c.step(pool.tensor_tensor(whole[:, :, 1], whole[:, :, 0], whole[:, :, 1], ALU.mult))
                    if h == 32:
                        pool.tensor_tensor(ko, ks, sv[:, :, 0, :], ALU.mult).then_inc(s_klev, 1)
                    else:
                        c.step(pool.tensor_tensor(ko, ks, sv[:, :, 0, :], ALU.mult))
                        c.wait()
                        total = rk[:].rearrange("p (n two h) -> p n two h", two=2, h=h)[:, :, 1, h - 1]
                        c.step(pool.tensor_tensor(sv[:, :, 0, :], sv[:, :, 0, :], spread(total, 2, h), ALU.mult))
                        c.wait()
                return c.n

            def values(g, half):
                kind = "VB" if half else "VA"
                for k in range(4):
                    if isfirst(g) and not half:
                        count = ahead_index("VA", 0, k) + 1
                    elif half:
                        count = fill_index(g, kind, k) + 1
                    elif isinstance(g, int):
                        count = fill_index(g - 1, kind, k) + 1
                    else:
                        count = fills_before(g, False) - 4 - (3 - k)
                    pool.wait_ge(s_pevac, 2 * count)
                    part = v1[:, 2 * k:2 * k + 2, 256 * half:256 * half + 256]
                    pool.tensor_tensor(part, part, spread(bv[:, 256 * half:256 * half + 256], 1, 2), ALU.add).then_inc(s_v, 1)

            pool.wait_ge(s_pads, 3)
            silu(0, uT[:, :, 0:TIME])
            pool.wait_ge(s_load, 16 * 9)
            for kind in (0, 3):
                w = wqk[:, kind].rearrange("p a (hh r d) -> p a hh r d", hh=2, r=2)[:, :, :, 1, :]
                pool.tensor_scalar(w, w, -1.0, None, ALU.mult).then_inc(s_signs, 1)
                b = bqk[:, 4 * kind:4 * kind + 4]
                pool.tensor_scalar(b, b, sign, None, ALU.mult).then_inc(s_signs, 1)
            pool.wait_ge(s_h0in, 16 * 8)
            h0im = h0[:].rearrange("p a (hh r e) -> p a hh r e", hh=2, r=2)[:, :, :, 1, :]
            pool.tensor_scalar(h0im, h0im, sign, None, ALU.mult).then_inc(s_h0sign, 1)
            pool.tensor_scalar(wy[:, 1, :, :], wy[:, 1, :, :], sign, None, ALU.mult).then_inc(s_h0sign, 1)
            n = rho(0, 0)
            pool.wait_ge(s_pfill, ahead_index("QB", 0, 3) + 1)
            pool.wait_ge(s_us, 8)
            silu(ahead_index("U", 1, 0), uT[:, :, 0:TIME])
            n += turn_k(0, 0, n)
            n += levels_k(0, 0, n)
            values(0, 0)
            n += rho(1, n)
            pool.wait_ge(s_load, 16 * 9)
            pool.wait_ge(s_xt_ps, 4)
            pool.tensor_tensor(x1[:], x1[:], spread(bout[0:ROWS, :], 1, TILES), ALU.add).then_inc(s_bout, 1)
            START, STEPS = n, 2 * (2 + 12) + 1

            def body(g):
                n = START + STEPS * g - isfinal(g)
                n += turn_k(g, 1, n)
                n += levels_k(g, 1, n)
                if has("Z", g):
                    if not (isinstance(g, int) and g == 1):
                        pool.wait_ge(s_vfill, fills_before(g, True))
                    silu(fill_index(g, "Z", 0), z2[:].rearrange("p (b t) -> p b t", b=GB))
                if has("U", g):
                    pool.wait_ge(s_pfill, fill_index(g, "QB", 3) + 1)
                    pool.wait_ge(s_us, 8 * g + 16)
                    silu(fill_index(g, "U", 0), uT[:, :, 0:TIME])
                values(g, 1)
                if not isfinal(g):
                    n += turn_k(g + 1, 0, n)
                    n += levels_k(g + 1, 0, n)
                    values(g + 1, 0)
                if has("U", g):
                    n += rho(g + 2, n)

            body(0)
            with pool.Fori(1, GROUPS - 2) as g:
                body(g)
            body(GROUPS - 2)
            body(LAST)
            pool.wait_ge(s_vfill, fills_before(LAST, True) + 2)
            silu(fills_before(LAST, False) + 5, z2[:].rearrange("p (b t) -> p b t", b=GB))

        @block.vector
        def _(dve):
            dve.memset(psum[:, 1024:2048], 0.0).then_inc(s_mask, 1)
            def cmul_split(c, t, out0, out1):
                c.step(dve.tensor_tensor(out0, t[:, 0, 0], t[:, 1, 1], ALU.subtract))
                c.step(dve.tensor_tensor(out1, t[:, 0, 1], t[:, 1, 0], ALU.add))

            def squares(g):
                dve.wait_ge(s_sq, 2 * g + 2)
                if not isfirst(g):
                    dve.wait_ge(s_rho, g)
                dve.tensor_tensor(mag[:], sq[:, 0, :], sq[:, 1, :], ALU.add).then_inc(s_mag, 1)

            def gates_1(c, g):
                dve.wait_ge(s_root, g + 1)
                c.step(dve.tensor_scalar(den[:], mag[:], 1.0, None, ALU.add))
                c.wait()
                c.step(dve.tensor_tensor(inv[:], root[:], den[:], ALU.mult))
                c.wait()
                c.step(dve.reciprocal(third[:], inv[:]))
                c.wait()

            def gates_1b(c, g):
                dve.tensor_tensor(inv[:], third[:], den[:], ALU.mult).then_inc(s_inv, 1)
                dve.wait_ge(s_inv, g + 1)
                t = tmp[:, 1, 0:8 * TP]
                c.step(dve.tensor_tensor(t, inv[:], inv[:], ALU.mult))
                c.wait()
                c.step(dve.tensor_tensor(t, t, mag[:], ALU.mult))
                c.wait()
                c.step(dve.tensor_scalar(t, t, -0.5, 1.5, ALU.mult, ALU.add))
                c.wait()
                c.step(dve.tensor_tensor(inv[:], inv[:], t, ALU.mult))
                c.wait()
                dve.tensor_tensor(pp[:].rearrange("p r c t -> p r (c t)"), ag[:].rearrange("p r c t -> p r (c t)"),
                                  spread(inv[:], 1, 2), ALU.mult).then_inc(s_pp, 1)

            def eighths(t):
                return t.rearrange("p r c (n j) -> p r (c n) j", j=8)

            def gates_2(c, g):
                run, one = eighths(gx[:, 1:3]), eighths(pp[:])
                dve.wait_ge(s_pp, g + 1)
                if not isfirst(g):
                    for half in range(2):
                        dve.wait_ge(s_exp[half], 128 * g)
                c.step(dve.tensor_copy(run[:, :, :, 0], one[:, :, :, 0]))
                yield
                t = small[:].rearrange("p (x r m) -> p x r m", x=2, r=2)
                for j in range(1, 8):
                    c.step(dve.tensor_tensor(t, spread(run[:, :, :, j - 1], 1, 2), spread(one[:, :, :, j], 2, 2), ALU.mult))
                    yield
                    cmul_split(c, t, run[:, 0, :, j], run[:, 1, :, j])
                    yield

            def gates_3(c, g):
                run = gx[:, 1:3].rearrange("p r c (n j) -> p r c n j", j=8)
                c.step(dve.memset(bp[:, 0, :, 0], 1.0))
                c.step(dve.memset(bp[:, 1, :, 0], 0.0))
                yield
                t = small[:, 0:32].rearrange("p (x r m) -> p x r m", x=2, r=2)
                for n in range(1, 8):
                    c.step(dve.tensor_tensor(t, spread(bp[:, :, :, n - 1], 1, 2), spread(run[:, :, :, n - 1, 7], 2, 2), ALU.mult))
                    yield
                    cmul_split(c, t, bp[:, 0, :, n], bp[:, 1, :, n])
                    yield

            def gates_4(c, g):
                run, b = eighths(gx[:, 1:3]), bp[:].rearrange("p r c n -> p r (c n)")
                ta = tmp[:, :, 0:512].rearrange("p r (m j) -> p r m j", j=8)
                tb = tmp[:, :, 512:1024].rearrange("p r (m j) -> p r m j", j=8)
                for r in range(2):
                    c.step(dve.tensor_tensor(ta[:, r], run[:, r], spread(b[:, 0], 2, 8), ALU.mult))
                    c.step(dve.tensor_tensor(tb[:, r], run[:, r], spread(b[:, 1], 2, 8), ALU.mult))
                c.wait()
                c.step(dve.tensor_tensor(run[:, 0], ta[:, 0], tb[:, 1], ALU.subtract))
                c.wait()
                dve.tensor_tensor(run[:, 1], ta[:, 1], tb[:, 0], ALU.add).then_inc(s_gates, 1)

            def turn_q(c, g, half):
                k = 2 * g + half
                dve.wait_ge(s_exp[half], 128 * g + 128)
                if not (isfirst(g) and half == 0):
                    dve.wait_ge(s_klev, k)
                pre = gd[:, 0, HALF * half:HALF * half + HALF].rearrange("p a b t -> p (a b t)")
                two = suf[:].rearrange("p (n two) -> p n two", two=2)
                dve.tensor_copy(rk[:], pre).then_inc(s_rk, 1)
                dve.tensor_copy(two[:, :, 0], pre.rearrange("p (n two) -> p n two", two=2)[:, :, 1]).then_inc(s_rk, 1)
                dve.memset(two[:, :, 1], 1.0).then_inc(s_rk, 1)
                dve.wait_ge(s_pevac, qk_read(g, half))
                dve.wait_ge(s_gates, g + 1)
                q = qk[:, 0:2, HALF * half:HALF * half + HALF].rearrange("p k a b t -> p k (a b t)")
                cr, ci = (gd[:, i, HALF * half:HALF * half + HALF].rearrange("p a b t -> p (a b t)") for i in (1, 2))
                ta, tb = (tmp[:, i].rearrange("p (v x) -> p v x", v=2) for i in range(2))
                out = qv[:, :, HB * half:HB * half + HB].rearrange("p v c t -> p v (c t)")
                c.step(dve.tensor_tensor(ta, q, spread(cr, 1, 2), ALU.mult))
                c.step(dve.tensor_tensor(tb, q, spread(ci, 1, 2), ALU.mult))
                c.wait()
                if not isfirst(g):
                    dve.wait_ge(s_S, 8 * g - 4 + 4 * half)
                dve.tensor_tensor(out[:, 0], ta[:, 0], tb[:, 1], ALU.subtract).then_inc(s_turn, 1)
                dve.tensor_tensor(out[:, 1], ta[:, 1], tb[:, 0], ALU.add).then_inc(s_qv, 1)

            def levels(c, g, half):
                pre = gd[:, 0, HALF * half:HALF * half + HALF].rearrange("p a b t -> p (a b t)")
                dve.wait_ge(s_rk, 3 * (2 * g + half) + 3)
                dve.wait_ge(s_turn, 2 * g + half + 1)
                dve.wait_ge(s_qv, 2 * g + half + 1)
                for h in HALVES[::-1]:
                    slot = HALVES.index(h)
                    pv = pre.rearrange("p (n two h) -> p n two h", two=2, h=h)
                    for v in range(2):
                        qs = qv[:, v, HB * half:HB * half + HB].rearrange("p c (n two h) -> p (c n) two h", two=2, h=h)[:, :, 1, :]
                        qo = ql[:, slot, v, HB * half:HB * half + HB].rearrange("p c (n h) -> p (c n) h", h=h)
                        c.step(dve.tensor_tensor(qo, qs, pv[:, :, 1, :], ALU.mult))
                    yield
                    c.step(dve.tensor_tensor(pv[:, :, 1, :], pv[:, :, 1, :], spread(pv[:, :, 0, h - 1], 2, h), ALU.mult))
                    yield
                dve.tensor_tensor(pre, qv[:, 0, HB * half:HB * half + HB].rearrange("p c t -> p (c t)"), pre, ALU.mult).then_inc(s_lev, 1)

            def masked(g, step):
                dve.wait_ge(s_S, 8 * g + step + 1)
                if not (isfirst(g) and step < 2):
                    dve.wait_ge(s_Y, 8 * g + step - 1)
                dve.tensor_tensor(sm[:, step % 2].rearrange("p u b v t -> p (u b v) t"),
                                  psum[:, 1024:2048].rearrange("p (n t) -> p n t", t=TP),
                                  spread(mask[:, step % 2, :], 1, 4 * GB), ALU.mult).then_inc(s_mask, 1)

            def residual(j0, index, banks):
                dve.wait_ge(s_bout, 1)
                for tl in range(2):
                    row = bass.ds(j0 + tl, 1)
                    tokens = x1[:, row, :].rearrange("p a d -> p (a d)")
                    dve.wait_ge(s_vfill, index + tl + 1)
                    dve.tensor_tensor(tokens, pb[banks[tl]][0:ROWS, 0:DM], tokens, ALU.add).then_inc(s_vevac, 1)
                    dve.wait_ge(s_vevac, index + tl + 1)
                    dve.bn_stats(stats[:, row, :].rearrange("p a d -> p (a d)"), tokens).then_inc(s_stats, 1)

            for i in range(4):
                dve.wait_ge(s_xt_ps, i + 1)
                dve.tensor_copy(xT[:, i * 4 * ROWS:(i + 1) * 4 * ROWS], pb[4 + i][:, 0:4 * ROWS]).then_inc(s_xt, 1)
            c = Chain(dve, s_dve, 0)
            squares(0)
            gates_1(c, 0)
            gates_1b(c, 0)
            in_turns(c, [[gates_2(c, 0), None]])
            in_turns(c, [[gates_3(c, 0), None]])
            gates_4(c, 0)
            squares(1)
            gates_1(c, 1)
            gates_1b(c, 1)
            turn_q(c, 0, 0)
            in_turns(c, [[levels(c, 0, 0), None], [gates_2(c, 1), None]])
            START = c.n

            def body(g, base):
                c = Chain(dve, s_dve, base)
                early = [[levels(c, g, 1), None]] + ([[gates_3(c, g + 1), None]] if has("QB", g) else [])
                late = ([[levels(c, g + 1, 0), None]] if has("QB", g) else []) + ([[gates_2(c, g + 2), None]] if has("A", g) else [])
                masked(g, 0)
                turn_q(c, g, 1)
                in_turns(c, early, 5)
                masked(g, 1)
                in_turns(c, early, 4)
                masked(g, 2)
                in_turns(c, early, 2)
                masked(g, 3)
                in_turns(c, early, None)
                if has("QB", g):
                    gates_4(c, g + 1)
                if has("A", g):
                    squares(g + 2)
                masked(g, 4)
                if has("A", g):
                    gates_1(c, g + 2)
                masked(g, 5)
                if has("A", g):
                    gates_1b(c, g + 2)
                if has("QB", g):
                    turn_q(c, g + 1, 0)
                masked(g, 6)
                in_turns(c, late, 6)
                masked(g, 7)
                in_turns(c, late, None)
                if has("O", g):
                    residual(2 * g - 2, fill_index(g, "O", 0), [RING["O", k] for k in range(2)])
                return c.n

            STEPS = body(0, START)
            with dve.Fori(1, GROUPS - 2) as g:
                body(g, START + STEPS * g)
            n = START + STEPS * (GROUPS - 2)
            n += body(GROUPS - 2, n)
            body(LAST, n)
            residual(2 * LAST, fills_before(LAST, True) + 2, (0, 1))
            dve.wait_ge(s_stats, TILES)



def cross(nc, io, keep, early, late, psum, pb):
    x1, x1T = keep["x1"], keep["xT"]
    QN = 4
    HQ = XH // QN
    S_FILLS = 9
    STAGED_AT = (0, 1, 3, 4, 5, 7, 8, 9, 11)
    with ExitStack() as ctx:
        def sb(name, shape, dt=F32):
            return ctx.enter_context(nc.sbuf_tensor("x_" + name, shape, dt))

        def sem(name):
            return ctx.enter_context(nc.semaphore("x_" + name))

        wq, wk, wvx, wo = (early["w"][n] for n in "qkvo")
        wom = sb("wom", [128, HQ, 128])
        wkh, wkl = sb("wkh", [128, 128], F32R), sb("wkl", [128, 128], F32R)
        qhi, qlo = late["q"]
        qr = sb("qr", [96, QN, TOKENS], F32R)
        qbd = [sb(f"qbd{i}", [96, QN, HQ, TIME], F32R) for i in range(2)]
        raw = early["raw"]
        ctxT = sb("ctxT", [128, CTX])
        chi, clo = sb("chi", [128, CTX], F32R), sb("clo", [128, CTX], F32R)
        khi, klo = sb("khi", [128, CTX], F32R), sb("klo", [128, CTX], F32R)
        k3 = [sb(f"k3_{i}", [96, QN, CTX], F32R) for i in range(2)]
        vx = [sb(f"v{i}", [KP, KT_N, 128]) for i in range(2)]
        probs = [sb(f"probs{i}", [KP, QN * QC]) for i in range(3)]
        o_sb = sb("o", [128, HQ, 2, TIME])
        stats, mv, rstd = keep["stats"], sb("mv", [ROWS, TILES, 2]), sb("rstd", [ROWS, TILES])

        s_x1, s_x1T_ps, s_x1T = sem("x1_ready"), sem("x1T_in_psum"), sem("x1T_ready")
        s_w, s_wom, s_wkh, s_wkl = early["sem"], sem("wo_masked"), sem("wk_hi"), sem("wk_lo")
        s_ctx, s_chi, s_clo, s_q3 = early["ctx"], sem("ctx_hi"), sem("ctx_lo"), sem("q_stacked")
        s_qf, s_qhi, s_qlo, s_qbd = sem("q_filled"), sem("q_hi"), sem("q_split"), sem("q_blocks")
        s_stage, s_read, s_khi = sem("staged"), sem("stage_read"), sem("k_hi")
        s_k3 = [sem("k_stacked0"), sem("k_stacked1")]
        s_qk, s_act, s_pv = sem("scores_made"), sem("probs_made"), sem("pv_done")
        s_oev, s_out, s_res, s_stats = sem("o_read"), sem("out_made"), sem("residual_added"), sem("stats_ready")
        s_ln, s_root, s_norm, s_x2 = sem("ln_chain"), sem("rstd_root"), sem("normed"), sem("x2_stored")

        bank_stage = [pb[5], pb[6]]

        def sfill(n):
            return 15 + S_FILLS * n

        def stacked(n, par):
            return 96 * (n - par) + 192

        block = ctx.enter_context(nc.Block())

        @block.sync
        def _(sp):
            def context(m, par):
                sp.dma_start(raw[par][:], io["ctx"][m].rearrange("(p k) d -> p k d", k=KT_N) if isinstance(m, int) else
                             io["ctx"][bass.ds(m, 1)].rearrange("a (p k) d -> p (a k) d", k=KT_N)).then_inc(s_ctx[par], 16)

            def stack(par):
                for part, half in enumerate((khi, khi, klo)):
                    for q in range(QN):
                        sp.dma_start(k3[par][32 * part:32 * part + 32, q, :].bitcast(F32), half[32 * q:32 * q + 32, :].bitcast(F32)).then_inc(s_k3[par], 16)

            for m in range(2):
                sp.wait_ge(s_read, 2 + 9 * m + 6)
                stack(m)
                sp.wait_ge(s_stage, 9 * m + 3)
                context(m + 2, m)
                if m == 0:
                    sp.wait_ge(s_qlo, 4)
                    for part, half in enumerate((qhi, qlo, qhi)):
                        for q in range(QN):
                            sp.dma_start(qr[32 * part:32 * part + 32, q, :].bitcast(F32), half[32 * q:32 * q + 32, :].bitcast(F32)).then_inc(s_q3, 16)
            sp.wait_ge(s_q3, 192)
            for (dst, src) in late["loads"]:
                sp.dma_start(dst, src).then_inc(late["sem"], 16)

            def pair(i, last):
                for par in range(2):
                    m = 2 * i + par
                    sp.wait_ge(s_read, 2 + 9 * m + 6)
                    sp.wait_ge(s_qk, 12 * m - 12)
                    stack(par)
                    if not last:
                        sp.wait_ge(s_stage, 9 * m + 3)
                        context(m + 2, par)

            with sp.Fori(1, TILES - 1) as i:
                pair(i, False)
            pair(TILES - 1, True)
            x2_v = late["x2d"].rearrange("(j r) d -> r j d", r=ROWS)
            for j in range(0, TILES, 4):
                sp.wait_ge(s_norm, j + 4)
                sp.dma_start(x2_v[:, j:j + 4, :], x1[:, j:j + 4, :]).then_inc(s_x2, 16)
            sp.wait_ge(s_x2, 64)
            sp.wait_ge(late["sem"], 16 * len(late["loads"]))

        @block.tensor
        def _(pe):
            pe.sem_inc(s_pv, 3)

            def transposes(m, par, c, f):
                if c == 0:
                    pe.wait_ge(s_ctx[par], 16 * (m // 2 + 1) if isinstance(m, int) else 8 * (m - par) + 16)
                pe.wait_ge(s_read, f + 1)
                for t in range(4):
                    i = pe.transpose(bank_stage[fpar(f)][:, t * KP:(t + 1) * KP], raw[par][:, 4 * c + t, :], keep["ident"][0:KP, 0:KP])
                i.then_inc(s_stage, 1)

            parity = [0]

            def fpar(f):
                return parity[0] % 2

            def keys(m, c, f):
                pe.wait_ge(s_clo, 3 * m + c + 1)
                pe.wait_ge(s_read, f + 1)
                for i, (w, x) in enumerate(((wkh, chi), (wkl, chi), (wkh, clo))):
                    t = pe.matmul(bank_stage[fpar(f)][:, 0:CH], w[:], x[:, c * CH:(c + 1) * CH], start=(i == 0), stop=(i == 2))
                t.then_inc(s_stage, 1)

            def vals(par, c, f):
                pe.wait_ge(s_read, f + 1)
                for t in range(4):
                    col = (4 * c + t) * KP
                    i = pe.matmul(bank_stage[fpar(f)][0:KP, t * 128:(t + 1) * 128], ctxT[:, col:col + KP], wvx[:],
                                  start=True, stop=True, skip_group_check=True)
                i.then_inc(s_stage, 1)

            def piece(n, par, k, f, has_v, has_tk):
                if k < 3 and has_v:
                    vals(1 - par, k, f)
                elif k >= 3 and has_tk:
                    if k < 6:
                        transposes(n + 2, par, k - 3, f)
                    else:
                        keys(n + 2, k - 6, f)
                parity[0] += 1

            for f, k in enumerate((3, 4, 5, 6, 7, 8, 0, 1, 2)):
                if f == 3:
                    pe.wait_ge(s_w, 64)
                    pe.wait_ge(s_wkl, 1)
                piece(-2 if k >= 3 else -1, k < 3, k, f, True, True)
            for j in range(TILES):
                if j % 4 == 0:
                    pe.wait_ge(s_x1, j + 4)
                t = pe.transpose(pb[j // 4][:, (j % 4) * ROWS:(j % 4 + 1) * ROWS], x1[:, j, :], keep["ident"][0:ROWS, 0:ROWS])
                if j % 4 == 3:
                    t.then_inc(s_x1T_ps, 1)
            for c in range(4):
                pe.wait_ge(s_x1T, c + 1)
                pe.matmul(pb[c][:, 0:4 * ROWS], wq[:], x1T[:, c * 4 * ROWS:(c + 1) * 4 * ROWS],
                          start=True, stop=True).then_inc(s_qf, 1)
            for f in range(9, 15):
                piece(-1, 1, f - 6, f, True, True)
            pe.wait_ge(s_qlo, 4)

            def out_proj(i):
                pe.wait_ge(s_oev, 2 * i + 2)
                pe.wait_ge(s_res, i)
                for h in range(HQ):
                    m = pe.matmul(pb[7][0:ROWS, 0:DM], o_sb[:, h, :, :].rearrange("p b t -> p (b t)"), wom[:, h, :],
                                  start=(h == 0), stop=(h == HQ - 1))
                m.then_inc(s_out, 1)

            def pv(n, par, k):
                T = 12 * n + k
                pe.wait_ge(s_act, T + 3)
                if k == 0:
                    pe.wait_ge(s_oev, n)
                for q in range(QN):
                    m = pe.matmul(pb[4][32 * q:32 * q + 32, 0:QC], vx[par][:, k, 32 * q:32 * q + 32],
                                  probs[k % 3][:, q * QC:(q + 1) * QC], start=(k == 0), stop=(k == KT_N - 1))
                m.then_inc(s_pv, 1)

            def batch(n, par, first, has_v, has_tk):
                parity[0] = 1 + par
                pe.wait_ge(s_qbd, n + 1)
                pe.wait_ge(s_k3[par], stacked(n, par))
                for k in range(KT_N):
                    T = 12 * n + k
                    pe.wait_ge(s_act, T + 1)
                    for q in range(QN):
                        m = pe.matmul(pb[2 * (k % 2) + q // 2][0:KP, (q % 2) * QC:(q % 2 + 1) * QC],
                                      k3[par][:, q, k * KP:(k + 1) * KP], qbd[par][:, q, :, :].rearrange("p h t -> p (h t)"),
                                      start=(q % 2 == 0), stop=True, skip_group_check=True)
                    m.then_inc(s_qk, 1)
                    if k in STAGED_AT:
                        p = STAGED_AT.index(k)
                        piece(n, par, p, sfill(n) + p, has_v, has_tk)
                    if k == 2 and par == 0 and not first:
                        out_proj((n - 1) // 2 if isinstance(n, int) else pair_of[0] - 1)
                    if k == 1:
                        pe.wait_ge(s_read, 2 + (sfill(n) - 6 if not (isinstance(n, int) and n == 0) else 9))
                    if k >= 1:
                        pv(n, par, k - 1)
                    elif not (isinstance(n, int) and n == 0):
                        pv(n - 1, 1 - par, KT_N - 1)

            pair_of = [0]

            def pair(i, first, last):
                pair_of[0] = i
                batch(2 * i, 0, first, True, not last)
                batch(2 * i + 1, 1, first, not last, not last)

            pair(0, True, False)
            with pe.Fori(1, TILES - 1) as i:
                pair(i, False, False)
            pair(TILES - 1, False, True)
            pv(BATCH - 1, 1, KT_N - 1)
            out_proj(TILES - 1)

        @block.scalar
        def _(act):
            act.sem_inc(s_act, 2)
            act.wait_ge(s_w, 64)
            act.activation(wkh[:], wk[:], ACT.Copy).then_inc(s_wkh, 1)

            def c_hi(c, f):
                act.wait_ge(s_read, 2 + f + 1)
                act.activation(chi[:, c * CH:(c + 1) * CH], ctxT[:, c * CH:(c + 1) * CH], ACT.Copy).then_inc(s_chi, 1)

            def k_hi(c, f, bank):
                act.wait_ge(s_stage, f + 1)
                act.activation(khi[:, c * CH:(c + 1) * CH], bank[:, 0:CH], ACT.Copy).then_inc(s_khi, 1)

            for c in range(3):
                c_hi(c, c)
            act.wait_ge(s_ln, TILES + 1)
            act.activation(rstd[:], rstd[:], ACT.Sqrt).then_inc(s_root, 1)
            for c in range(3):
                k_hi(c, 3 + c, bank_stage[(3 + c) % 2])
            for c in range(4):
                act.wait_ge(s_qf, c + 1)
                act.activation(qhi[:, c * 4 * ROWS:(c + 1) * 4 * ROWS], pb[c][:, 0:4 * ROWS], ACT.Copy).then_inc(s_qhi, 1)
            for c in range(3):
                c_hi(c, 9 + c)
            act.wait_ge(s_k3[0], 192)
            for c in range(3):
                k_hi(c, 12 + c, bank_stage[(12 + c) % 2])

            def batch(n, par, has_tk):
                for k in range(KT_N):
                    T = 12 * n + k
                    act.wait_ge(s_qk, T + 1)
                    act.wait_ge(s_pv, T + 1)
                    src = psum[0:KP, 1024 * (k % 2):1024 * (k % 2) + 1024].rearrange("p (a c) -> p a c", a=2)[:, :, 0:2 * QC]
                    act.activation(probs[k % 3][:].rearrange("p (a c) -> p a c", a=2), src, ACT.Sigmoid, scale=XSCALE).then_inc(s_act, 1)
                    p = STAGED_AT.index(k) if k in STAGED_AT else -1
                    if has_tk and 3 <= p < 6:
                        c_hi(p - 3, sfill(n) + p)
                    if has_tk and 6 <= p < 9:
                        if p == 6:
                            act.wait_ge(s_k3[1 - par], stacked(n + 1, 1 - par))
                        k_hi(p - 6, sfill(n) + p, bank_stage[(1 + par + p) % 2])

            with act.Fori(0, TILES - 1) as i:
                batch(2 * i, 0, True)
                batch(2 * i + 1, 1, True)
            batch(2 * TILES - 2, 0, False)
            batch(2 * TILES - 1, 1, False)
            act.wait_ge(s_ln, 2 * TILES + 3)
            act.activation(rstd[:], rstd[:], ACT.Sqrt).then_inc(s_root, 1)

        @block.gpsimd
        def _(pool):
            def c_lo(m, c):
                pool.wait_ge(s_chi, 3 * m + c + 1)
                cols = slice(c * CH, (c + 1) * CH)
                pool.tensor_tensor(clo[:, cols], ctxT[:, cols], chi[:, cols].bitcast(F32), ALU.subtract).then_inc(s_clo, 1)

            pool.wait_ge(s_wkh, 1)
            pool.tensor_tensor(wkl[:], wk[:], wkh[:].bitcast(F32), ALU.subtract).then_inc(s_wkl, 1)
            for c in range(3):
                c_lo(0, c)
            with pool.Fori(1, BATCH) as m:
                for c in range(3):
                    c_lo(m, c)

        @block.vector
        def _(dve):
            dve.sem_inc(s_read, 2)
            def blocks(n, par):
                src = qr[:, :, bass.ds(n * TIME, TIME)].bitcast(F32)
                dve.tensor_tensor(qbd[par][:], spread(src, 2, HQ),
                                  keep["hmask"][0:96, 0:HQ].unsqueeze(1).unsqueeze(3).broadcast_to([96, QN, HQ, TIME]), ALU.mult).then_inc(s_qbd, 1)

            def t_read(c, f, bank):
                dve.wait_ge(s_stage, f + 1)
                dve.tensor_copy(ctxT[:, c * CH:(c + 1) * CH], bank[:, 0:CH]).then_inc(s_read, 1)

            def k_lo(c, f, bank, khis):
                dve.wait_ge(s_khi, khis)
                dve.tensor_tensor(klo[:, c * CH:(c + 1) * CH], bank[:, 0:CH],
                                  khi[:, c * CH:(c + 1) * CH].bitcast(F32), ALU.subtract).then_inc(s_read, 1)

            def v_read(par, c, f, bank):
                dve.wait_ge(s_stage, f + 1)
                dve.tensor_copy(vx[par][:, 4 * c:4 * c + 4, :], bank[0:KP, :].rearrange("p (t d) -> p t d", t=4)).then_inc(s_read, 1)

            def tk(m, f, p):
                for k in range(6):
                    if k == 3 and not (isinstance(m, int) and m == 0):
                        dve.wait_ge(s_k3[(p + 1) % 2], stacked(m - 1, (p + 1) % 2))
                    bank = bank_stage[(p + k) % 2]
                    if k < 3:
                        t_read(k, f + k, bank)
                    else:
                        k_lo(k - 3, f + k, bank, 3 * m + k - 3 + 1)

            def normalize(steps, done):
                for j in range(TILES):
                    dve.bn_aggr(mv[:, j, :], stats[:, j, :]).then_inc(s_ln, 1)
                dve.wait_ge(s_ln, steps + TILES)
                dve.tensor_scalar(rstd[:], mv[:, :, 1], EPS, None, ALU.add).then_inc(s_ln, 1)
                dve.wait_ge(s_root, 1 if steps == 0 else 2)
                dve.reciprocal(rstd[:], rstd[:]).then_inc(s_ln, 1)
                dve.wait_ge(s_ln, steps + TILES + 2)
                for j in range(TILES):
                    dve.tensor_scalar(x1[:, j, :], x1[:, j, :], mv[:, j, 0:1], rstd[:, j:j + 1], ALU.subtract, ALU.mult).then_inc(done, 1)

            for c in range(3):
                t_read(c, c, bank_stage[c % 2])
            normalize(0, s_x1)
            for c in range(3):
                k_lo(c, 3 + c, bank_stage[(3 + c) % 2], c + 1)
            for c in range(3):
                v_read(0, c, 6 + c, bank_stage[(6 + c) % 2])
            for c in range(4):
                dve.wait_ge(s_x1T_ps, c + 1)
                dve.tensor_copy(x1T[:, c * 4 * ROWS:(c + 1) * 4 * ROWS], pb[c][:, 0:4 * ROWS]).then_inc(s_x1T, 1)
            for c in range(4):
                cols = slice(c * 4 * ROWS, (c + 1) * 4 * ROWS)
                dve.wait_ge(s_qhi, c + 1)
                dve.tensor_tensor(qlo[:, cols], pb[c][:, 0:4 * ROWS], qhi[:, cols].bitcast(F32), ALU.subtract).then_inc(s_qlo, 1)
            dve.wait_ge(s_w, 64)
            for h in range(HQ):
                dve.tensor_scalar(wom[:, h, :], wo[:], keep["hmask"][:, h:h + 1], None, ALU.mult).then_inc(s_wom, 1)

            tk(1, 9, 1)
            dve.wait_ge(s_q3, 192)
            blocks(0, 0)

            def o_read(n, par, i):
                if par == 0 and not (isinstance(i, int) and i == 0):
                    dve.wait_ge(s_out, i)
                dve.wait_ge(s_pv, 3 + 12 * n + 12)
                dve.tensor_copy(o_sb[:, :, par, :], pb[4][:, 0:QC].rearrange("p (h t) -> p h t", h=HQ)).then_inc(s_oev, 1)

            def batch(n, par, has_next, has_tk, i):
                if par == 1:
                    o_read(n - 1, 0, i)
                elif not (isinstance(i, int) and i == 0):
                    o_read(n - 1, 1, i)
                if has_next:
                    dve.wait_ge(s_qk, 12 * n)
                    blocks(n + 1, 1 - par)
                    for c in range(3):
                        v_read(1 - par, c, sfill(n) + c, bank_stage[(1 + par + c) % 2])
                if has_tk:
                    tk(n + 2, sfill(n) + 3, par)

            def residual(i):
                row = bass.ds(i, 1)
                dve.wait_ge(s_out, i + 1)
                dve.tensor_tensor(x1[:, row, :].rearrange("p a d -> p (a d)"), pb[7][0:ROWS, 0:DM],
                                  x1[:, row, :].rearrange("p a d -> p (a d)"), ALU.add).then_inc(s_res, 1)
                dve.wait_ge(s_res, i + 1)
                dve.bn_stats(stats[:, row, :].rearrange("p a d -> p (a d)"), x1[:, row, :].rearrange("p a d -> p (a d)")).then_inc(s_stats, 1)

            def pair(i, last):
                batch(2 * i, 0, True, not last, i)
                if not (isinstance(i, int) and i == 0):
                    residual(i - 1)
                batch(2 * i + 1, 1, not last, not last, i)

            pair(0, False)
            with dve.Fori(1, TILES - 1) as i:
                pair(i, False)
            pair(TILES - 1, True)
            o_read(BATCH - 1, 1, TILES - 1)
            residual(TILES - 1)
            dve.wait_ge(s_stats, TILES)
            dve.wait_ge(s_x1, TILES)
            normalize(TILES + 2, s_norm)



def experts(nc, io, keep, late, psum, pb):
    CE = CAP * EX
    KK = 4
    w = late["t"]
    with ExitStack() as ctx:
        def sb(name, shape, dt=F32):
            return ctx.enter_context(nc.sbuf_tensor("e_" + name, shape, dt))

        def sem(name):
            return ctx.enter_context(nc.semaphore("e_" + name))

        ident = keep["ident"]
        X2 = sb("x2", [128, KL, DM])
        X2T = sb("x2T", [128, KL, 128])
        lg = sb("lg", [128, KL, EX])
        red = sb("red", [128, KL])
        pr = sb("pr", [128, 16, CAP, EX])
        sc = sb("sc", [128, 16, BATCH])
        oh = sb("oh", [128, 16, BATCH])
        t1 = sb("t1", [128, 16, BATCH])
        i1, i2, m1 = sb("i1", [128, 16]), sb("i2", [128, 16]), sb("m1", [128, 16])
        ohn = sb("ohn", [128, 16, 4, CE])
        hg = sb("hg", [128, CE, TIME])
        qkv = sb("qkv", [TIME, EX, CAP, 3 * EDH])
        ta, tb = sb("ta", [TIME, EX, EDH]), sb("tb", [TIME, EX, EDH])
        att = sb("att", [TIME, EX, CAP, CAP])
        attT = sb("attT", [64, TIME])
        am, asum = sb("am", [64, 1]), sb("asum", [64, 1])
        pT = sb("pT", [TIME, EX, CAP, CAP])
        av = sb("av", [TIME, CAP, EX, EDH])
        avT = sb("avT", [128, EX // 2, CAP, TIME])
        ao = sb("ao", [CAP * TIME, EX, DM])
        aoT = sb("aoT", [128, KK, 4, DM])
        y = sb("y", [128, KL, DM])
        xb = sb("xb", [128, KL, DM])
        stats, mv, rstd = sb("stats", [128, KL, 6]), sb("mv", [128, KL, 2]), sb("rstd", [128, KL])
        shift = sb("shift", [128, KL])
        BY_DVE = KL // 2

        s_x2, s_x2T_ps, s_x2T = sem("x2_loaded"), sem("x2T_in_psum"), sem("x2T_ready")
        s_lg, s_sub, s_exp, s_pr, s_sc_ps, s_oh, s_ohn_ps, s_ohn = (sem(n) for n in (
            "logits", "logits_less_max", "exps", "probs", "probs_turned", "one_hot", "one_hot_turned", "one_hot_read"))
        s_hg_ps, s_hg, s_qkv_ps, s_qkv, s_att = (sem(n) for n in ("gathered", "gathered_read", "qkv_filled", "qkv_read", "att_ready"))
        s_attT, s_amax, s_aexp, s_pn, s_pT_ps, s_pT = (sem(n) for n in (
            "att_turned", "att_max", "att_exp", "att_normed", "p_turned", "p_ready"))
        s_av, s_avT_ps, s_avT, s_ao_ps, s_ao, s_aod, s_aoT = (sem(n) for n in (
            "av_ready", "av_turned", "avT_ready", "ao_filled", "ao_read", "ao_stored", "ao_loaded"))
        s_y_ps, s_var, s_root, s_res, s_outn, s_fin = (sem(n) for n in ("scattered", "variance", "root", "residual", "out_normed", "out_stored"))
        s_dve = sem("dve_chain")
        s_pad = sem("pad_set")
        s_xb, s_qkvc, s_qkvd = sem("x_plus_b"), sem("qkv_copied"), sem("qkv_even_read")
        s_neg, s_outa = sem("mean_negated"), sem("out_normed_by_act")

        block = ctx.enter_context(nc.Block())

        @block.sync
        def _(sp):
            src = late["x2d"].rearrange("(n k q) d -> q n k d", k=KL, q=4)
            for q in range(4):
                sp.dma_start(X2[32 * q:32 * q + 32, :, :], src[q]).then_inc(s_x2, 16)
            sp.wait_ge(s_ao, 4)
            for i in range(CAP):
                sp.dma_start(late["aod"][i * EX:(i + 1) * EX, 0:TIME].rearrange("e l d -> l e d"),
                             ao[i * TIME:(i + 1) * TIME, :, :]).then_inc(s_aod, 16)
            sp.wait_ge(s_aod, 16 * CAP)
            src = late["aod"].rearrange("c (kk k4 q) d -> k4 c kk (q d)", kk=KK, k4=4)
            for k4 in range(4):
                n = KK if k4 < 2 else KK - 1
                sp.dma_start(aoT[32 * k4:32 * k4 + 32, 0:n, :, :].rearrange("c k q d -> c k (q d)"), src[k4][:, 0:n, :]).then_inc(s_aoT, 16)
            dst = io["out"].rearrange("n (k q) d -> q n k d", q=4)
            sp.wait_ge(s_outn, BY_DVE)
            sp.wait_ge(s_outa, KL - BY_DVE)
            for q in range(4):
                sp.dma_start(dst[q], y[32 * q:32 * q + 32, :, :]).then_inc(s_fin, 16)
            sp.wait_ge(s_fin, 64)

        @block.tensor
        def _(pe):
            pe.wait_ge(s_x2, 64)
            for k in range(KL):
                t = pe.transpose(pb[k // 4][:, (k % 4) * 128:(k % 4 + 1) * 128], X2[:, k, :], ident[:])
                if k % 4 == 3 or k == KL - 1:
                    t.then_inc(s_x2T_ps, 1)
            for k in range(KL):
                if k % 4 == 0:
                    pe.wait_ge(s_x2T, k // 4 + 1)
                m = pe.matmul(pb[4][:, k * EX:(k + 1) * EX], X2T[:, k, :], w["wg"], start=True, stop=True, skip_group_check=True)
            m.then_inc(s_lg, 1)
            pe.wait_ge(s_pr, 2)
            for kk in range(KK):
                t = pe.transpose(pb[5][:, kk * 128:(kk + 1) * 128], pr[:, 4 * kk:4 * kk + 4, :, :].rearrange("p k c e -> p (k c e)"), ident[:])
            t.then_inc(s_sc_ps, 1)
            pe.wait_ge(s_oh, 1)
            for kk in range(KK):
                t = pe.transpose(pb[6][:, kk * 128:(kk + 1) * 128], oh[:, 4 * kk:4 * kk + 4, :].rearrange("p q n -> p (q n)"), ident[:])
            t.then_inc(s_ohn_ps, 1)
            for k in range(KL):
                if k % 4 == 0:
                    pe.wait_ge(s_ohn, k // 4 + 1)
                m = pe.matmul(pb[k // 4][:, (k % 4) * 128:(k % 4 + 1) * 128], X2[:, k, :], ohn[:, k, :, :].rearrange("p q c -> p (q c)"),
                              start=True, stop=True, skip_group_check=True)
                if k % 4 == 3 or k == KL - 1:
                    m.then_inc(s_hg_ps, 1)
            pe.wait_ge(s_hg, 4)
            for e in range(EX):
                if e >= 4:
                    pe.wait_ge((s_qkvd, s_qkvc)[e % 2], e // 2 - 1)
                for c in range(CAP):
                    m = pe.matmul(pb[4 + e % 4][0:TIME, c * 192:(c + 1) * 192], hg[:, c * EX + e, :], w["wqkv"][:, e, :],
                                  start=(c == 0), stop=True, skip_group_check=True)
                m.then_inc(s_qkv_ps, 1)
            pe.wait_ge(s_att, 8)
            pe.transpose(pb[0][0:64, 0:TIME], att[:].rearrange("l e i j -> l (e i j)"), ident[0:TIME, 0:TIME]).then_inc(s_attT, 1)
            pe.wait_ge(s_pn, 1)
            pe.transpose(pb[1][0:TIME, 0:64], attT[:], ident[0:64, 0:64]).then_inc(s_pT_ps, 1)
            for i in range(CAP):
                pe.wait_ge(s_av, i + 1)
                for hp in range(EX // 2):
                    t = pe.transpose(pb[2 + i][:, hp * TIME:(hp + 1) * TIME], av[:, i, 2 * hp:2 * hp + 2, :].rearrange("l e d -> l (e d)"), ident[0:TIME, 0:TIME])
                t.then_inc(s_avT_ps, 1)
            pe.wait_ge(s_avT, CAP)
            for hp in range(EX // 2):
                m = pe.matmul(pb[4 + hp // 2][0:CAP * TIME, (hp % 2) * 2 * DM:(hp % 2 + 1) * 2 * DM], avT[:, hp, :, :],
                              w["woP"][:, hp, :], start=True, stop=True, skip_group_check=True)
                if hp % 2 == 1:
                    m.then_inc(s_ao_ps, 1)
            pe.wait_ge(s_aoT, 64)
            for k4 in range(4):
                for kk in range(KK if k4 < 2 else KK - 1):
                    for q in range(4):
                        rows = slice(32 * k4, 32 * k4 + 32)
                        m = pe.matmul(pb[k4][32 * q:32 * q + 32, kk * DM:(kk + 1) * DM], oh[rows, 4 * kk + q, :], aoT[rows, kk, q, :],
                                      start=True, stop=True, skip_group_check=True)
                m.then_inc(s_y_ps, 1)

        @block.scalar
        def _(act):
            act.wait_ge(s_sub, 1)
            act.activation(lg[:], lg[:], ACT.Exp).then_inc(s_exp, 1)
            for e in range(1, EX, 2):
                act.wait_ge(s_qkv_ps, e + 1)
                act.activation(qkv[:, e, :, :].rearrange("l c x -> l (c x)"), pb[4 + e % 4][0:TIME, 0:CAP * 192], ACT.Copy).then_inc(s_qkvc, 1)
            act.wait_ge(s_amax, 1)
            act.activation(attT[:], pb[0][0:64, 0:TIME], ACT.Exp, bias=am[:, 0:1], scale=float(EDH) ** -0.5, accum_out=asum[:, 0:1]).then_inc(s_aexp, 1)
            for r in range(2):
                act.wait_ge(s_var, r + 1)
                act.activation(rstd[:], rstd[:], ACT.Sqrt).then_inc(s_root, 1)
            act.wait_ge(s_neg, 1)
            for k in range(BY_DVE, KL):
                act.activation(y[:, k, :], y[:, k, :], ACT.Identity, bias=shift[:, k:k + 1], scale=rstd[:, k:k + 1]).then_inc(s_outa, 1)

        @block.gpsimd
        def _(pool):
            pool.memset(pr[:, KL:16, :, :], 0.0).then_inc(s_pad, 1)
            pool.wait_ge(s_x2, 64)
            pool.tensor_tensor(xb[:], X2[:], spread(w["lnb"], 1, KL), ALU.add).then_inc(s_xb, 1)
            for e in range(1, EX, 2):
                pool.wait_ge(s_qkvc, e // 2 + 1)
                pool.tensor_tensor(qkv[:, e, :, :], qkv[:, e, :, :], spread(w["bqkv"][:, e, :], 1, CAP), ALU.add).then_inc(s_qkv, 1)

        @block.vector
        def _(dve):
            c = Chain(dve, s_dve, 0)
            for b in range(4):
                n = 4 if b < 3 else KL - 12
                dve.wait_ge(s_x2T_ps, b + 1)
                dve.tensor_copy(X2T[:, 4 * b:4 * b + n, :], pb[b][:, 0:n * 128].rearrange("p (k t) -> p k t", t=128)).then_inc(s_x2T, 1)
            dve.wait_ge(s_lg, 1)
            L = pb[4][:, 0:KL * EX].rearrange("p (k e) -> p k e", e=EX)
            c.step(dve.tensor_reduce(red[:], L, AX.X, ALU.max))
            c.wait()
            dve.tensor_tensor(lg[:], L, spread(red[:], 2, EX), ALU.subtract).then_inc(s_sub, 1)
            dve.wait_ge(s_exp, 1)
            c.step(dve.tensor_reduce(red[:], lg[:], AX.X, ALU.add))
            c.wait()
            c.step(dve.reciprocal(red[:], red[:]))
            c.wait()
            dve.wait_ge(s_pad, 1)
            for h in range(CAP):
                dve.tensor_tensor(pr[:, 0:KL, h, :], lg[:], spread(red[:], 2, EX), ALU.mult).then_inc(s_pr, 1)
            iota = spread(w["iota"], 1, 16)
            dve.wait_ge(s_sc_ps, 1)
            c.step(dve.tensor_copy(sc[:], pb[5][:, :].rearrange("p (l n) -> p l n", n=BATCH)))
            c.wait()
            for rnd, idx in enumerate((i1, i2)):
                c.step(dve.tensor_reduce(m1[:], sc[:], AX.X, ALU.max))
                c.wait()
                c.step(dve.tensor_tensor(t1[:], sc[:], spread(m1[:], 2, BATCH), ALU.is_equal))
                c.wait()
                c.step(dve.tensor_tensor(t1[:], t1[:], iota, ALU.mult))
                c.wait()
                c.step(dve.tensor_reduce(idx[:], t1[:], AX.X, ALU.max))
                c.wait()
                if rnd == 0:
                    c.step(dve.tensor_tensor(t1[:], iota, spread(idx[:], 2, BATCH), ALU.is_equal))
                    c.wait()
                    c.step(dve.scalar_tensor_tensor(sc[:], t1[:], -4.0, sc[:], ALU.mult, ALU.add))
                    c.wait()
            c.step(dve.tensor_tensor(m1[:], i1[:], i2[:], ALU.max))
            c.step(dve.tensor_tensor(i1[:], i1[:], i2[:], ALU.min))
            c.wait()
            c.step(dve.tensor_tensor(m1[:], m1[:], i1[:], ALU.subtract))
            c.wait()
            c.step(dve.tensor_scalar(m1[:], m1[:], w["first"][:, 0:1], None, ALU.mult))
            c.wait()
            c.step(dve.tensor_tensor(i1[:], i1[:], m1[:], ALU.add))
            c.wait()
            dve.tensor_tensor(oh[:], iota, spread(i1[:], 2, BATCH), ALU.is_equal).then_inc(s_oh, 1)
            dve.wait_ge(s_ohn_ps, 1)
            for kk in range(KK):
                dve.tensor_tensor(ohn[:, 4 * kk:4 * kk + 4, :, :], spread(pb[6][:, kk * 128:(kk + 1) * 128].rearrange("p (k c) -> p k c", c=CE), 2, 4),
                                  spread(spread(w["qmask"], 1, 4), 3, CE), ALU.mult).then_inc(s_ohn, 1)
            for b in range(4):
                n = 4 if b < 3 else KL - 12
                dve.wait_ge(s_hg_ps, b + 1)
                dve.tensor_copy(hg[:, :, 16 * b:16 * b + 4 * n].rearrange("p c l -> p l c"),
                                pb[b][:, 0:n * 128].rearrange("p (l c) -> p l c", c=CE)).then_inc(s_hg, 1)
            GE = 4
            for g in range(EX // GE):
                es = slice(GE * g, GE * g + GE)
                for e in range(GE * g, GE * g + GE, 2):
                    dve.wait_ge(s_qkv_ps, e + 1)
                    dve.tensor_tensor(qkv[:, e, :, :], pb[4 + e % 4][0:TIME, 0:CAP * 192].rearrange("l (c x) -> l c x", c=CAP),
                                      spread(w["bqkv"][:, e, :], 1, CAP), ALU.add).then_inc(s_qkvd, 1)
                dve.wait_ge(s_qkvd, 2 * g + 2)
                dve.wait_ge(s_qkv, 2 * g + 2)
                if g > 0:
                    dve.wait_ge(s_att, 2 * g)
                for i in range(CAP):
                    out = (ta, tb)[i]
                    c.step(dve.tensor_tensor(out[:, 0:2 * GE, :].rearrange("l (e j) d -> l e j d", j=CAP),
                                             spread(qkv[:, es, i, 0:EDH], 2, CAP), qkv[:, es, :, EDH:2 * EDH], ALU.mult))
                c.wait()
                for i in range(CAP):
                    out = (ta, tb)[i]
                    dve.tensor_reduce(att[:, es, i, :], out[:, 0:2 * GE, :].rearrange("l (e j) d -> l e j d", j=CAP), AX.X, ALU.add).then_inc(s_att, 1)
            dve.wait_ge(s_att, 2 * EX // GE)
            dve.wait_ge(s_attT, 1)
            c.step(dve.tensor_reduce(am[:], pb[0][0:64, 0:TIME], AX.X, ALU.max))
            c.wait()
            dve.tensor_scalar(am[:], am[:], -float(EDH) ** -0.5, None, ALU.mult).then_inc(s_amax, 1)
            dve.wait_ge(s_aexp, 1)
            c.step(dve.reciprocal(asum[:], asum[:]))
            c.wait()
            dve.tensor_scalar(attT[:], attT[:], asum[:, 0:1], None, ALU.mult).then_inc(s_pn, 1)
            dve.wait_ge(s_pT_ps, 1)
            dve.tensor_copy(pT[:].rearrange("l e i j -> l (e i j)"), pb[1][0:TIME, 0:64]).then_inc(s_pT, 1)
            dve.wait_ge(s_pT, 1)
            for i in range(CAP):
                c.step(dve.tensor_tensor(ta[:], qkv[:, :, 0, 2 * EDH:], spread(pT[:, :, i, 0], 2, EDH), ALU.mult))
                c.step(dve.tensor_tensor(tb[:], qkv[:, :, 1, 2 * EDH:], spread(pT[:, :, i, 1], 2, EDH), ALU.mult))
                c.wait()
                dve.tensor_tensor(av[:, i, :, :], ta[:], tb[:], ALU.add).then_inc(s_av, 1)
                dve.wait_ge(s_av, i + 1)
            for i in range(CAP):
                dve.wait_ge(s_avT_ps, i + 1)
                dve.tensor_copy(avT[:, :, i, :], pb[2 + i][:, 0:EX // 2 * TIME].rearrange("p (a t) -> p a t", t=TIME)).then_inc(s_avT, 1)
            for b in range(4):
                dve.wait_ge(s_ao_ps, b + 1)
                dve.tensor_tensor(ao[:, 4 * b:4 * b + 4, :], pb[4 + b][0:CAP * TIME, :].rearrange("l (s d) -> l s d", s=4),
                                  spread(w["bo"][0:CAP * TIME, :], 1, 4), ALU.add).then_inc(s_ao, 1)
            for k4 in range(4):
                n = KK if k4 < 2 else KK - 1
                dve.wait_ge(s_y_ps, k4 + 1)
                c.step(dve.tensor_tensor(y[:, k4::4, :], pb[k4][:, 0:n * DM].rearrange("p (k d) -> p k d", d=DM), X2[:, k4::4, :], ALU.add))
            for r in range(2):
                c.wait()
                for k in range(KL):
                    c.step(dve.bn_stats(stats[:, k, :], y[:, k, :]))
                c.wait()
                for k in range(KL):
                    c.step(dve.bn_aggr(mv[:, k, :], stats[:, k, :]))
                c.wait()
                dve.tensor_scalar(rstd[:], mv[:, :, 1], EPS, None, ALU.add).then_inc(s_var, 1)
                dve.wait_ge(s_root, r + 1)
                c.step(dve.reciprocal(rstd[:], rstd[:]))
                c.wait()
                if r == 0:
                    dve.wait_ge(s_xb, 1)
                    for k in range(KL):
                        c.step(dve.scalar_tensor_tensor(y[:, k, :], y[:, k, :], mv[:, k, 0:1], w["lng"], ALU.subtract, ALU.mult))
                    c.wait()
                    for k in range(KL):
                        c.step(dve.scalar_tensor_tensor(y[:, k, :], y[:, k, :], rstd[:, k:k + 1], xb[:, k, :], ALU.mult, ALU.add))
                else:
                    dve.scalar_tensor_tensor(shift[:], mv[:, :, 0], -1.0, rstd[:], ALU.mult, ALU.mult).then_inc(s_neg, 1)
                    for k in range(BY_DVE):
                        dve.tensor_scalar(y[:, k, :], y[:, k, :], mv[:, k, 0:1], rstd[:, k:k + 1], ALU.subtract, ALU.mult).then_inc(s_outn, 1)



def program(nc, io):
    with ExitStack() as ctx:
        def sb(name, shape):
            return ctx.enter_context(nc.sbuf_tensor(name, shape, F32))

        psum = ctx.enter_context(nc.psum_tensor("psum", [128, 8 * 512], F32))
        pb = [psum[:, 512 * i:512 * i + 512] for i in range(8)]
        keep = {"ident": sb("ident", [128, 128]), "hmask": sb("hmask", [128, 5]), "stats": sb("stats", [ROWS, TILES, 6]),
                "x1": sb("x1", [ROWS, TILES, DM]), "xT": sb("xT", [128, TOKENS])}
        x = {n: sb("x_w" + n, [128, 128]) for n in ("q", "k", "v", "o")}
        raw = [sb(f"x_ctx{i}", [KP, KT_N, DM]) for i in range(2)]
        early = {"w": x, "raw": raw, "sem": ctx.enter_context(nc.semaphore("x_weights_loaded")),
                 "ctx": [ctx.enter_context(nc.semaphore(f"x_ctx_loaded{i}")) for i in range(2)]}
        mixer(nc, io, keep, early, psum, pb)
        space = sb("late", [128, 2 * 3 * EX * EDH + EX * DM])
        wide = 3 * EX * EDH
        t = {"wqkv": space[:, 0:wide].rearrange("p (e x) -> p e x", e=EX),
             "bqkv": space[0:TIME, wide:2 * wide].rearrange("p (e x) -> p e x", e=EX),
             "woP": space[:, 2 * wide:].rearrange("p (e x) -> p e x", e=EX // 2)}
        for n, shape in (("wg", [128, EX]), ("bo", [128, DM]), ("lng", [128, DM]), ("lnb", [128, DM]), ("iota", [128, BATCH]), ("first", [128, 1]), ("qmask", [128, 4])):
            t[n] = sb(n, shape)[:]
        late = {"t": t, "sem": ctx.enter_context(nc.semaphore("late_loads")),
                "q": [space[:, TOKENS * i:TOKENS * (i + 1)].bitcast(F32R) for i in range(2)],
                "loads": [(t[n], io["e_" + n].partition_broadcast(t[n].shape[0]) if n in ("bqkv", "bo", "lng", "lnb", "iota")
                           else io["e_" + n]) for n in t],
                "x2d": nc.dram_tensor("x2_scratch", (TOKENS, DM), F32, kind="Internal").ap(),
                "aod": nc.dram_tensor("ao_scratch", (CAP * EX, 64, DM), F32, kind="Internal").ap()}
        cross(nc, io, keep, early, late, psum, pb)
        experts(nc, io, keep, late, psum, pb)


def layouts(inputs):
    a = {k: np.ascontiguousarray(v) for k, v in inputs.items()}
    out = {"x": a["x"], "ctx": a["ctx_1024"]}
    out["w_inT"] = a["L0_attn_W_in"].T
    out["w_outT"] = a["L0_attn_W_out"].T
    w = a["L0_attn_W_qkva"].reshape(PAIRS, 2, DH, 4, 2, DM)
    b = a["L0_attn_b_qkva"].reshape(PAIRS, 2, DH, 4, 2)
    kinds = [(0, (0, 1)), (0, (1, 0)), (1, (0, 1)), (1, (1, 0))]
    out["w_qk"] = np.stack([w[:, :, :, c][:, :, :, list(r)].transpose(4, 0, 1, 3, 2).reshape(DM, PAIRS, 128) for c, r in kinds], 1)
    out["b_qk"] = np.stack([b[:, :, :, c][:, :, :, list(r)].transpose(1, 3, 2, 0).reshape(128, PAIRS) for c, r in kinds], 1).reshape(128, 16)
    wa = w[:, :, :, 3].reshape(2, 2, 2, DH, 2, DM)
    out["w_gate"] = wa.transpose(5, 4, 0, 2, 1, 3).reshape(DM, 2, 2, 128)
    out["b_gate"] = b[:, :, :, 3].reshape(2, 2, 2, DH, 2).transpose(2, 1, 3, 4, 0).reshape(128, 4)
    out["w_v"] = w[:, :, :, 2].transpose(4, 0, 1, 3, 2).reshape(DM, 512)
    out["b_v"] = b[:, :, :, 2].transpose(0, 1, 3, 2).reshape(512)
    out["b_col"] = np.stack([a["L0_attn_b_in"], a["L0_attn_b_y"]], 1)
    out["b_out"] = a["L0_attn_b_out"]
    wy = a["L0_attn_W_y"].reshape(DM, PAIRS, 2, DH, 2)
    out["w_yT"] = np.stack([wy[..., r].transpose(2, 4, 3, 1, 0).reshape(128, PAIRS, DM) for r in ([0, 1], [1, 0])], 1)
    out["h0_re"], out["h0_im"] = a["L0_attn_h0_re"], a["L0_attn_h0_im"]
    for n in "qkvo":
        out["x_w" + n] = a["L0_xattn_W" + n].T
    out["e_wg"] = a["L0_ffn_Wg"]
    out["e_wqkv"] = np.concatenate([a["L0_ffn_Wq"], a["L0_ffn_Wkv"]], 2).transpose(1, 0, 2)
    out["e_bqkv"] = np.concatenate([a["L0_ffn_bq"], a["L0_ffn_bkv"]], 1)
    wo = np.zeros((2, EDH, EX // 2, 2, DM), np.float32)
    for i in range(2):
        wo[i, :, :, i] = a["L0_ffn_Wo"][i::2].transpose(1, 0, 2)
    out["e_woP"] = wo.reshape(2 * EDH, EX // 2, 2 * DM)
    out["e_qmask"] = (np.arange(128)[:, None] // BATCH == np.arange(4)).astype(np.float32)
    out["e_bo"], out["e_lng"], out["e_lnb"] = a["L0_ffn_bo"], a["L0_ffn_ln_g"], a["L0_ffn_ln_b"]
    out["e_iota"] = np.arange(BATCH, 0, -1).astype(np.float32)
    out["e_first"] = (np.arange(128) // EX % CAP == 0).astype(np.float32)[:, None]
    out["ident"] = np.eye(128, dtype=np.float32)
    mask = np.zeros((2, 4, 32, TP), np.float32)
    for slot in range(SLOTS):
        for i in range(32):
            if slot < 6:
                h = HALVES[slot]
                s = i // h * 2 * h + i % h
                t = [t for t in range(TP) if t // (2 * h) == s // (2 * h) and t // h % 2]
            else:
                s = 32 * (slot - 6) + i
                t = [s]
            if s < TIME:
                mask[slot // 4, slot % 4, i, t] = 1
    out["mask"] = mask.transpose(1, 2, 0, 3).reshape(128, 2, TP)
    head = np.arange(128) // XD
    rows = np.arange(128)[:, None]
    out["hmask"] = np.concatenate([head[:, None] % 4 == np.arange(4), 1 - 2 * (rows // DH % 2)], 1).astype(np.float32)
    return {k: np.ascontiguousarray(v) for k, v in out.items()}


def kernel(**inputs):
    import concourse.bacc as bacc
    from concourse.bass_utils import run_bass_kernel_spmd

    arrays = layouts(inputs)
    nc = bacc.Bacc("TRN2", target_bir_lowering=False, num_devices=1)
    io = {n: nc.dram_tensor(f"in_{n}", a.shape, mybir.dt.from_np(a.dtype), kind="ExternalInput").ap() for n, a in arrays.items()}
    io["out"] = nc.dram_tensor("out", (BATCH, TIME, DM), F32, kind="ExternalOutput").ap()
    program(nc, io)
    r = run_bass_kernel_spmd(nc, [{f"in_{n}": a for n, a in arrays.items()}], core_ids=[0])
    return r.results[0]["out"]
```
